# Optimizing a Trainium2 kernel written in Bass

```python
import numpy as np
import jax
import jax.numpy as jnp

def _softmax(x, axis=-1):
    return jax.nn.softmax(x, axis=axis)

def _gelu(x):
    return jax.nn.gelu(x, approximate=True)

def _silu(x):
    return jax.nn.silu(x)

def _sigmoid(x):
    return jax.nn.sigmoid(x)

def _layernorm(x, axis=-1, eps=1e-05):
    m = jnp.mean(x, axis=axis, keepdims=True)
    v = jnp.var(x, axis=axis, keepdims=True)
    return (x - m) / jnp.sqrt(v + eps)

def _scatter_add(tgt, idx, src, axis=0):
    return tgt.at[idx].add(src)

def _segment_sum(src, seg, n):
    return jax.ops.segment_sum(src, seg, n)
kernel_name = 'mk_perceiver_d2_seqx_r4_06816e'

def setup_inputs(seed: int=0):
    np.random.seed(seed)
    _w = jnp.asarray

    def _rec_inputs():
        import jax
        import jax.numpy as jnp
        _rk = jax.random.key(seed)
        x = -0.0005207 + 1.001 * jax.random.normal(jax.random.fold_in(_rk, 1), (64, 32, 256), jnp.float32)
        _lenS = 32 - jax.random.randint(jax.random.fold_in(_rk, 7), (64,), 0, max(1, 32 // 4) + 1, jnp.int32)
        _lenS2 = 257 - jax.random.randint(jax.random.fold_in(_rk, 8), (64,), 0, max(1, 257 // 4) + 1, jnp.int32)
        _ctx_1024P = jax.random.normal(jax.random.fold_in(_rk, 11), (64, 16, 256), jnp.float32)
        _ctx_1024c = jax.random.dirichlet(jax.random.fold_in(_rk, 511), 0.3 * jnp.ones((16,), jnp.float32), (64, 257))
        _ctx_1024t = jnp.einsum('bsk,bkd->bsd', _ctx_1024c, _ctx_1024P)
        _ctx_1024t = _ctx_1024t * jax.lax.rsqrt(jnp.mean(jnp.square(_ctx_1024t)) + 1e-12) * 0.953939
        ctx_1024 = -0.000514642 + 1.00011 * (_ctx_1024t + 0.3 * jax.random.normal(jax.random.fold_in(_rk, 611), (64, 257, 256), jnp.float32))
        _validS = jnp.arange(32)[None, :] < _lenS[:, None]
        _validS2 = jnp.arange(257)[None, :] < _lenS2[:, None]
        _causal = jnp.tril(jnp.ones((32, 32), dtype=bool))
        mask_Bx1xSxS2_bf0 = jnp.logical_not(jnp.ones((64, 1, 32, 257), dtype=bool))
        return (x, ctx_1024, mask_Bx1xSxS2_bf0)
    x, ctx_1024, mask_Bx1xSxS2_bf0 = _rec_inputs()

    def _L0_xattn_setup():
        import jax, jax.numpy as jnp
        import numpy as np
        EMBED_DIM = 256
        NUM_HEADS = 16
        HEAD_DIM = EMBED_DIM // NUM_HEADS
        WINDOW = 64

        def apply_rope(x):
            B, H, S, d = x.shape
            half = d // 2
            pos = jnp.arange(S, dtype=x.dtype)
            freqs = 1.0 / 10000.0 ** (jnp.arange(half, dtype=x.dtype) / half)
            ang = pos[:, None] * freqs[None, :]
            cos, sin = (jnp.cos(ang), jnp.sin(ang))
            x1, x2 = (x[..., :half], x[..., half:])
            return jnp.concatenate([x1 * cos - x2 * sin, x1 * sin + x2 * cos], axis=-1)

        def _forward(query, key, value, q_w, q_b, k_w, k_b, v_w, v_b, o_w, o_b):
            B, S_q, D = query.shape
            S_k = key.shape[1]
            H, d, W = (NUM_HEADS, HEAD_DIM, WINDOW)
            q = (query @ q_w.T + q_b).reshape(B, S_q, H, d).transpose(0, 2, 1, 3)
            k = (key @ k_w.T + k_b).reshape(B, S_k, H, d).transpose(0, 2, 1, 3)
            v = (value @ v_w.T + v_b).reshape(B, S_k, H, d).transpose(0, 2, 1, 3)
            q = apply_rope(q) * d ** (-0.5)
            k = apply_rope(k)
            q_pos = jnp.arange(S_q)[:, None]
            offsets = jnp.arange(-W, 1)[None, :]
            idx = q_pos + offsets
            local_mask = (idx < 0) | (idx >= S_k)
            gidx = jnp.clip(idx, 0, S_k - 1)
            k_win = k[:, :, gidx, :]
            v_win = v[:, :, gidx, :]
            scores = jnp.einsum('bhqd,bhqwd->bhqw', q, k_win)
            mask = local_mask[None, None, :, :]
            scores = jnp.where(mask, -jnp.inf, scores)
            m = jnp.max(scores, axis=-1, keepdims=True)
            m = jnp.where(jnp.isfinite(m), m, 0.0)
            e = jnp.exp(scores - m)
            denom = jnp.sum(e, axis=-1, keepdims=True)
            probs = jnp.where(denom > 0, e / jnp.where(denom > 0, denom, 1.0), 0.0)
            ctx = jnp.einsum('bhqw,bhqwd->bhqd', probs, v_win)
            ctx = ctx.transpose(0, 2, 1, 3).reshape(B, S_q, D)
            return ctx @ o_w.T + o_b
        key = jax.random.key(seed)
        ks = jax.random.split(key, 12)
        B, S, D = (1, 512, EMBED_DIM)
        scale = 1.0 / np.sqrt(D)
        inp = {'query': jax.random.normal(ks[0], (B, S, D), jnp.float32), 'key': jax.random.normal(ks[1], (B, S, D), jnp.float32), 'value': jax.random.normal(ks[2], (B, S, D), jnp.float32), 'q_w': jax.random.normal(ks[3], (D, D), jnp.float32) * scale, 'q_b': jax.random.normal(ks[4], (D,), jnp.float32) * 0.01, 'k_w': jax.random.normal(ks[5], (D, D), jnp.float32) * scale, 'k_b': jax.random.normal(ks[6], (D,), jnp.float32) * 0.01, 'v_w': jax.random.normal(ks[7], (D, D), jnp.float32) * scale, 'v_b': jax.random.normal(ks[8], (D,), jnp.float32) * 0.01, 'o_w': jax.random.normal(ks[9], (D, D), jnp.float32) * scale, 'o_b': jax.random.normal(ks[10], (D,), jnp.float32) * 0.01}
        return inp
    _L0_xattn_all = _L0_xattn_setup()
    _L0_xattn_in = {k: v for k, v in _L0_xattn_all.items() if k in ('q_w', 'q_b', 'k_w', 'k_b', 'v_w', 'v_b', 'o_w', 'o_b')}
    del _L0_xattn_all

    def _L0_attn_setup():
        import jax, jax.numpy as jnp
        import numpy as np
        D_MODEL = 256
        NUM_HEADS = 16
        D_K = D_MODEL // NUM_HEADS
        MAX_SEQ = 512

        def _rope_tables(seq_len):
            inv_freq = 1.0 / 10000.0 ** (jnp.arange(0, D_K, 2, dtype=jnp.float32) / D_K)
            pos = jnp.arange(seq_len, dtype=jnp.float32)
            freqs = jnp.einsum('i,j->ij', pos, inv_freq)
            return (jnp.cos(freqs), jnp.sin(freqs))

        def _apply_rope(x, cos_half, sin_half):
            x_even = x[..., ::2]
            x_odd = x[..., 1::2]
            r_even = x_even * cos_half - x_odd * sin_half
            r_odd = x_even * sin_half + x_odd * cos_half
            return jnp.stack([r_even, r_odd], axis=-1).reshape(x.shape)
        key = jax.random.key(seed)
        ks = jax.random.split(key, 9)
        B, S = (2, 512)
        scale = 1.0 / np.sqrt(D_MODEL)
        x = jax.random.normal(ks[0], (B, S, D_MODEL), dtype=jnp.float32)
        Wq = jax.random.normal(ks[1], (D_MODEL, D_MODEL), dtype=jnp.float32) * scale
        Wk = jax.random.normal(ks[2], (D_MODEL, D_MODEL), dtype=jnp.float32) * scale
        Wv = jax.random.normal(ks[3], (D_MODEL, D_MODEL), dtype=jnp.float32) * scale
        Wo = jax.random.normal(ks[4], (D_MODEL, D_MODEL), dtype=jnp.float32) * scale
        bq = jnp.zeros((D_MODEL,), jnp.float32)
        bk = jnp.zeros((D_MODEL,), jnp.float32)
        bv = jnp.zeros((D_MODEL,), jnp.float32)
        bo = jnp.zeros((D_MODEL,), jnp.float32)
        return {'x': x, 'Wq': Wq, 'bq': bq, 'Wk': Wk, 'bk': bk, 'Wv': Wv, 'bv': bv, 'Wo': Wo, 'bo': bo}
    _L0_attn_all = _L0_attn_setup()
    _L0_attn_in = {k: v for k, v in _L0_attn_all.items() if k in ('Wq', 'bq', 'Wk', 'bk', 'Wv', 'bv', 'Wo', 'bo')}
    del _L0_attn_all

    def _L0_ffn_setup():
        import jax, jax.numpy as jnp
        import numpy as np
        FP8_MAX = 448.0
        FP8 = jnp.float8_e4m3fn
        key = jax.random.key(seed)
        kx, kw, kb = jax.random.split(key, 3)
        B, S, D_in, D_out = (4, 2048, 256, 256)
        x = jax.random.normal(kx, (B, S, D_in), dtype=jnp.float32)
        w = jax.random.normal(kw, (D_out, D_in), dtype=jnp.float32) * 0.02
        weight_scale = jnp.maximum(jnp.max(jnp.abs(w)), 1e-12) / FP8_MAX
        weight = (w / weight_scale).astype(FP8)
        bias = jax.random.normal(kb, (D_out,), dtype=jnp.float32) * 0.01
        return {'x': x, 'weight': weight, 'weight_scale': weight_scale, 'bias': bias}
    _L0_ffn_all = _L0_ffn_setup()
    _L0_ffn_in = {k: v for k, v in _L0_ffn_all.items() if k in ('weight', 'weight_scale', 'bias')}
    del _L0_ffn_all

    def _L1_xattn_setup():
        import jax, jax.numpy as jnp
        import numpy as np
        N_HEAD = 16
        DIM = 256
        DIM_HEAD = DIM // N_HEAD
        B, S = (4, 512)

        def _split_heads(x):
            b, s, _ = x.shape
            return x.reshape(b, s, N_HEAD, DIM_HEAD).transpose(0, 2, 1, 3)
        key = jax.random.key(seed)
        ks = jax.random.split(key, 12)
        p = lambda k, shape: jax.random.normal(k, shape, dtype=jnp.float32) * 0.02
        return {'query': jax.random.normal(ks[0], (B, S, DIM), dtype=jnp.float32), 'key': jax.random.normal(ks[1], (B, S, DIM), dtype=jnp.float32), 'value': jax.random.normal(ks[2], (B, S, DIM), dtype=jnp.float32), 'mask': jnp.zeros((B, 1, S, S), dtype=bool), 'w_q': p(ks[3], (DIM, DIM)), 'b_q': jnp.zeros((DIM,), jnp.float32), 'w_k': p(ks[4], (DIM, DIM)), 'b_k': jnp.zeros((DIM,), jnp.float32), 'w_v': p(ks[5], (DIM, DIM)), 'b_v': jnp.zeros((DIM,), jnp.float32), 'w_o': p(ks[6], (DIM, DIM)), 'b_o': jnp.zeros((DIM,), jnp.float32)}
    _L1_xattn_all = _L1_xattn_setup()
    _L1_xattn_in = {k: v for k, v in _L1_xattn_all.items() if k in ('w_q', 'b_q', 'w_k', 'b_k', 'w_v', 'b_v', 'w_o', 'b_o')}
    del _L1_xattn_all

    def _L1_attn_setup():
        import jax, jax.numpy as jnp
        import numpy as np
        B, L, D, R, GH = (4, 1024, 256, 32, 64)

        def _xavier(key, shape, gain=1.0):
            fan_in, fan_out = (shape[0], shape[1])
            lim = gain * np.sqrt(6.0 / (fan_in + fan_out))
            return jax.random.uniform(key, shape, jnp.float32, -lim, lim)
        key = jax.random.key(seed)
        ks = jax.random.split(key, 9)
        x = jax.random.normal(ks[0], (B, L, D), jnp.float32)
        gate_w1 = _xavier(ks[1], (D, GH), 1.0)
        gate_b1 = jnp.zeros((GH,), jnp.float32)
        gate_w2 = _xavier(ks[2], (GH, R), 1.0)
        gate_b2 = jnp.zeros((R,), jnp.float32)
        U_w = _xavier(ks[3], (D, R), 0.02)
        V_w = _xavier(ks[4], (D, R), 0.02)
        conv_w = jax.random.normal(ks[5], (D, 3), jnp.float32) * 0.02
        out_w = _xavier(ks[6], (R, D), 1.0)
        out_b = jnp.zeros((D,), jnp.float32)
        return {'x': x, 'gate_w1': gate_w1, 'gate_b1': gate_b1, 'gate_w2': gate_w2, 'gate_b2': gate_b2, 'U_w': U_w, 'V_w': V_w, 'conv_w': conv_w, 'out_w': out_w, 'out_b': out_b}
    _L1_attn_all = _L1_attn_setup()
    _L1_attn_in = {k: v for k, v in _L1_attn_all.items() if k in ('gate_w1', 'gate_b1', 'gate_w2', 'gate_b2', 'U_w', 'V_w', 'conv_w', 'out_w', 'out_b')}
    del _L1_attn_all

    def _L1_ffn_setup():
        import jax, jax.numpy as jnp
        import numpy as np
        D = 256
        H = 512
        E = 8
        TOP_K = 2
        N_SHARED = 1
        B, S = (2, 256)
        key = jax.random.key(seed)
        ks = jax.random.split(key, 12)
        sc = 0.02
        return {'hidden': jax.random.normal(ks[0], (B, S, D), jnp.float32), 'router_w': jax.random.normal(ks[1], (D, E), jnp.float32) * sc, 'router_b': jnp.zeros((E,), jnp.float32), 'sw1': jax.random.normal(ks[2], (D, H), jnp.float32) * sc, 'sb1': jnp.zeros((H,), jnp.float32), 'sw2': jax.random.normal(ks[3], (H, D), jnp.float32) * sc, 'sb2': jnp.zeros((D,), jnp.float32), 'rw1': jax.random.normal(ks[4], (E, D, H), jnp.float32) * sc, 'rb1': jnp.zeros((E, H), jnp.float32), 'rw2': jax.random.normal(ks[5], (E, H, D), jnp.float32) * sc, 'rb2': jnp.zeros((E, D), jnp.float32)}
    _L1_ffn_all = _L1_ffn_setup()
    _L1_ffn_in = {k: v for k, v in _L1_ffn_all.items() if k in ('router_w', 'router_b', 'sw1', 'sb1', 'sw2', 'sb2', 'rw1', 'rb1', 'rw2', 'rb2')}
    del _L1_ffn_all
    return {'x': x, 'ctx_1024': ctx_1024, 'mask_Bx1xSxS2_bf0': mask_Bx1xSxS2_bf0, 'L0_xattn_q_w': _L0_xattn_in['q_w'], 'L0_xattn_q_b': _L0_xattn_in['q_b'], 'L0_xattn_k_w': _L0_xattn_in['k_w'], 'L0_xattn_k_b': _L0_xattn_in['k_b'], 'L0_xattn_v_w': _L0_xattn_in['v_w'], 'L0_xattn_v_b': _L0_xattn_in['v_b'], 'L0_xattn_o_w': _L0_xattn_in['o_w'], 'L0_xattn_o_b': _L0_xattn_in['o_b'], 'L0_attn_Wq': _L0_attn_in['Wq'], 'L0_attn_bq': _L0_attn_in['bq'], 'L0_attn_Wk': _L0_attn_in['Wk'], 'L0_attn_bk': _L0_attn_in['bk'], 'L0_attn_Wv': _L0_attn_in['Wv'], 'L0_attn_bv': _L0_attn_in['bv'], 'L0_attn_Wo': _L0_attn_in['Wo'], 'L0_attn_bo': _L0_attn_in['bo'], 'L0_ffn_weight': _L0_ffn_in['weight'], 'L0_ffn_weight_scale': _L0_ffn_in['weight_scale'], 'L0_ffn_bias': _L0_ffn_in['bias'], 'L1_xattn_w_q': _L1_xattn_in['w_q'], 'L1_xattn_b_q': _L1_xattn_in['b_q'], 'L1_xattn_w_k': _L1_xattn_in['w_k'], 'L1_xattn_b_k': _L1_xattn_in['b_k'], 'L1_xattn_w_v': _L1_xattn_in['w_v'], 'L1_xattn_b_v': _L1_xattn_in['b_v'], 'L1_xattn_w_o': _L1_xattn_in['w_o'], 'L1_xattn_b_o': _L1_xattn_in['b_o'], 'L1_attn_gate_w1': _L1_attn_in['gate_w1'], 'L1_attn_gate_b1': _L1_attn_in['gate_b1'], 'L1_attn_gate_w2': _L1_attn_in['gate_w2'], 'L1_attn_gate_b2': _L1_attn_in['gate_b2'], 'L1_attn_U_w': _L1_attn_in['U_w'], 'L1_attn_V_w': _L1_attn_in['V_w'], 'L1_attn_conv_w': _L1_attn_in['conv_w'], 'L1_attn_out_w': _L1_attn_in['out_w'], 'L1_attn_out_b': _L1_attn_in['out_b'], 'L1_ffn_router_w': _L1_ffn_in['router_w'], 'L1_ffn_router_b': _L1_ffn_in['router_b'], 'L1_ffn_sw1': _L1_ffn_in['sw1'], 'L1_ffn_sb1': _L1_ffn_in['sb1'], 'L1_ffn_sw2': _L1_ffn_in['sw2'], 'L1_ffn_sb2': _L1_ffn_in['sb2'], 'L1_ffn_rw1': _L1_ffn_in['rw1'], 'L1_ffn_rb1': _L1_ffn_in['rb1'], 'L1_ffn_rw2': _L1_ffn_in['rw2'], 'L1_ffn_rb2': _L1_ffn_in['rb2']}

def reference(x, ctx_1024, mask_Bx1xSxS2_bf0, L0_xattn_q_w, L0_xattn_q_b, L0_xattn_k_w, L0_xattn_k_b, L0_xattn_v_w, L0_xattn_v_b, L0_xattn_o_w, L0_xattn_o_b, L0_attn_Wq, L0_attn_bq, L0_attn_Wk, L0_attn_bk, L0_attn_Wv, L0_attn_bv, L0_attn_Wo, L0_attn_bo, L0_ffn_weight, L0_ffn_weight_scale, L0_ffn_bias, L1_xattn_w_q, L1_xattn_b_q, L1_xattn_w_k, L1_xattn_b_k, L1_xattn_w_v, L1_xattn_b_v, L1_xattn_w_o, L1_xattn_b_o, L1_attn_gate_w1, L1_attn_gate_b1, L1_attn_gate_w2, L1_attn_gate_b2, L1_attn_U_w, L1_attn_V_w, L1_attn_conv_w, L1_attn_out_w, L1_attn_out_b, L1_ffn_router_w, L1_ffn_router_b, L1_ffn_sw1, L1_ffn_sb1, L1_ffn_sw2, L1_ffn_sb2, L1_ffn_rw1, L1_ffn_rb1, L1_ffn_rw2, L1_ffn_rb2):
    import jax
    import jax.numpy as jnp

    def _L0_xattn_ref(query, key, value, q_w, q_b, k_w, k_b, v_w, v_b, o_w, o_b):
        import jax, jax.numpy as jnp
        import numpy as np
        EMBED_DIM = 256
        NUM_HEADS = 16
        HEAD_DIM = EMBED_DIM // NUM_HEADS
        WINDOW = 64

        def apply_rope(x):
            B, H, S, d = x.shape
            half = d // 2
            pos = jnp.arange(S, dtype=x.dtype)
            freqs = 1.0 / 10000.0 ** (jnp.arange(half, dtype=x.dtype) / half)
            ang = pos[:, None] * freqs[None, :]
            cos, sin = (jnp.cos(ang), jnp.sin(ang))
            x1, x2 = (x[..., :half], x[..., half:])
            return jnp.concatenate([x1 * cos - x2 * sin, x1 * sin + x2 * cos], axis=-1)

        def _forward(query, key, value, q_w, q_b, k_w, k_b, v_w, v_b, o_w, o_b):
            B, S_q, D = query.shape
            S_k = key.shape[1]
            H, d, W = (NUM_HEADS, HEAD_DIM, WINDOW)
            q = (query @ q_w.T + q_b).reshape(B, S_q, H, d).transpose(0, 2, 1, 3)
            k = (key @ k_w.T + k_b).reshape(B, S_k, H, d).transpose(0, 2, 1, 3)
            v = (value @ v_w.T + v_b).reshape(B, S_k, H, d).transpose(0, 2, 1, 3)
            q = apply_rope(q) * d ** (-0.5)
            k = apply_rope(k)
            q_pos = jnp.arange(S_q)[:, None]
            offsets = jnp.arange(-W, 1)[None, :]
            idx = q_pos + offsets
            local_mask = (idx < 0) | (idx >= S_k)
            gidx = jnp.clip(idx, 0, S_k - 1)
            k_win = k[:, :, gidx, :]
            v_win = v[:, :, gidx, :]
            scores = jnp.einsum('bhqd,bhqwd->bhqw', q, k_win)
            mask = local_mask[None, None, :, :]
            scores = jnp.where(mask, -jnp.inf, scores)
            m = jnp.max(scores, axis=-1, keepdims=True)
            m = jnp.where(jnp.isfinite(m), m, 0.0)
            e = jnp.exp(scores - m)
            denom = jnp.sum(e, axis=-1, keepdims=True)
            probs = jnp.where(denom > 0, e / jnp.where(denom > 0, denom, 1.0), 0.0)
            ctx = jnp.einsum('bhqw,bhqwd->bhqd', probs, v_win)
            ctx = ctx.transpose(0, 2, 1, 3).reshape(B, S_q, D)
            return ctx @ o_w.T + o_b
        return _forward(query, key, value, q_w, q_b, k_w, k_b, v_w, v_b, o_w, o_b)

    def _L0_attn_ref(x, Wq, bq, Wk, bk, Wv, bv, Wo, bo):
        import jax, jax.numpy as jnp
        import numpy as np
        D_MODEL = 256
        NUM_HEADS = 16
        D_K = D_MODEL // NUM_HEADS
        MAX_SEQ = 512

        def _rope_tables(seq_len):
            inv_freq = 1.0 / 10000.0 ** (jnp.arange(0, D_K, 2, dtype=jnp.float32) / D_K)
            pos = jnp.arange(seq_len, dtype=jnp.float32)
            freqs = jnp.einsum('i,j->ij', pos, inv_freq)
            return (jnp.cos(freqs), jnp.sin(freqs))

        def _apply_rope(x, cos_half, sin_half):
            x_even = x[..., ::2]
            x_odd = x[..., 1::2]
            r_even = x_even * cos_half - x_odd * sin_half
            r_odd = x_even * sin_half + x_odd * cos_half
            return jnp.stack([r_even, r_odd], axis=-1).reshape(x.shape)
        B, S, _ = x.shape
        H, dk = (NUM_HEADS, D_K)
        q = (x @ Wq + bq).reshape(B, S, H, dk)
        k = (x @ Wk + bk).reshape(B, S, H, dk)
        v = (x @ Wv + bv).reshape(B, S, H, dk)
        cos_half, sin_half = _rope_tables(S)
        cos_half = cos_half[None, :, None, :]
        sin_half = sin_half[None, :, None, :]
        q = _apply_rope(q, cos_half, sin_half)
        k = _apply_rope(k, cos_half, sin_half)
        q = q.transpose(0, 2, 1, 3)
        k = k.transpose(0, 2, 1, 3)
        v = v.transpose(0, 2, 1, 3)
        scores = jnp.einsum('bhqd,bhkd->bhqk', q, k) / jnp.sqrt(jnp.float32(dk))
        causal = jnp.where(jnp.tril(jnp.ones((S, S), jnp.float32)) == 0, -1000000000.0, 0.0)
        scores = scores + causal
        attn = jax.nn.softmax(scores, axis=-1)
        out = jnp.einsum('bhqk,bhkd->bhqd', attn, v)
        out = out.transpose(0, 2, 1, 3).reshape(B, S, H * dk)
        return out @ Wo + bo

    def _L0_ffn_ref(x, weight, weight_scale, bias):
        import jax, jax.numpy as jnp
        import numpy as np
        FP8_MAX = 448.0
        FP8 = jnp.float8_e4m3fn
        amax = jnp.max(jnp.abs(x), axis=-1, keepdims=True)
        x_scale = jnp.maximum(amax, 1e-12) / FP8_MAX
        qinput = (x / x_scale).astype(FP8)
        A = qinput.astype(x.dtype) * x_scale
        Bm = weight.astype(x.dtype) * weight_scale
        out = jnp.einsum('bsk,nk->bsn', A, Bm) + bias
        return out.astype(x.dtype)

    def _L1_xattn_ref(query, key, value, mask, w_q, b_q, w_k, b_k, w_v, b_v, w_o, b_o):
        import jax, jax.numpy as jnp
        import numpy as np
        N_HEAD = 16
        DIM = 256
        DIM_HEAD = DIM // N_HEAD
        B, S = (4, 512)

        def _split_heads(x):
            b, s, _ = x.shape
            return x.reshape(b, s, N_HEAD, DIM_HEAD).transpose(0, 2, 1, 3)
        Q = _split_heads(query @ w_q.T + b_q)
        K = _split_heads(key @ w_k.T + b_k)
        V = _split_heads(value @ w_v.T + b_v)
        scale = 1.0 / np.sqrt(DIM_HEAD).astype(np.float32)
        scores = jnp.einsum('bhqd,bhkd->bhqk', Q, K) * scale
        scores = jnp.where(mask, -jnp.inf, scores)
        probs = jax.nn.softmax(scores, axis=-1)
        attn = jnp.einsum('bhqk,bhkd->bhqd', probs, V)
        b, h, s, dh = attn.shape
        merged = attn.transpose(0, 2, 1, 3).reshape(b, s, h * dh)
        return merged @ w_o.T + b_o

    def _L1_attn_ref(x, gate_w1, gate_b1, gate_w2, gate_b2, U_w, V_w, conv_w, out_w, out_b):
        import jax, jax.numpy as jnp
        import numpy as np
        B, L, D, R, GH = (4, 1024, 256, 32, 64)

        def _xavier(key, shape, gain=1.0):
            fan_in, fan_out = (shape[0], shape[1])
            lim = gain * np.sqrt(6.0 / (fan_in + fan_out))
            return jax.random.uniform(key, shape, jnp.float32, -lim, lim)
        h = jax.nn.relu(jnp.einsum('bld,dg->blg', x, gate_w1) + gate_b1)
        gate = jax.nn.sigmoid(jnp.einsum('blg,gr->blr', h, gate_w2) + gate_b2)
        U = jnp.einsum('bld,dr->blr', x, U_w)
        V = jnp.einsum('bld,dr->blr', x, V_w)
        S = jnp.cumsum(V, axis=1)
        glob = gate * U * S
        y_global = jnp.einsum('blr,rd->bld', glob, out_w) + out_b
        xpad = jnp.pad(x, ((0, 0), (1, 1), (0, 0)))
        t_out = xpad[:, :-2] * conv_w[:, 0] + xpad[:, 1:-1] * conv_w[:, 1] + xpad[:, 2:] * conv_w[:, 2]
        return t_out + y_global

    def _L1_ffn_ref(hidden, router_w, router_b, sw1, sb1, sw2, sb2, rw1, rb1, rw2, rb2):
        import jax, jax.numpy as jnp
        import numpy as np
        D = 256
        H = 512
        E = 8
        TOP_K = 2
        N_SHARED = 1
        B, S = (2, 256)
        b, s, d = hidden.shape
        T = b * s
        flat = hidden.reshape(T, d)
        router_logits = flat @ router_w + router_b
        router_probs = jax.nn.softmax(router_logits, axis=-1)
        topk_probs, topk_idx = jax.lax.top_k(router_probs, TOP_K)
        weights = jnp.zeros_like(router_probs).at[jnp.arange(T)[:, None], topk_idx].add(topk_probs)
        sh = jax.nn.gelu(flat @ sw1 + sb1, approximate=False)
        shared_out = (sh @ sw2 + sb2) / N_SHARED
        h1 = jax.nn.gelu(jnp.einsum('td,edh->teh', flat, rw1) + rb1[None], approximate=False)
        expert_out = jnp.einsum('teh,ehd->ted', h1, rw2) + rb2[None]
        mixed = jnp.einsum('ted,te->td', expert_out, weights)
        return (shared_out + mixed).reshape(b, s, d)
    x = x + _L0_xattn_ref(_layernorm(x, axis=-1), ctx_1024, ctx_1024, L0_xattn_q_w, L0_xattn_q_b, L0_xattn_k_w, L0_xattn_k_b, L0_xattn_v_w, L0_xattn_v_b, L0_xattn_o_w, L0_xattn_o_b)
    x = x + _L0_attn_ref(_layernorm(x, axis=-1), L0_attn_Wq, L0_attn_bq, L0_attn_Wk, L0_attn_bk, L0_attn_Wv, L0_attn_bv, L0_attn_Wo, L0_attn_bo)
    x = x + _L0_ffn_ref(_layernorm(x, axis=-1), L0_ffn_weight, L0_ffn_weight_scale, L0_ffn_bias)
    x = x + _L1_xattn_ref(_layernorm(x, axis=-1), ctx_1024, ctx_1024, mask_Bx1xSxS2_bf0, L1_xattn_w_q, L1_xattn_b_q, L1_xattn_w_k, L1_xattn_b_k, L1_xattn_w_v, L1_xattn_b_v, L1_xattn_w_o, L1_xattn_b_o)
    x = x + _L1_attn_ref(_layernorm(x, axis=-1), L1_attn_gate_w1, L1_attn_gate_b1, L1_attn_gate_w2, L1_attn_gate_b2, L1_attn_U_w, L1_attn_V_w, L1_attn_conv_w, L1_attn_out_w, L1_attn_out_b)
    x = x + _L1_ffn_ref(_layernorm(x, axis=-1), L1_ffn_router_w, L1_ffn_router_b, L1_ffn_sw1, L1_ffn_sb1, L1_ffn_sw2, L1_ffn_sb2, L1_ffn_rw1, L1_ffn_rb1, L1_ffn_rw2, L1_ffn_rb2)
    return x

_drawn_inputs = setup_inputs


def setup_inputs(seed=0):
    import zlib

    import numpy as np

    out = dict(_drawn_inputs(seed))
    spreads = {'L0_attn_bq': (0.0, 0.439),
     'L0_attn_bk': (0.0, 0.745),
     'L0_attn_bv': (0.0, 0.1),
     'L0_attn_bo': (0.0, 0.1),
     'L1_xattn_b_q': (0.0, 0.8),
     'L1_xattn_b_k': (0.0, 2.0),
     'L1_xattn_b_v': (0.0, 0.321),
     'L1_xattn_b_o': (0.0, 0.1),
     'L1_attn_gate_b1': (0.0, 0.8),
     'L1_attn_gate_b2': (0.0, 2.0),
     'L1_attn_out_b': (0.0, 0.1),
     'L1_ffn_router_b': (0.0, 0.645),
     'L1_ffn_sb1': (0.0, 0.463),
     'L1_ffn_sb2': (0.0, 0.1),
     'L1_ffn_rb1': (0.0, 0.8),
     'L1_ffn_rb2': (0.0, 0.448)}
    factors = {'L0_xattn_q_b': 8.0,
     'L0_xattn_k_b': 8.0,
     'L0_xattn_v_b': 5.663,
     'L0_xattn_o_b': 5.267,
     'L0_ffn_bias': 7.55,
     'L1_xattn_w_q': 8.0,
     'L1_xattn_w_k': 8.0,
     'L1_attn_gate_w1': 8.0,
     'L1_attn_gate_w2': 8.0,
     'L1_attn_U_w': 8.0,
     'L1_attn_V_w': 8.0,
     'L1_attn_out_w': 8.0,
     'L1_ffn_router_w': 2.846,
     'L1_ffn_rw1': 4.074,
     'L1_ffn_rw2': 3.822}
    for name, (base, spread) in spreads.items():
        noise = np.random.default_rng([zlib.crc32(name.encode()), seed]).standard_normal(out[name].shape)
        drawn = base * np.exp(spread * noise) if base else spread * noise
        out[name] = jnp.asarray(drawn.astype(out[name].dtype))
    for name, factor in factors.items():
        out[name] = (out[name] * factor).astype(out[name].dtype)
    return out
```

```python
from contextlib import ExitStack

import numpy as np

import concourse.bass as bass
from concourse import mybir

F32 = mybir.dt.float32
F32R = mybir.dt.float32r
BF16 = mybir.dt.bfloat16
I32 = mybir.dt.int32
U8 = mybir.dt.uint8
FP8 = mybir.dt.float8e4
ALU = mybir.AluOpType
ACT = mybir.ActivationFunctionType
AX = mybir.AxisListType

B, S, D = 64, 32, 256
SK = 257
P = 128
NT = B * S // P
BT = P // S
H, DH = 16, 16
G = H // BT
L = BT
KC = D // P
U = 4
R, GH = 32, 64
E, HID = 8, 512
EX = E + 1
HM = HID // P
TG = 4
EPS = 1e-5
MASKED = -1e30
CAUSAL = -1e9


def build(nc, a):
    with ExitStack() as ctx:

        def sb(name, shape, dt=F32):
            return ctx.enter_context(nc.sbuf_tensor(name, shape, dt))

        def sem(name):
            return ctx.enter_context(nc.semaphore(name))

        class Scratch(ExitStack):
            def __call__(self, name, shape, dt=F32):
                return self.enter_context(nc.sbuf_tensor(name, shape, dt))

        psum = ctx.enter_context(nc.psum_tensor("psum", [P, 8, 512], F32))

        x = sb("x", [P, NT, D])
        ln_mv = sb("ln_mv", [P, NT, 2])
        ln_rstd = sb("ln_rstd", [P, NT])
        ln_tmp = sb("ln_tmp", [P, 2, NT])
        ident = sb("ident", [P, P])
        eps = sb("eps", [P, 1])
        head_scale = sb("head_scale", [P, L])
        bn_out = sb("bn_out", [P, U, 6])
        bn_mv = sb("bn_mv", [P, U, 2])

        x_loaded = sem("x_loaded")
        consts_loaded = sem("consts_loaded")
        consts_cast = sem("consts_cast")
        x_tiles = a["x"].rearrange("(t p) c -> p t c", p=P)
        out_tiles = a["out"].rearrange("(t p) c -> p t c", p=P)
        x_stats = sem("x_stats")
        chain = sem("chain")
        chained = [0]

        passed = {}

        def hold(eng, semaphore, count):
            if eng not in passed:
                passed[eng] = sem(f"passed_{len(passed)}")
            eng.wait_ge(semaphore, count)
            eng.sem_inc(passed[eng], 1)

        def link(dve, ins, n=1):
            ins.then_inc(chain, 1)
            chained[0] += 1
            dve.wait_ge(chain, chained[0])

        layers = ["xattn0", "attn0", "ffn0", "xattn1", "mix1", "moe1"]
        var_ready, sqrt_ready, rstd_ready = sem("var_ready"), sem("sqrt_ready"), sem("rstd_ready")

        def act_sqrt(act, n):
            act.wait_ge(var_ready, layers.index(n) + 1)
            nc.scalar.activation(ln_tmp[:, 0, :], ln_mv[:, :, 1], ACT.Sqrt, bias=eps[:, 0:1]).then_inc(sqrt_ready, 1)

        def dve_rstd(dve, n):
            dve.wait_ge(sqrt_ready, layers.index(n) + 1)
            r, s = ln_rstd[:, :], ln_tmp[:, 1, :]
            link(dve, nc.vector.reciprocal(r, ln_tmp[:, 0, :]))
            link(dve, nc.vector.scalar_tensor_tensor(out=s, in0=ln_mv[:, :, 1], scalar=eps[:, 0:1], in1=r,
                                                     op0=ALU.add, op1=ALU.mult))
            link(dve, nc.vector.tensor_tensor(s, s, r, ALU.mult))
            link(dve, nc.vector.tensor_scalar(s, s, -0.5, 1.5, ALU.mult, ALU.add))
            ins = nc.vector.tensor_tensor(r, r, s, ALU.mult)
            ins.then_inc(rstd_ready, 1)
            dve.wait_ge(rstd_ready, layers.index(n) + 1)

        def dve_normalise(t, out):
            return nc.vector.tensor_scalar(out, x[:, t, :], ln_mv[:, t, 0:1], ln_rstd[:, bass.ds(t, 1)],
                                           ALU.subtract, ALU.mult)

        class Small:

            def __init__(self, name, cross):
                self.name, self.cross = name, cross

        sm_xn = sb("sm_xn", [P, U, D])
        rope_cos = sb("rope_cos", [P, DH])
        rope_sin = sb("rope_sin", [P, DH])
        ident_b = sb("ident_b", [P, P], BF16)
        causal = sb("causal", [P, S])
        causal_b = sb("causal_b", [P, S], BF16)

        sm = {s: sem(f"small_{s}") for s in (
            "norm_ready", "xT_done", "xT_ready", "biased", "qk_done", "v_done", "v_ready", "rope_parts", "rope_ready", "qkT_done",
            "qbd_ready", "kT_ready", "scores_done", "max_ready", "shifted", "exp_ready", "sum_ready", "rinv_ready", "pT_done",
            "pT_ready", "pv_done", "heads_ready", "oT_done", "oT_ready", "out_done", "x_biased", "x_updated", "stats_ready")}
        smalls = []
        for name, cross in (("xattn0", True), ("attn0", False)):
            c = Small(name, cross)
            c.w_qkv = sb(f"{name}_w_qkv", [P, KC, 3 * D])
            c.w_o = sb(f"{name}_w_o", [P, KC, D])
            c.b_qk = sb(f"{name}_b_qk", [P, 2 * D])
            c.b_v = sb(f"{name}_b_v", [P, KC, P])
            c.b_o = sb(f"{name}_b_o", [P, D])
            c.before = len(smalls) * NT
            c.weights_loaded, c.bias_product = sem(f"{name}_weights_loaded"), sem(f"{name}_bias_product")
            c.bias_ready, c.ctx_loaded = sem(f"{name}_bias_ready"), sem(f"{name}_ctx_loaded")
            smalls.append(c)
        small = {c.name: c for c in smalls}
        sm_zeroed = sem("small_zeroed")

        def bank(u, k):
            return psum[:, 2 * u + k, :]

        def small_tensor(pe, c):
            pe.wait_ge(c.weights_loaded, 16 * 5)
            for k in range(KC):
                mm = nc.tensor.matmul(bank(0, 0)[:, 0:D], c.b_v[:, k, :], c.w_o[:, k, :], start=(k == 0), stop=(k == KC - 1))
            mm.then_inc(c.bias_product, 1)
            pe.wait_ge(c.bias_ready, 1)
            with pe.Fori(0, NT // U) as i:
                n = lambda u: c.before + U * i + u + 1
                for u in range(U):
                    pe.wait_ge(sm["norm_ready"], n(u))
                    for k in range(KC):
                        mm = nc.tensor.transpose(bank(u, 0)[:, k * P:(k + 1) * P], sm_xn[:, u, k * P:(k + 1) * P], ident[:])
                    mm.then_inc(sm["xT_done"], 1)
                if c.cross:
                    pe.wait_ge(c.ctx_loaded, 16 * (i + 1))
                for u in range(U):
                    pe.wait_ge(sm["xT_ready"], n(u))
                    kv = sm_cT if c.cross else sm_xT
                    if c.cross:
                        for k in range(KC):
                            nc.tensor.matmul(bank(u, 1)[:, 0:D], sm_xT[:, u, k, :], c.w_qkv[:, k, 0:D],
                                             start=(k == 0), stop=(k == KC - 1), skip_group_check=True)
                        for k in range(KC):
                            mm = nc.tensor.matmul(bank(u, 1)[:, D:2 * D], kv[:, u, k, :], c.w_qkv[:, k, D:2 * D],
                                                  start=(k == 0), stop=(k == KC - 1), skip_group_check=True)
                    else:
                        for k in range(KC):
                            mm = nc.tensor.matmul(bank(u, 1), kv[:, u, k, :], c.w_qkv[:, k, 0:2 * D],
                                                  start=(k == 0), stop=(k == KC - 1))
                    mm.then_inc(sm["qk_done"], 1)
                    for k in range(KC):
                        mm = nc.tensor.matmul(bank(u, 0)[:, 0:D], kv[:, u, k, :], c.w_qkv[:, k, 2 * D:3 * D],
                                              start=(k == 0), stop=(k == KC - 1))
                    mm.then_inc(sm["v_done"], 1)
                for u in range(U):
                    pe.wait_ge(sm["rope_ready"], n(u))
                    pe.wait_ge(sm["v_ready"], n(u))
                    for s in range(2):
                        for k in range(KC):
                            mm = nc.tensor.transpose(bank(u, 1 - s)[:, k * P:(k + 1) * P],
                                                     sm_qk[:, u, s, k * P:(k + 1) * P], ident[:])
                    mm.then_inc(sm["qkT_done"], 1)
                for u in range(U):
                    pe.wait_ge(sm["kT_ready"], n(u))
                    pe.wait_ge(sm["qbd_ready"], n(u))
                    for r in range(2):
                        nc.tensor.matmul(bank(u, r)[:, 0:D], ident_b[:], causal_b[:].unsqueeze(1).broadcast_to([P, D // S, S]),
                                         start=True, stop=False, skip_group_check=True)
                        for k in range(KC):
                            for b in range(BT):
                                j = k * BT + b
                                mm = nc.tensor.matmul(bank(u, r)[:, j * S:(j + 1) * S], sm_qbd[64 * r:64 * r + 64, u, k, b, :],
                                                      sm_kT[64 * r:64 * r + 64, u, k, b * S:(b + 1) * S],
                                                      start=False, stop=(j == KC * BT - 1), skip_group_check=True)
                    mm.then_inc(sm["scores_done"], 1)
                for u in range(U):
                    pe.wait_ge(sm["exp_ready"], n(u))
                    for g in range(G):
                        v = sm_p[:, u, g * BT:(g + 1) * BT, :].rearrange("p b s -> p (b s)")
                        mm = nc.tensor.transpose(bank(u, 1)[:, g * P:(g + 1) * P], v, ident[:])
                    mm.then_inc(sm["pT_done"], 1)
                for u in range(U):
                    pe.wait_ge(sm["pT_ready"], n(u))
                    for gp in range(G):
                        mm = nc.tensor.matmul(bank(u, gp // 2)[:, (gp % 2) * D:(gp % 2 + 1) * D], sm_pT[:, u, gp, :],
                                              sm_vbd[:, u, :, (gp // 2 + 2 * (gp % 2)) * 64:(gp // 2 + 2 * (gp % 2) + 1) * 64],
                                              start=True, stop=True, skip_group_check=True)
                    mm.then_inc(sm["pv_done"], 1)
                for u in range(U):
                    pe.wait_ge(sm["heads_ready"], n(u))
                    for k in range(BT // 2):
                        mm = nc.tensor.transpose(bank(u, 0)[:, k * P:(k + 1) * P],
                                                 sm_o[:, u, k * 2 * G:(k + 1) * 2 * G, :].rearrange("p j d -> p (j d)"), ident[:])
                    mm.then_inc(sm["oT_done"], 1)
                for u in range(U):
                    pe.wait_ge(sm["oT_ready"], n(u))
                    for k in range(KC):
                        mm = nc.tensor.matmul(bank(u, 1)[:, 0:D], sm_oT[:, u, k, :, :].rearrange("p b s -> p (b s)"), c.w_o[:, k, :],
                                              start=(k == 0), stop=(k == KC - 1))
                    mm.then_inc(sm["out_done"], 1)

        def small_scalar(act, c):
            act.wait_ge(sm_zeroed, 1)
            act_sqrt(act, c.name)
            nc.scalar.preload_act_table(ACT.Exp)
            with act.Fori(0, NT // U) as i:
                n = lambda u: c.before + U * i + u + 1
                for u in range(U):
                    act.wait_ge(sm["xT_done"], n(u))
                    nc.scalar.activation(sm_xT[:, u, :, :].rearrange("p k s -> p (k s)"), bank(u, 0)[:, 0:D],
                                         ACT.Copy).then_inc(sm["xT_ready"], 1)
                for u in range(U):
                    act.wait_ge(sm["v_done"], n(u))
                    for b in range(BT):
                        rows = slice(b * S, (b + 1) * S)
                        ins = nc.scalar.copy(sm_vbd[rows, u, b, :], bank(u, 0)[rows, 0:D])
                    ins.then_inc(sm["v_ready"], 1)
                for u in range(U):
                    act.wait_ge(sm["qkT_done"], n(u))
                    nc.scalar.activation(sm_kT[:, u, :, :].rearrange("p k s -> p (k s)"), bank(u, 0)[:, 0:D],
                                         ACT.Copy).then_inc(sm["kT_ready"], 1)
                for u in range(U):
                    act.wait_ge(sm["shifted"], n(u))
                    v = sm_p[:, u, :, :].rearrange("p j s -> p (j s)")
                    nc.scalar.activation(v, v, ACT.Exp).then_inc(sm["exp_ready"], 1)
                for u in range(U):
                    act.wait_ge(sm["pT_done"], n(u))
                    nc.scalar.activation(sm_pT[:, u, :, :].rearrange("p g s -> p (g s)"), bank(u, 1), ACT.Copy).then_inc(sm["pT_ready"], 1)
                for u in range(U):
                    act.wait_ge(sm["oT_done"], n(u))
                    spread_heads(nc.scalar.copy, bank(u, 0), sm_oT[:, u, :, :, :]).then_inc(sm["oT_ready"], 1)

        def spread_heads(copy, src, dst):
            for r in range(2):
                for rb in range(2):
                    v = src[64 * rb:64 * rb + 64, 0:D].rearrange("p (bb j r q) -> p r bb j q", bb=BT // 2, j=L // 2, r=2)[:, r]
                    w = dst[64 * r:64 * r + 64].rearrange("p j (bb rb) q -> p rb bb j q", rb=2)[:, rb]
                    ins = copy(w, v)
            return ins

        def small_vector(dve, c):
            dve_rstd(dve, c.name)
            dve.wait_ge(c.weights_loaded, 16 * 5)
            dve.wait_ge(c.bias_product, 1)
            nc.vector.tensor_tensor(c.b_o[:], bank(0, 0)[:, 0:D], c.b_o[:], ALU.add).then_inc(c.bias_ready, 1)
            with dve.Fori(0, NT // U) as i:
                n = lambda u: c.before + U * i + u + 1
                hold(dve, sm["stats_ready"], 1 + STATS * (c.before // U + i))
                for u in range(U):
                    dve_normalise(U * i + u, sm_xn[:, u, :]).then_inc(sm["norm_ready"], 1)
                for u in range(U):
                    dve.wait_ge(sm["qk_done"], n(u))
                    qk = sm_qk[:, u, :, :].rearrange("p s c -> p (s c)")
                    nc.vector.tensor_tensor(qk, bank(u, 1), c.b_qk[:], ALU.add).then_inc(sm["biased"], 1)
                    dve.wait_ge(sm["biased"], n(u))
                    qk3 = sm_qk[:, u, :, :].rearrange("p s (h d) -> p (s h) d", d=DH)
                    cs3 = sm_cosd[:, u, :, :].rearrange("p s (h d) -> p (s h) d", d=DH)
                    sn3 = sm_sind[:, u, :, :].rearrange("p s (h d) -> p (s h) d", d=DH)
                    wide = [P, 2 * H, DH]
                    half = [P, 2 * H, DH // 2]
                    nc.vector.tensor_tensor(cs3, qk3, rope_cos[:].unsqueeze(1).broadcast_to(wide), ALU.mult).then_inc(sm["rope_parts"], 1)
                    nc.vector.tensor_tensor(sn3[:, :, 0:8], qk3[:, :, 8:16],
                                            rope_sin[:, 0:8].unsqueeze(1).broadcast_to(half), ALU.mult).then_inc(sm["rope_parts"], 1)
                    nc.vector.tensor_tensor(sn3[:, :, 8:16], qk3[:, :, 0:8],
                                            rope_sin[:, 8:16].unsqueeze(1).broadcast_to(half), ALU.mult).then_inc(sm["rope_parts"], 1)
                    dve.wait_ge(sm["rope_parts"], 3 * n(u))
                    nc.vector.tensor_tensor(qk, cs3, sn3, ALU.add).then_inc(sm["rope_ready"], 1)
                for u in range(U):
                    dve.wait_ge(sm["qkT_done"], n(u))
                    for k in range(KC):
                        spread_queries(nc.vector, sm_qbd[:, u, k, :, :],
                                       bank(u, 1)[:, k * P:(k + 1) * P]).then_inc(sm["qbd_ready"], 1) if k == KC - 1 else \
                            spread_queries(nc.vector, sm_qbd[:, u, k, :, :], bank(u, 1)[:, k * P:(k + 1) * P])
                for u in range(U):
                    dve.wait_ge(sm["scores_done"], n(u))
                    sc = psum[:, 2 * u:2 * u + 2, 0:D].rearrange("p r (j s) -> p r j s", s=S)
                    nc.vector.tensor_reduce(sm_max[:, u, :].rearrange("p (r j) -> p r j", r=2), sc, AX.X, ALU.max).then_inc(sm["max_ready"], 1)
                    dve.wait_ge(sm["max_ready"], n(u))
                    nc.vector.tensor_tensor(sm_p[:, u, :, :].rearrange("p (r j) s -> p r j s", r=2), sc,
                                            sm_max[:, u, :].rearrange("p (r j) -> p r j", r=2).unsqueeze(3).broadcast_to([P, 2, BT * G // 2, S]),
                                            ALU.subtract).then_inc(sm["shifted"], 1)
                for u in range(U):
                    dve.wait_ge(sm["exp_ready"], n(u))
                    nc.vector.tensor_reduce(sm_max[:, u, :], sm_p[:, u, :, :], AX.X, ALU.add).then_inc(sm["sum_ready"], 1)
                    dve.wait_ge(sm["sum_ready"], n(u))
                    nc.vector.reciprocal(sm_rinv[:, u, :], sm_max[:, u, :]).then_inc(sm["rinv_ready"], 1)
                for u in range(U):
                    dve.wait_ge(sm["rinv_ready"], n(u))
                    dve.wait_ge(sm["pv_done"], n(u))
                    pick_heads(psum[:, 2 * u:2 * u + 2, :], sm_rinv[:, u, :], sm_o[:, u, :, :].rearrange("p (b g) d -> p g b d", b=BT)).then_inc(sm["heads_ready"], 1)
                for u in range(U):
                    dve.wait_ge(sm["out_done"], n(u))
                    dve.wait_ge(sm["x_biased"], n(u))
                    nc.vector.tensor_tensor(x[:, U * i + u, :], bank(u, 1)[:, 0:D], x[:, U * i + u, :], ALU.add).then_inc(sm["x_updated"], 1)
                for u in range(U):
                    row_stats(dve, U * i + u, u, sm["x_updated"], n(u), sm["stats_ready"])
                keep_stats(dve, U * i, U, sm["stats_ready"], STATS * (c.before // U + i))
            dve.wait_ge(sm["stats_ready"], 1 + STATS * (c.before + NT) // U)

        def spread_queries(eng, dst, src):
            return eng.tensor_tensor(
                dst.rearrange("p b (l q) -> p b l q", l=L),
                src.rearrange("p (b q) -> p b q", b=BT).unsqueeze(2).broadcast_to([P, BT, L, S]),
                head_scale[:].unsqueeze(1).unsqueeze(3).broadcast_to([P, BT, L, S]), ALU.mult)

        def pick_heads(src, rinv, dst):
            for l in range(L):
                q = slice(S * l, S * l + S)
                v = src[q].rearrange("p k (j l d) -> p l (k j) d", l=L, d=DH)[:, l]
                r = rinv[q].unsqueeze(2).broadcast_to([S, BT * G, DH])
                o = dst[q]
                if len(o.shape) == 4:
                    v, r = (z.rearrange("p (g b) d -> p g b d", g=G) for z in (v, r))
                ins = nc.vector.tensor_tensor(o, v, r, ALU.mult)
            return ins

        STATS = 2 * U + 1

        def row_stats(dve, t, u, updated, count, stats):
            hold(dve, updated, count)
            nc.vector.bn_stats(bn_out[:, u, :], x[:, t, :]).then_inc(stats, 1)

        def keep_stats(dve, t0, n, stats, before):
            for u in range(n):
                hold(dve, stats, 1 + before + n + u)
                nc.vector.bn_aggr(bn_mv[:, u, :], bn_out[:, u, :]).then_inc(stats, 1)
            hold(dve, stats, 1 + before + 2 * n)
            nc.vector.tensor_copy(ln_mv[:, bass.ds(t0, n), :], bn_mv[:, 0:n, :]).then_inc(stats, 1)

        def pool_bias(pool, norm_ready, x_biased, bias_ready, b_o, before=0):
            pool.wait_ge(bias_ready, 1)
            with pool.Fori(0, NT) as t:
                pool.wait_ge(norm_ready, before + t + 1)
                nc.gpsimd.tensor_tensor(x[:, t, :], x[:, t, :], b_o, ALU.add).then_inc(x_biased, 1)

        f8_bias = sb("f8_bias", [P, D])
        f8_ws = sb("f8_ws", [P, 1])
        f8_bits = sb("f8_bits", [P, KC * D], U8)
        f8_w = sb("f8_w", [P, KC, D], BF16)
        f8 = {s: sem(f"ffn0_{s}") for s in (
            "weights_loaded", "w_ready", "norm_ready", "amax_ready", "scale_ready", "inv_ready", "scaled", "exponent_ready",
            "magic_ready", "added", "q_ready", "total_ready", "qT_done", "qT_ready", "out_done", "x_biased", "x_updated",
            "stats_ready")}

        def ffn_weights(dve):
            dve.wait_ge(f8["weights_loaded"], 16 * 3)
            link(dve, nc.vector.tensor_copy(f8_int[:], f8_bits[:]))
            link(dve, nc.vector.tensor_scalar(f8_mag[:], f8_int[:], 127, None, ALU.bitwise_and))
            link(dve, nc.vector.tensor_scalar(f8_high[:], f8_mag[:], 120.0, None, ALU.is_ge))
            link(dve, nc.vector.scalar_tensor_tensor(out=f8_byte[:], in0=f8_high[:], scalar=-8.0, in1=f8_int[:],
                                                     op0=ALU.mult, op1=ALU.add))
            nc.vector.scalar_tensor_tensor(out=f8_w[:].rearrange("p k n -> p (k n)"), in0=f8_high[:], scalar=1.0,
                                           in1=f8_byte[:].bitcast(FP8), op0=ALU.add, op1=ALU.mult).then_inc(f8["w_ready"], 1)

        def ffn_vector(dve):
            dve_rstd(dve, "ffn0")
            with dve.Fori(0, NT // U) as i:
                n = lambda u: U * i + u + 1
                hold(dve, f8["stats_ready"], 1 + STATS * i)
                for u in range(U):
                    dve_normalise(U * i + u, f8_xn[:, u, :]).then_inc(f8["norm_ready"], 1)
                for u in range(U):
                    dve.wait_ge(f8["norm_ready"], n(u))
                    nc.vector.tensor_reduce(f8_amax[:, u:u + 1], f8_xn[:, u, :], AX.X, ALU.max,
                                            apply_absolute_value=True).then_inc(f8["amax_ready"], 1)
                dve.wait_ge(f8["amax_ready"], n(U - 1))
                nc.vector.tensor_scalar(f8_scale[:], f8_amax[:], 1e-12, 1.0 / 448.0, ALU.max, ALU.mult).then_inc(f8["scale_ready"], 1)
                dve.wait_ge(f8["scale_ready"], i + 1)
                nc.vector.reciprocal(f8_inv[:], f8_scale[:]).then_inc(f8["inv_ready"], 1)
                nc.vector.tensor_scalar(f8_total[:], f8_scale[:], f8_ws[:, 0:1], None, ALU.mult).then_inc(f8["total_ready"], 1)
                dve.wait_ge(f8["inv_ready"], i + 1)
                for u in range(U):
                    nc.vector.tensor_scalar(f8_xn[:, u, :], f8_xn[:, u, :], f8_inv[:, u:u + 1], None,
                                            ALU.mult).then_inc(f8["scaled"], 1)
                for u in range(U):
                    dve.wait_ge(f8["scaled"], n(u))
                    nc.vector.tensor_scalar(f8_magic[:, u, :].bitcast(I32), f8_xn[:, u, :].bitcast(I32), 0x7F800000, None,
                                            ALU.bitwise_and).then_inc(f8["exponent_ready"], 1)
                for u in range(U):
                    dve.wait_ge(f8["exponent_ready"], n(u))
                    nc.vector.tensor_scalar(f8_magic[:, u, :], f8_magic[:, u, :], 2.0 ** -6, 1.5 * 2.0 ** 20, ALU.max,
                                            ALU.mult).then_inc(f8["magic_ready"], 1)
                for u in range(U):
                    dve.wait_ge(f8["magic_ready"], n(u))
                    nc.vector.tensor_tensor(f8_xn[:, u, :], f8_xn[:, u, :], f8_magic[:, u, :], ALU.add).then_inc(f8["added"], 1)
                for u in range(U):
                    dve.wait_ge(f8["added"], n(u))
                    nc.vector.tensor_tensor(f8_q[:, u, :], f8_xn[:, u, :], f8_magic[:, u, :], ALU.subtract).then_inc(f8["q_ready"], 1)
                dve.wait_ge(f8["total_ready"], i + 1)
                for u in range(U):
                    t = U * i + u
                    dve.wait_ge(f8["out_done"], n(u))
                    dve.wait_ge(f8["x_biased"], n(u))
                    nc.vector.scalar_tensor_tensor(out=x[:, t, :], in0=bank(u, 1)[:, 0:D], scalar=f8_total[:, u:u + 1],
                                                   in1=x[:, t, :], op0=ALU.mult, op1=ALU.add).then_inc(f8["x_updated"], 1)
                for u in range(U):
                    row_stats(dve, U * i + u, u, f8["x_updated"], n(u), f8["stats_ready"])
                keep_stats(dve, U * i, U, f8["stats_ready"], STATS * i)
            dve.wait_ge(f8["stats_ready"], 1 + STATS * (NT // U))

        def ffn_tensor(pe):
            pe.wait_ge(f8["w_ready"], 1)
            with pe.Fori(0, NT // U) as i:
                n = lambda u: U * i + u + 1
                for u in range(U):
                    pe.wait_ge(f8["q_ready"], n(u))
                    for k in range(KC):
                        mm = nc.tensor.transpose(bank(u, 0).bitcast(BF16)[:, k * P:(k + 1) * P], f8_q[:, u, k * P:(k + 1) * P], ident_b[:])
                    mm.then_inc(f8["qT_done"], 1)
                for u in range(U):
                    pe.wait_ge(f8["qT_ready"], n(u))
                    for k in range(KC):
                        mm = nc.tensor.matmul(bank(u, 1)[:, 0:D], f8_qT[:, u, k, :], f8_w[:, k, :], start=(k == 0), stop=(k == KC - 1))
                    mm.then_inc(f8["out_done"], 1)

        def ffn_scalar(act):
            act_sqrt(act, "ffn0")
            with act.Fori(0, NT // U) as i:
                for u in range(U):
                    act.wait_ge(f8["qT_done"], U * i + u + 1)
                    nc.scalar.activation(f8_qT[:, u, :, :].rearrange("p k s -> p (k s)"), bank(u, 0).bitcast(BF16)[:, 0:D],
                                         ACT.Copy).then_inc(f8["qT_ready"], 1)

        x1_xn = sm_xn
        x1_wq = sb("x1_wq", [P, KC, D])
        x1_wk = sb("x1_wk", [P, KC, D])
        x1_wv = sb("x1_wv", [P, KC, D])
        x1_wo = sb("x1_wo", [P, KC, D])
        x1_bq = sb("x1_bq", [P, KC])
        x1_bk = sb("x1_bk", [P, KC])
        x1_bv = sb("x1_bv", [P, KC, P])
        x1_bo = sb("x1_bo", [P, D])
        x1_ctx = [sb(f"x1_ctx{n}", [P, KC, BT * SK + BT * G]) for n in range(2)]
        x1_mask8 = sb("x1_mask8", [S, BT, SK], U8)
        hide = sb("hide", [S, L, S])
        hide_b = sb("hide_b", [S, L, S], BF16)
        row_pick = sb("row_pick", [BT * G, BT * G])
        x1 = {s: sem(f"xattn1_{s}") for s in (
            "weights_loaded", "bias_product", "bias_ready", "norm_ready", "xT_done", "xT_ready", "q_done", "q_ready",
            "ctx0", "ctx1", "mask_loaded", "mask_ready", "qbd_ready", "kv0_done", "kv1_done", "kv0_free", "kv1_free",
            "scores_done", "max_ready", "exp_ready", "pT_done", "pT_ready", "pv_done",
            "plT_ready", "last_done", "vl_read", "vlbd_ready", "rinv_ready", "heads_ready", "out_read", "x_biased", "x_updated",
            "stats_ready", "tile_done")}
        J = BT * G

        def x1q_vector(dve):
            dve_rstd(dve, "xattn1")
            dve.wait_ge(x1["weights_loaded"], 16 * 8)
            dve.wait_ge(x1["bias_product"], 1)
            nc.vector.tensor_tensor(x1_bo[:], bank(0, 0)[:, 0:D], x1_bo[:], ALU.add).then_inc(x1["bias_ready"], 1)
            with dve.Fori(0, NT // U) as i:
                for u in range(U):
                    dve.wait_ge(x1["xT_done"], 1 + U * i)
                    dve_normalise(U * i + u, x1_xn[:, u, :]).then_inc(x1["norm_ready"], 1)

        def x1q_tensor(pe):
            pe.wait_ge(x1["weights_loaded"], 16 * 8)
            for k in range(KC):
                mm = nc.tensor.matmul(bank(0, 0)[:, 0:D], x1_bv[:, k, :], x1_wo[:, k, :], start=(k == 0), stop=(k == KC - 1))
            mm.then_inc(x1["bias_product"], 1)
            pe.wait_ge(x1["bias_ready"], 1)
            with pe.Fori(0, NT // U) as i:
                for u in range(U):
                    pe.wait_ge(x1["norm_ready"], U * i + u + 1)
                    for k in range(KC):
                        mm = nc.tensor.transpose(bank(u, 0)[:, k * P:(k + 1) * P], x1_xn[:, u, k * P:(k + 1) * P], ident[:])
                    mm.then_inc(x1["xT_done"], 1)
                pe.wait_ge(x1["xT_ready"], U * (i + 1))
                for m in range(KC):
                    for k in range(KC):
                        mm = nc.tensor.matmul(bank(m, 1), x1_wq[:, k, m * P:(m + 1) * P], x1_xT[:, k, :],
                                              start=(k == 0), stop=(k == KC - 1))
                    mm.then_inc(x1["q_done"], 1)

        def x1q_scalar(act):
            act_sqrt(act, "xattn1")
            with act.Fori(0, NT // U) as i:
                for u in range(U):
                    act.wait_ge(x1["xT_done"], 1 + U * i + u + 1)
                    nc.scalar.activation(x1_xT[:, :, u * P:(u + 1) * P], bank(u, 0)[:, 0:D].rearrange("p (k s) -> p k s", k=KC),
                                         ACT.Copy).then_inc(x1["xT_ready"], 1)
                for m in range(KC):
                    hold(act, x1["q_done"], KC * i + m + 1)
                    nc.scalar.activation(x1_qT[:, m, bass.ds(i * (U * P), U * P)], bank(m, 1), ACT.Identity,
                                         bias=x1_bq[:, m:m + 1]).then_inc(x1["q_ready"], 1)

        PIECES = 16

        def kv_bank(n):
            return psum[:, n % 2, :]

        def piece_of(kind, b=0):
            return {"vl": 0, "k0": 1 + 3 * b, "k1": 2 + 3 * b, "v": 3 + 3 * b, "plT": 13, "oT": 14, "out": 15}[kind]

        def kv_free(eng, n, t):
            eng.wait_ge(x1[f"kv{n % 2}_free"], PIECES // 2 * t + n // 2 + 1)

        def kv_done(eng, n, t):
            eng.wait_ge(x1[f"kv{n % 2}_done"], PIECES // 2 * t + n // 2 + 1)

        def x1_tile_tensor(pe, t, par):
            ct = x1_ctx[par]
            pe.wait_ge(x1[f"ctx{par}"], 16 * (t // 2 + 1) if isinstance(t, int) else (t - par) * 8 + 16)

            def piece(kind, b=0):
                n = piece_of(kind, b)
                kv_free(pe, n, t)
                out = kv_bank(n)
                if kind == "vl":
                    for k in range(KC):
                        mm = nc.tensor.matmul(out[0:J, 0:D], ct[:, k, BT * SK:], x1_wv[:, k, :],
                                              start=(k == 0), stop=(k == KC - 1))
                elif kind in ("k0", "k1"):
                    m = int(kind[1])
                    for k in range(KC):
                        mm = nc.tensor.matmul(out[:, 0:SK], x1_wk[:, k, m * P:(m + 1) * P], ct[:, k, b * SK:(b + 1) * SK],
                                              start=(k == 0), stop=(k == KC - 1))
                elif kind == "v":
                    for c in range(2):
                        for k in range(KC):
                            mm = nc.tensor.matmul(out[:, c * D:(c + 1) * D], ct[:, k, b * SK + c * P:b * SK + (c + 1) * P], x1_wv[:, k, :],
                                                  start=(k == 0), stop=(k == KC - 1), skip_group_check=True)
                elif kind == "plT":
                    mm = nc.tensor.transpose(out[0:J, 0:P], x1_p[:, :, SK - 1], ident[:])
                elif kind == "oT":
                    pe.wait_ge(x1["heads_ready"], t + 1)
                    for k in range(BT // 2):
                        mm = nc.tensor.transpose(out[:, k * P:(k + 1) * P],
                                                 x1_o[:, k * 2 * G:(k + 1) * 2 * G, :].rearrange("p j d -> p (j d)"), ident[:])
                elif kind == "out":
                    kv_free(pe, n + 1, t)
                    for k in range(KC):
                        mm = nc.tensor.matmul(out[:, 0:D], x1_oT[:, k, :, :].rearrange("p b s -> p (b s)"), x1_wo[:, k, :],
                                              start=(k == 0), stop=(k == KC - 1))
                mm.then_inc(x1[f"kv{n % 2}_done"], 1)

            piece("vl")
            for kind in ("k0", "k1", "v"):
                piece(kind, 0)
            rest = [(kind, b) for b in range(1, BT) for kind in ("k0", "k1", "v")]
            pe.wait_ge(x1["qbd_ready"], t + 1)
            for s in range(J + 3):
                if s < J:
                    b, g = s // G, s % G
                    r, k = 64 * (g % 2), g // 2
                    if g == 0:
                        kv_free(pe, piece_of("k1", b) + 2, t)
                        kv_free(pe, piece_of("k0", b) + 2, t)
                    if s == 0:
                        pe.wait_ge(x1["mask_ready"], 1 + t + 1)
                    if s >= 2:
                        pe.wait_ge(x1["exp_ready"], J * t + s - 1)
                    sc = psum[:, 2 + s % 2, 0:SK]
                    nc.tensor.matmul(sc, hide_b[:].rearrange("p l q -> p (l q)"), x1_mask[par][:, b, :], start=True, stop=False)
                    nc.tensor.matmul(sc, x1_qbd[r:r + 64, k, b, :], x1_k[r:r + 64, b % 2, k, :],
                                     start=False, stop=True).then_inc(x1["scores_done"], 1)
                if rest and (s % 4 != 3):
                    piece(*rest.pop(0))
                if 2 <= s < J + 2:
                    j = s - 2
                    pe.wait_ge(x1["exp_ready"], J * t + j + 1)
                    if j >= 2:
                        pe.wait_ge(x1["pT_ready"], J * t + j - 1)
                    for c in range(2):
                        mm = nc.tensor.transpose(psum[:, 4 + j % 2, c * P:(c + 1) * P], x1_p[:, j, c * P:(c + 1) * P], ident[:])
                    mm.then_inc(x1["pT_done"], 1)
                if s >= 3:
                    j = s - 3
                    b, g = j // G, j % G
                    pe.wait_ge(x1["pT_ready"], J * t + j + 1)
                    if g == 0:
                        kv_free(pe, piece_of("v", b) + 2, t)
                    for c in range(2):
                        mm = nc.tensor.matmul(psum[:, 6 + b // 2, (b % 2) * D + g * 64:(b % 2) * D + (g + 1) * 64],
                                              x1_pT[:, j % 2, c, :], x1_v[:, b % 2, c, g * 64:(g + 1) * 64],
                                              start=(b % 2 == 0 and g == 0 and c == 0), stop=False, skip_group_check=True)
                    mm.then_inc(x1["pv_done"], 1)
            piece("plT")
            kv_free(pe, piece_of("plT") + 2, t)
            pe.wait_ge(x1["vlbd_ready"], t + 1)
            for k in range(2):
                mm = nc.tensor.matmul(psum[:, 6 + k, :], x1_plT[:], x1_vlbd[:, k * 8:(k + 1) * 8, :].rearrange("p j d -> p (j d)"),
                                      start=False, stop=True, skip_group_check=True)
            mm.then_inc(x1["last_done"], 1)
            piece("oT")
            piece("out")

        def x1_tensor(pe):
            pe.wait_ge(x1["q_ready"], KC * NT // U)
            for k in range(2):
                pe.sem_inc(x1[f"kv{k}_free"], 1)
            with pe.Fori(0, NT // 2) as i:
                for par in range(2):
                    x1_tile_tensor(pe, 2 * i + par, par)

        def x1_scalar(act):
            nc.scalar.preload_act_table(ACT.Exp)
            with act.Fori(0, NT) as t:
                def keys(b):
                    if b >= 2:
                        act.wait_ge(x1["scores_done"], 1 + J * t + (b - 1) * G)
                    for m in range(KC):
                        n = piece_of(f"k{m}", b)
                        kv_done(act, n, t)
                        nc.scalar.activation(x1_k[:, b % 2, m, :], kv_bank(n)[:, 0:SK], ACT.Identity,
                                             bias=x1_bk[:, m:m + 1]).then_inc(x1[f"kv{n % 2}_free"], 1)

                keys(0)
                for s in range(J):
                    act.wait_ge(x1["max_ready"], J * t + s + 1)
                    nc.scalar.activation(x1_p[:, s, :], psum[:, 2 + s % 2, 0:SK], ACT.Exp, bias=x1_nmax[:, s:s + 1],
                                         accum_out=x1_sum[:, s:s + 1]).then_inc(x1["exp_ready"], 1)
                    if s % 4 == 1 and s // 4 + 1 < BT:
                        keys(s // 4 + 1)
                n = piece_of("oT")
                kv_done(act, n, t)
                spread_heads(nc.scalar.copy, kv_bank(n), x1_oT[:]).then_inc(x1[f"kv{n % 2}_free"], 1)

        def x1_vector(dve):
            dve.wait_ge(x1["x_biased"], NT)
            with dve.Fori(0, NT) as t:
                def values(b):
                    n = piece_of("v", b)
                    kv_done(dve, n, t)
                    if b >= 2:
                        dve.wait_ge(x1["pv_done"], J * t + (b - 1) * G)
                    nc.vector.tensor_copy(x1_v[:, b % 2, :, :].rearrange("p c n -> p (c n)"), kv_bank(n)).then_inc(x1[f"kv{n % 2}_free"], 1)

                dve.wait_ge(x1["stats_ready"], 1 + 3 * t)
                n = piece_of("vl")
                kv_done(dve, n, t)
                nc.vector.tensor_copy(x1_vl[:], kv_bank(n)[0:J, 0:D]).then_inc(x1[f"kv{n % 2}_free"], 1)
                values(0)
                for s in range(J + 2):
                    if s < J:
                        dve.wait_ge(x1["scores_done"], 1 + J * t + s + 1)
                        nc.vector.tensor_reduce(x1_nmax[:, s:s + 1], psum[:, 2 + s % 2, 0:SK], AX.X, ALU.max,
                                                negate=True).then_inc(x1["max_ready"], 1)
                    if s >= 2:
                        j = s - 2
                        dve.wait_ge(x1["pT_done"], J * t + j + 1)
                        if j >= 2:
                            dve.wait_ge(x1["pv_done"], J * t + j - 1)
                        nc.vector.tensor_copy(x1_pT[:, j % 2, :, :].rearrange("p c n -> p (c n)"),
                                              psum[:, 4 + j % 2, 0:D]).then_inc(x1["pT_ready"], 1)
                    if s % 4 == 3 and s // 4 + 1 < BT:
                        values(s // 4 + 1)
                n = piece_of("plT")
                kv_done(dve, n, t)
                nc.vector.tensor_copy(x1_plT[:], kv_bank(n)[0:J, 0:P]).then_inc(x1[f"kv{n % 2}_free"], 1)
                dve.wait_ge(x1["exp_ready"], J * (t + 1))
                nc.vector.tensor_scalar(x1_void[:], x1_nmax[:], 1e10, 0.0, ALU.mult, ALU.mult).then_inc(x1["rinv_ready"], 1)
                nc.vector.reciprocal(x1_rinv[:], x1_sum[:]).then_inc(x1["rinv_ready"], 1)
                dve.wait_ge(x1["rinv_ready"], 3 * t + 2)
                nc.vector.tensor_tensor(x1_rinv[:], x1_rinv[:], x1_void[:], ALU.add).then_inc(x1["rinv_ready"], 1)
                dve.wait_ge(x1["rinv_ready"], 3 * t + 3)
                dve.wait_ge(x1["last_done"], 1 + t + 1)
                pick_heads(psum[:, 6:8, :], x1_rinv[:], x1_o[:]).then_inc(x1["heads_ready"], 1)
                n = piece_of("out")
                kv_done(dve, n, t)
                nc.vector.tensor_tensor(x[:, t, :], kv_bank(n)[:, 0:D], x[:, t, :], ALU.add).then_inc(x1[f"kv{n % 2}_free"], 1)
                hold(dve, x1[f"kv{n % 2}_free"], PIECES // 2 * (t + 1) + 1)
                nc.vector.bn_stats(bn_out[:, 0, :], x[:, t, :]).then_inc(x1["stats_ready"], 1)
                keep_stats(dve, t, 1, x1["stats_ready"], 3 * t)
            dve.wait_ge(x1["stats_ready"], 1 + 3 * NT)

        def x1_pool(pool):
            pool.wait_ge(x1["q_ready"], KC * NT // U)
            with pool.Fori(0, NT // 2) as i:
                for par in range(2):
                    t = 2 * i + par
                    hold(pool, x1["mask_loaded"], 16 * (t + 1))
                    nc.gpsimd.tensor_copy(x1_mask[par][:], x1_mask8[:]).then_inc(x1["mask_ready"], 1)
                    pool.wait_ge(x1["scores_done"], 1 + J * t)
                    for k in range(KC):
                        ins = nc.gpsimd.tensor_tensor(
                            x1_qbd[:, k, :, :].rearrange("p b (l q) -> p b l q", l=L),
                            x1_qT[:, k, bass.ds(t * P, P)].rearrange("p (b q) -> p b q", b=BT).unsqueeze(2).broadcast_to([P, BT, L, S]),
                            head_scale[:].unsqueeze(1).unsqueeze(3).broadcast_to([P, BT, L, S]), ALU.mult)
                    ins.then_inc(x1["qbd_ready"], 1)
                    pool.wait_ge(x1["last_done"], 1 + t)
                    kv_free(pool, piece_of("vl") + 2, t)
                    nc.gpsimd.tensor_tensor(
                        x1_vlbd[:].rearrange("p (b g) d -> p b g d", b=BT),
                        x1_vl[:].rearrange("p (g d) -> p g d", g=G).unsqueeze(1).broadcast_to([J, BT, G, 64]),
                        row_pick[:].rearrange("p (b g) -> p b g", b=BT).unsqueeze(3).broadcast_to([J, BT, G, 64]),
                        ALU.mult).then_inc(x1["vlbd_ready"], 1)

        mx_w1 = sb("mx_w1", [P, KC, GH])
        mx_b1 = sb("mx_b1", [GH, 1])
        mx_w2 = sb("mx_w2", [GH, R])
        mx_b2 = sb("mx_b2", [R, 1])
        mx_wu = sb("mx_wu", [P, KC, R])
        mx_wv = sb("mx_wv", [P, KC, R])
        mx_conv = sb("mx_conv", [P, KC, 3])
        mx_wo = sb("mx_wo", [R, D])
        mx_bo = sb("mx_bo", [P, D])
        mx_keep = sb("mx_keep", [R, U * P])
        mx = {s: sem(f"mix1_{s}") for s in (
            "weights_loaded", "taps_ready", "bias_ready", "norm_ready", "xT_done", "xT_ready", "h_done", "h_ready", "uv_done",
            "gate_done", "gate_ready", "sum_ready", "gu_ready", "glob_ready", "out_done", "x_biased", "x_updated", "stats_ready")}

        def mix_vector(dve):
            dve.wait_ge(mx["weights_loaded"], 16 * 10)
            for k in range(KC):
                for j in range(3):
                    nc.vector.tensor_scalar(mx_taps[:, k, j, :], ident[:], mx_conv[:, k, j:j + 1], None,
                                            ALU.mult).then_inc(mx["taps_ready"], 1)
            nc.vector.memset(mx_xT[:], 0.0).then_inc(mx["taps_ready"], 1)
            dve_rstd(dve, "mix1")
            with dve.Fori(0, NT // U) as i:
                n = lambda u: U * i + u + 1
                hold(dve, mx["stats_ready"], 1 + STATS * i)
                for u in range(U):
                    dve_normalise(U * i + u, sm_xn[:, u, :]).then_inc(mx["norm_ready"], 1)
                dve.wait_ge(mx["uv_done"], i + 1)
                nc.vector.tensor_tensor_scan(mx_sum[:], mx_keep[:], psum[0:R, 3, :], 0.0, ALU.mult, ALU.add).then_inc(mx["sum_ready"], 1)
                dve.wait_ge(mx["gate_ready"], i + 1)
                nc.vector.tensor_tensor(mx_gu[:], psum[0:R, 5, :], mx_gate[:], ALU.mult).then_inc(mx["gu_ready"], 1)
                dve.wait_ge(mx["gu_ready"], i + 1)
                dve.wait_ge(mx["sum_ready"], i + 1)
                nc.vector.tensor_tensor(mx_glob[:], mx_gu[:], mx_sum[:], ALU.mult).then_inc(mx["glob_ready"], 1)
                for u in range(U):
                    dve.wait_ge(mx["out_done"], n(u))
                    dve.wait_ge(mx["x_biased"], n(u))
                    nc.vector.tensor_tensor(x[:, U * i + u, :], bank(u, 0)[:, 0:D], x[:, U * i + u, :], ALU.add).then_inc(mx["x_updated"], 1)
                for u in range(U):
                    row_stats(dve, U * i + u, u, mx["x_updated"], n(u), mx["stats_ready"])
                keep_stats(dve, U * i, U, mx["stats_ready"], STATS * i)
            dve.wait_ge(mx["stats_ready"], 1 + STATS * (NT // U))

        def mix_tensor(pe):
            pe.wait_ge(mx["weights_loaded"], 16 * 10)
            pe.wait_ge(mx["taps_ready"], 3 * KC + 1)
            with pe.Fori(0, NT // U) as i:
                for u in range(U):
                    pe.wait_ge(mx["norm_ready"], U * i + u + 1)
                    for k in range(KC):
                        mm = nc.tensor.transpose(bank(u, 0)[:, k * P:(k + 1) * P], sm_xn[:, u, k * P:(k + 1) * P], ident[:])
                    mm.then_inc(mx["xT_done"], 1)
                pe.wait_ge(mx["xT_ready"], U * (i + 1))
                rows = [mx_xT[:, 1, k, 1:1 + U * P] for k in range(KC)]
                for k in range(KC):
                    mm = nc.tensor.matmul(psum[0:GH, 1, :], mx_w1[:, k, :], rows[k], start=(k == 0), stop=(k == KC - 1))
                mm.then_inc(mx["h_done"], 1)
                for w, q in ((mx_wv, 3), (mx_wu, 5)):
                    for k in range(KC):
                        mm = nc.tensor.matmul(psum[0:R, q, :], w[:, k, :], rows[k], start=(k == 0), stop=(k == KC - 1))
                mm.then_inc(mx["uv_done"], 1)
                hold(pe, mx["h_ready"], i + 1)
                nc.tensor.matmul(psum[0:R, 7, :], mx_w2[:], mx_h[:], start=True, stop=True).then_inc(mx["gate_done"], 1)
                for u in range(U):
                    for k in range(KC):
                        for j in range(3):
                            nc.tensor.matmul(bank(u, 0)[:, k * P:(k + 1) * P], mx_xT[:, j, k, u * P + j:(u + 1) * P + j],
                                             mx_taps[:, k, j, :], start=(k == 0 and j == 0), stop=False, skip_group_check=True)
                pe.wait_ge(mx["glob_ready"], i + 1)
                for u in range(U):
                    nc.tensor.matmul(bank(u, 0)[:, 0:D], mx_glob[:, u * P:(u + 1) * P], mx_wo[:], start=False, stop=True,
                                     skip_group_check=True).then_inc(mx["out_done"], 1)

        def mix_scalar(act):
            act_sqrt(act, "mix1")
            nc.scalar.preload_act_table(ACT.Sigmoid)
            act.wait_ge(mx["taps_ready"], 3 * KC + 1)
            with act.Fori(0, NT // U) as i:
                for u in range(U):
                    act.wait_ge(mx["xT_done"], U * i + u + 1)
                    for j, (s0, s1) in enumerate(((0, S - 1), (0, S), (1, S))):
                        src = bank(u, 0)[:, 0:D].rearrange("p (k b s) -> p k b s", k=KC, b=BT)
                        dst = mx_xT[:, j, :, 1 + u * P:1 + (u + 1) * P].rearrange("p k (b s) -> p k b s", b=BT)
                        ins = nc.scalar.activation(dst[:, :, :, s0:s1], src[:, :, :, s0:s1], ACT.Copy)
                    ins.then_inc(mx["xT_ready"], 1)
                act.wait_ge(mx["h_done"], i + 1)
                nc.scalar.activation(mx_h[:], psum[0:GH, 1, :], ACT.Relu, bias=mx_b1[:, 0:1]).then_inc(mx["h_ready"], 1)
                act.wait_ge(mx["gate_done"], i + 1)
                nc.scalar.activation(mx_gate[:], psum[0:R, 7, :], ACT.Sigmoid, bias=mx_b2[:, 0:1]).then_inc(mx["gate_ready"], 1)

        me_raw = sb("me_raw", [P, 2, 1024])
        me_b1 = sb("me_b1", [P, EX, HM])
        me_b2 = sb("me_b2", [EX, D])
        me_rw = sb("me_rw", [P, KC, E])
        me_rb = sb("me_rb", [P, E])
        me_before = sb("me_before", [P, E, E])
        me = {s: sem(f"moe1_{s}") for s in (
            "weights_loaded", "router_split", "norm_ready", "xT_done", "xh_ready", "xl_ready", "logits_done", "logits_read",
            "exp_ready", "gate_ready", "gT_done", "gT_ready", "b2_done", "b2_added", "raw_loaded", "w1h", "w1_split", "w2_split",
            "up_done", "h_ready", "hh_ready", "hl_ready", "down_done", "acc_ready", "stored")}

        def moe_prep_vector(dve):
            dve.wait_ge(me["weights_loaded"], 16 * 5)
            link(dve, nc.vector.tensor_copy(me_rwh[:], me_rw[:]))
            link(dve, nc.vector.tensor_tensor(me_rwl[:], me_rw[:], me_rwh[:].bitcast(F32), ALU.subtract))
            nc.vector.memset(me_gate[:], 1.0).then_inc(me["router_split"], 1)
            dve_rstd(dve, "moe1")
            with dve.Fori(0, NT // U) as i:
                for u in range(U):
                    dve_normalise(U * i + u, sm_xn[:, u, :]).then_inc(me["norm_ready"], 1)
                for u in range(U):
                    t = U * i + u
                    dve.wait_ge(me["xh_ready"], t + 1)
                    nc.vector.tensor_tensor(me_xl[:, :, bass.ds(t * P, P)], bank(u, 0)[:, 0:D].rearrange("p (k s) -> p k s", k=KC),
                                            me_xh[:, :, bass.ds(t * P, P)].bitcast(F32), ALU.subtract).then_inc(me["xl_ready"], 1)
            dve.wait_ge(me["logits_done"], NT)
            dve.wait_ge(me["router_split"], 1)
            wide = [P, NT, E]
            link(dve, nc.vector.tensor_tensor(me_pr[:], logits(), me_rb[:].unsqueeze(1).broadcast_to(wide), ALU.add))
            link(dve, nc.vector.tensor_reduce(me_st[:], me_pr[:], AX.X, ALU.max))
            nc.vector.tensor_tensor(me_pr[:], me_pr[:], me_st[:].unsqueeze(2).broadcast_to(wide), ALU.subtract).then_inc(me["logits_read"], 1)
            dve.wait_ge(me["exp_ready"], 1)
            link(dve, nc.vector.tensor_reduce(me_st[:], me_pr[:], AX.X, ALU.add))
            link(dve, nc.vector.reciprocal(me_st[:], me_st[:]))
            link(dve, nc.vector.tensor_tensor(me_pr[:], me_pr[:], me_st[:].unsqueeze(2).broadcast_to(wide), ALU.mult))
            full = [P, NT, E, E]
            mine, other = me_pr[:].unsqueeze(3).broadcast_to(full), me_pr[:].unsqueeze(2).broadcast_to(full)
            link(dve, nc.vector.tensor_tensor(me_cmp[:], other, mine, ALU.is_equal))
            link(dve, nc.vector.tensor_tensor(me_cmp[:], me_cmp[:], me_before[:].unsqueeze(1).broadcast_to(full), ALU.mult))
            link(dve, nc.vector.tensor_tensor(me_cmp2[:], other, mine, ALU.is_gt))
            link(dve, nc.vector.tensor_tensor(me_cmp[:], me_cmp[:], me_cmp2[:], ALU.add))
            link(dve, nc.vector.tensor_reduce(me_rank[:], me_cmp[:], AX.X, ALU.add))
            link(dve, nc.vector.tensor_scalar(me_rank[:], me_rank[:], 2.0, None, ALU.is_lt))
            nc.vector.tensor_tensor(me_gate[:, :, 0:E], me_rank[:], me_pr[:], ALU.mult).then_inc(me["gate_ready"], 1)
            with dve.Fori(0, NT // U) as i:
                for u in range(U):
                    dve.wait_ge(me["b2_done"], U * i + u + 1)
                    nc.vector.tensor_tensor(x[:, U * i + u, :], bank(u, 1)[:, 0:D], x[:, U * i + u, :], ALU.add).then_inc(me["b2_added"], 1)

        def logits():
            return bank(0, 1)[:, 0:NT * E].rearrange("p (t e) -> p t e", t=NT)

        def moe_prep_tensor(pe):
            pe.wait_ge(me["router_split"], 1)
            with pe.Fori(0, NT // U) as i:
                for u in range(U):
                    pe.wait_ge(me["norm_ready"], U * i + u + 1)
                    for k in range(KC):
                        mm = nc.tensor.transpose(bank(u, 0)[:, k * P:(k + 1) * P], sm_xn[:, u, k * P:(k + 1) * P], ident[:])
                    mm.then_inc(me["xT_done"], 1)
                pe.wait_ge(me["xl_ready"], U * (i + 1))
            for t in range(NT):
                for n, (v, w) in enumerate(((me_xh, me_rwh), (me_xh, me_rwl), (me_xl, me_rwh))):
                    for k in range(KC):
                        mm = nc.tensor.matmul(bank(0, 1)[:, t * E:(t + 1) * E], v[:, k, t * P:(t + 1) * P], w[:, k, :],
                                              start=(n == 0 and k == 0), stop=(n == 2 and k == KC - 1), skip_group_check=True)
                mm.then_inc(me["logits_done"], 1)
            pe.wait_ge(me["gate_ready"], 1)
            for i in range(NT // U):
                for u in range(U):
                    nc.tensor.transpose(bank(u, 0)[0:EX, 0:P], me_gate[:, U * i + u, :], ident[:]).then_inc(me["gT_done"], 1)
                for u in range(U):
                    pe.wait_ge(me["gT_ready"], U * i + u + 1)
                    if i > 0:
                        pe.wait_ge(me["b2_added"], U * (i - 1) + u + 1)
                    nc.tensor.matmul(bank(u, 1)[:, 0:D], me_gT[:, u, :], me_b2[:], start=True, stop=True).then_inc(me["b2_done"], 1)

        def moe_prep_scalar(act):
            act_sqrt(act, "moe1")
            with act.Fori(0, NT // U) as i:
                for u in range(U):
                    t = U * i + u
                    hold(act, me["xT_done"], t + 1)
                    nc.scalar.activation(me_xh[:, :, bass.ds(t * P, P)], bank(u, 0)[:, 0:D].rearrange("p (k s) -> p k s", k=KC),
                                         ACT.Copy).then_inc(me["xh_ready"], 1)
            act.wait_ge(me["logits_read"], 1)
            nc.scalar.activation(me_pr[:], me_pr[:], ACT.Exp).then_inc(me["exp_ready"], 1)
            for i in range(NT // U):
                for u in range(U):
                    act.wait_ge(me["gT_done"], U * i + u + 1)
                    if i > 0:
                        act.wait_ge(me["b2_done"], U * (i - 1) + u + 1)
                    nc.scalar.copy(me_gT[:, u, :], bank(u, 0)[0:EX, 0:P]).then_inc(me["gT_ready"], 1)

        NG = NT // TG

        def down_psum(gr, tau):
            return psum[:, 4 + 2 * (gr % 2) + tau // 2, (tau % 2) * D:(tau % 2) * D + D]

        def moe_tensor(pe):
            pe.wait_ge(me["b2_added"], NT)
            pairs = lambda vh, vl, wh, wl: ((vh, wh), (vh, wl), (vl, wh))
            with pe.Fori(0, EX) as e:
                pe.wait_ge(me["w1_split"], e + 1)
                for gr in range(NG):
                    done = NG * e + gr
                    toks = slice(gr * 512, (gr + 1) * 512)
                    for m in range(HM):
                        n = 0
                        for k in range(KC):
                            cols = slice(k * 512 + m * P, k * 512 + (m + 1) * P)
                            for w, v in pairs(me_wh[:, 0, cols], me_wl[:, 0, cols], me_xh[:, k, toks], me_xl[:, k, toks]):
                                mm = nc.tensor.matmul(psum[:, m, :], w, v, start=(n == 0), stop=(n == 5))
                                n += 1
                        mm.then_inc(me["up_done"], 1)
                    if gr == 0:
                        pe.wait_ge(me["w2_split"], 1 + e + 1)
                    if gr >= 2:
                        pe.wait_ge(me["acc_ready"], TG * (done - 1))
                    for m in range(HM):
                        pe.wait_ge(me["hl_ready"], HM * done + m + 1)
                        w2 = slice(m * D, (m + 1) * D)
                        for tau in range(TG):
                            rows = slice(tau * P, (tau + 1) * P)
                            for n, (v, w) in enumerate(pairs(me_hh[:, m, rows], me_hl[:, m, rows], me_wh[:, 1, w2], me_wl[:, 1, w2])):
                                mm = nc.tensor.matmul(down_psum(gr, tau), v, w, start=(m == 0 and n == 0 and tau % 2 == 0),
                                                      stop=(m == HM - 1 and n == 2), skip_group_check=True)
                    mm.then_inc(me["down_done"], 1)

        def moe_scalar(act):
            nc.scalar.preload_act_table(ACT.Gelu)
            with act.Fori(0, EX) as e:
                for gr in range(NG):
                    for m in range(HM):
                        n = HM * (NG * e + gr) + m + 1
                        hold(act, me["up_done"], 1 + n)
                        nc.scalar.activation(me_h[:, m, :], psum[:, m, :], ACT.Gelu, bias=me_b1[:, e, m:m + 1]).then_inc(me["h_ready"], 1)

        def split(dve, high, low, src, sem_h, count, sem_l):
            nc.vector.tensor_copy(high, src).then_inc(sem_h, 1)
            dve.wait_ge(sem_h, count)
            nc.vector.tensor_tensor(low, src, high.bitcast(F32), ALU.subtract).then_inc(sem_l, 1)

        def moe_vector(dve):
            with dve.Fori(0, EX) as e:
                dve.wait_ge(me["raw_loaded"], 16 * (e + 1))
                dve.wait_ge(me["up_done"], 1 + HM * NG * e)
                split(dve, me_wh[:, 0, :], me_wl[:, 0, :], me_raw[:, 0, :], me["w1h"], 2 * e + 1, me["w1_split"])
                dve.wait_ge(me["down_done"], 1 + NG * e)
                split(dve, me_wh[:, 1, :], me_wl[:, 1, :], me_raw[:, 1, :], me["w1h"], 2 * e + 2, me["w2_split"])
                for gr in range(NG):
                    for m in range(HM):
                        n = HM * (NG * e + gr) + m + 1
                        dve.wait_ge(me["h_ready"], n)
                        split(dve, me_hh[:, m, :], me_hl[:, m, :], me_h[:, m, :], me["hh_ready"], n, me["hl_ready"])
                    dve.wait_ge(me["down_done"], 1 + NG * e + gr + 1)
                    for tau in range(TG):
                        t = TG * gr + tau
                        nc.vector.scalar_tensor_tensor(out=x[:, t, :], in0=down_psum(gr, tau), scalar=me_gate[:, t, bass.ds(e, 1)],
                                                       in1=x[:, t, :], op0=ALU.mult, op1=ALU.add).then_inc(me["acc_ready"], 1)

        with Scratch() as scratch:
            sm_xT = scratch("sm_xT", [P, U, KC, P])
            sm_cT = scratch("sm_cT", [P, U, KC, P])
            sm_qk = scratch("sm_qk", [P, U, 2, D])
            sm_cosd = scratch("sm_cosd", [P, U, 2, D])
            sm_sind = scratch("sm_sind", [P, U, 2, D])
            sm_vbd = scratch("sm_vbd", [P, U, BT, D])
            sm_qbd = scratch("sm_qbd", [P, U, KC, BT, P])
            sm_kT = scratch("sm_kT", [P, U, KC, P])
            sm_p = scratch("sm_p", [P, U, BT * G, S])
            sm_max = scratch("sm_max", [P, U, BT * G])
            sm_rinv = scratch("sm_rinv", [P, U, BT * G])
            sm_pT = scratch("sm_pT", [P, U, G, P])
            sm_o = scratch("sm_o", [P, U, BT * G, DH])
            sm_oT = scratch("sm_oT", [P, U, KC, BT, S])
            f8_xn = scratch("f8_xn", [P, U, D])
            f8_magic = scratch("f8_magic", [P, U, D])
            f8_q = scratch("f8_q", [P, U, D], BF16)
            f8_qT = scratch("f8_qT", [P, U, KC, P], BF16)
            f8_amax = scratch("f8_amax", [P, U])
            f8_scale = scratch("f8_scale", [P, U])
            f8_inv = scratch("f8_inv", [P, U])
            f8_total = scratch("f8_total", [P, U])
            f8_int = scratch("f8_int", [P, KC * D], I32)
            f8_mag = scratch("f8_mag", [P, KC * D], I32)
            f8_high = scratch("f8_high", [P, KC * D])
            f8_byte = scratch("f8_byte", [P, KC * D], U8)
        with Scratch() as scratch:
            x1_xT = scratch("x1_xT", [P, KC, U * P])
            x1_qT = scratch("x1_qT", [P, KC, NT * P])
            x1_mask = [scratch(f"x1_mask{n}", [S, BT, SK], BF16) for n in range(2)]
            x1_qbd = scratch("x1_qbd", [P, KC, BT, P])
            x1_k = scratch("x1_k", [P, 2, KC, SK])
            x1_v = scratch("x1_v", [P, 2, 2, D])
            x1_vl = scratch("x1_vl", [BT * G, D])
            x1_vlbd = scratch("x1_vlbd", [BT * G, BT * G, 64])
            x1_p = scratch("x1_p", [P, BT * G, SK])
            x1_nmax = scratch("x1_nmax", [P, BT * G])
            x1_sum = scratch("x1_sum", [P, BT * G])
            x1_rinv = scratch("x1_rinv", [P, BT * G])
            x1_void = scratch("x1_void", [P, BT * G])
            x1_pT = scratch("x1_pT", [P, 2, 2, P])
            x1_plT = scratch("x1_plT", [BT * G, P])
            x1_o = scratch("x1_o", [P, BT * G, DH])
            x1_oT = scratch("x1_oT", [P, KC, BT, S])
            mx_taps = scratch("mx_taps", [P, KC, 3, P])
            mx_xT = scratch("mx_xT", [P, 3, KC, U * P + 2])
            mx_h = scratch("mx_h", [GH, U * P])
            mx_gate = scratch("mx_gate", [R, U * P])
            mx_sum = scratch("mx_sum", [R, U * P])
            mx_gu = scratch("mx_gu", [R, U * P])
            mx_glob = scratch("mx_glob", [R, U * P])
        with Scratch() as scratch:
            me_xh = scratch("me_xh", [P, KC, NT * P], F32R)
            me_xl = scratch("me_xl", [P, KC, NT * P], F32R)
            me_wh = scratch("me_wh", [P, 2, 1024], F32R)
            me_wl = scratch("me_wl", [P, 2, 1024], F32R)
            me_h = scratch("me_h", [P, HM, 512])
            me_hh = scratch("me_hh", [P, HM, 512], F32R)
            me_hl = scratch("me_hl", [P, HM, 512], F32R)
            me_rwh = scratch("me_rwh", [P, KC, E], F32R)
            me_rwl = scratch("me_rwl", [P, KC, E], F32R)
            me_pr = scratch("me_pr", [P, NT, E])
            me_st = scratch("me_st", [P, NT])
            me_cmp = scratch("me_cmp", [P, NT, E, E])
            me_cmp2 = scratch("me_cmp2", [P, NT, E, E])
            me_rank = scratch("me_rank", [P, NT, E])
            me_gate = scratch("me_gate", [P, NT, EX])
            me_gT = scratch("me_gT", [EX, U, P])

        block = ctx.enter_context(nc.Block())

        @block.sync
        def _(sp):
            for dst, src in ((ident, "ident"), (eps, "eps"), (head_scale, "head_scale"), (rope_cos, "rope_cos"),
                             (rope_sin, "rope_sin"), (causal, "causal"), (hide, "hide"),
                             (row_pick, "row_pick")):
                sp.dma_start(dst[:], a[src]).then_inc(consts_loaded, 16)
            sp.dma_start(x[:], x_tiles).then_inc(x_loaded, 16)
            for c in smalls:
                for w, dst in (("w_qkv", c.w_qkv), ("w_o", c.w_o), ("b_qk", c.b_qk), ("b_v", c.b_v), ("b_o", c.b_o)):
                    sp.dma_start(dst[:], a[f"{c.name}_{w}"]).then_inc(c.weights_loaded, 16)
                if c.cross:
                    with sp.Fori(0, NT // U) as i:
                        hold(sp, sm["norm_ready"], U * i + 1)
                        sp.dma_start(sm_cT[:], a["ctx32"][i]).then_inc(c.ctx_loaded, 16)
            sp.dma_start(f8_bits[:], a["ffn0_w"]).then_inc(f8["weights_loaded"], 16)
            sp.dma_start(f8_ws[:], a["ffn0_ws"]).then_inc(f8["weights_loaded"], 16)
            sp.dma_start(f8_bias[:], a["ffn0_bias"]).then_inc(f8["weights_loaded"], 16)
            for dst, src in ((x1_wq, "wq"), (x1_wk, "wk"), (x1_wv, "wv"), (x1_wo, "wo"), (x1_bq, "bq"), (x1_bk, "bk"),
                             (x1_bv, "bv"), (x1_bo, "bo")):
                sp.dma_start(dst[:], a[f"xattn1_{src}"]).then_inc(x1["weights_loaded"], 16)
            for dst, src in ((mx_w1, "w1"), (mx_b1, "b1"), (mx_w2, "w2"), (mx_b2, "b2"), (mx_wu, "wu"), (mx_wv, "wv"),
                             (mx_conv, "conv"), (mx_wo, "wo"), (mx_bo, "bo"), (mx_keep, "keep")):
                sp.dma_start(dst[:], a[f"mix1_{src}"]).then_inc(mx["weights_loaded"], 16)
            for dst, src in ((me_b1, "b1"), (me_b2, "b2"), (me_rw, "rw"), (me_rb, "rb"), (me_before, "before")):
                sp.dma_start(dst[:], a[f"moe1_{src}"]).then_inc(me["weights_loaded"], 16)
            with sp.Fori(0, NT // 2) as i:
                for par in range(2):
                    hold(sp, x1["last_done"], 1 + 2 * i)
                    sp.dma_start(x1_ctx[par][:], a["ctx"][2 * i + par]).then_inc(x1[f"ctx{par}"], 16)
                    hold(sp, x1["mask_ready"], 1 + 2 * i + par)
                    sp.dma_start(x1_mask8[:], a["mask"][2 * i + par]).then_inc(x1["mask_loaded"], 16)
            with sp.Fori(0, EX) as e:
                hold(sp, me["w2_split"], 1 + e)
                sp.dma_start(me_raw[:], a["moe1_w"][e]).then_inc(me["raw_loaded"], 16)
            sp.wait_ge(me["acc_ready"], TG * NG * EX)
            sp.dma_start(out_tiles, x[:]).then_inc(me["stored"], 16)
            sp.wait_ge(me["stored"], 16)

        @block.tensor
        def _(pe):
            for s in (x1["xT_done"], x1["scores_done"], x1["last_done"], me["up_done"], me["down_done"]):
                pe.sem_inc(s, 1)
            pe.wait_ge(consts_loaded, 16 * 8)
            pe.wait_ge(consts_cast, 3)
            small_tensor(pe, small["xattn0"])
            small_tensor(pe, small["attn0"])
            ffn_tensor(pe)
            x1q_tensor(pe)
            x1_tensor(pe)
            mix_tensor(pe)
            moe_prep_tensor(pe)
            moe_tensor(pe)

        @block.scalar
        def _(act):
            act.wait_ge(consts_loaded, 16 * 8)
            small_scalar(act, small["xattn0"])
            small_scalar(act, small["attn0"])
            ffn_scalar(act)
            x1q_scalar(act)
            x1_scalar(act)
            mix_scalar(act)
            moe_prep_scalar(act)
            moe_scalar(act)

        @block.vector
        def _(dve):
            for s in (x_stats, sm["stats_ready"], f8["stats_ready"], x1["stats_ready"], mx["stats_ready"], me["w2_split"]):
                dve.sem_inc(s, 1)
            dve.wait_ge(consts_loaded, 16 * 8)
            dve.wait_ge(x_loaded, 16)
            with dve.Fori(0, NT // U) as i:
                hold(dve, x_stats, 1 + (2 * U + 1) * i)
                for u in range(U):
                    nc.vector.bn_stats(bn_out[:, u, :], x[:, U * i + u, :]).then_inc(x_stats, 1)
                hold(dve, x_stats, 1 + (2 * U + 1) * i + U)
                for u in range(U):
                    nc.vector.bn_aggr(bn_mv[:, u, :], bn_out[:, u, :]).then_inc(x_stats, 1)
                hold(dve, x_stats, 1 + (2 * U + 1) * i + 2 * U)
                nc.vector.tensor_copy(ln_mv[:, bass.ds(U * i, U), :], bn_mv[:]).then_inc(x_stats, 1)
            dve.wait_ge(x_stats, 1 + (2 * U + 1) * (NT // U))
            dve.sem_inc(var_ready, 1)
            small_vector(dve, small["xattn0"])
            dve.sem_inc(var_ready, 1)
            small_vector(dve, small["attn0"])
            dve.sem_inc(var_ready, 1)
            ffn_weights(dve)
            ffn_vector(dve)
            dve.sem_inc(var_ready, 1)
            x1q_vector(dve)
            x1_vector(dve)
            dve.sem_inc(var_ready, 1)
            mix_vector(dve)
            dve.sem_inc(var_ready, 1)
            moe_prep_vector(dve)
            moe_vector(dve)

        @block.gpsimd
        def _(pool):
            pool.sem_inc(x1["mask_ready"], 1)
            nc.gpsimd.memset(sm_vbd[:], 0.0).then_inc(sm_zeroed, 1)
            pool.wait_ge(consts_loaded, 16 * 8)
            nc.gpsimd.tensor_copy(ident_b[:], ident[:]).then_inc(consts_cast, 1)
            nc.gpsimd.tensor_copy(causal_b[:], causal[:]).then_inc(consts_cast, 1)
            nc.gpsimd.tensor_copy(hide_b[:], hide[:]).then_inc(consts_cast, 1)
            for c in smalls:
                pool_bias(pool, sm["norm_ready"], sm["x_biased"], c.bias_ready, c.b_o[:], c.before)
            pool_bias(pool, f8["norm_ready"], f8["x_biased"], f8["w_ready"], f8_bias[:])
            pool_bias(pool, x1["norm_ready"], x1["x_biased"], x1["bias_ready"], x1_bo[:])
            x1_pool(pool)
            pool_bias(pool, mx["norm_ready"], mx["x_biased"], mx["taps_ready"], mx_bo[:])


def layout(inputs):
    f = {k: np.asarray(v) for k, v in inputs.items()}
    out = {}
    rows = lambda w: np.ascontiguousarray(w.reshape(KC, P, -1).transpose(1, 0, 2))
    wide = lambda v: np.ascontiguousarray(np.broadcast_to(v.reshape(1, -1), (P, v.size)))
    heads = lambda w, order=range(G): np.ascontiguousarray(
        w.reshape(G, 2, 2, DH, -1)[list(order)].transpose(2, 0, 3, 1, 4).reshape(P, KC, -1))
    parity = [g for r in range(2) for g in range(r, G, 2)]
    half = np.array([h * DH + d for h in range(H) for d in list(range(0, DH, 2)) + list(range(1, DH, 2))])

    out["x"] = f["x"].reshape(B * S, D)
    ctx = f["ctx_1024"].reshape(NT, BT, SK, KC, P).transpose(0, 4, 3, 1, 2)
    last = np.repeat(ctx[..., SK - 1], G, axis=-1)
    out["ctx"] = np.concatenate([ctx.reshape(NT, P, KC, BT * SK), last], axis=-1)
    out["ctx32"] = np.ascontiguousarray(
        ctx[..., :S].reshape(NT // U, U, P, KC, BT * S).transpose(0, 2, 1, 3, 4))
    out["mask"] = np.ascontiguousarray(f["mask_Bx1xSxS2_bf0"].reshape(NT, BT, S, SK).transpose(0, 2, 1, 3))

    for name, q, k, v, o, perm in (
            ("xattn0", "L0_xattn_q", "L0_xattn_k", "L0_xattn_v", "L0_xattn_o", slice(None)),
            ("attn0", "q", "k", "v", "o", half)):
        if name == "xattn0":
            w = [f[f"{n}_w"].T for n in (q, k, v, o)]
            b = [f[f"{n}_b"] for n in (q, k, v, o)]
        else:
            w = [f[f"L0_attn_W{n}"] for n in (q, k, v, o)]
            b = [f[f"L0_attn_b{n}"] for n in (q, k, v, o)]
        out[f"{name}_w_qkv"] = rows(np.concatenate([w[0][:, perm], w[1][:, perm], w[2]], axis=1))
        out[f"{name}_w_o"] = heads(w[3], parity)
        out[f"{name}_b_qk"] = wide(np.concatenate([b[0][perm], b[1][perm]]))
        out[f"{name}_b_v"] = np.ascontiguousarray(np.broadcast_to(heads(b[2], parity), (P, KC, P)))
        out[f"{name}_b_o"] = wide(b[3])

    out["ffn0_w"] = rows(f["L0_ffn_weight"].view(np.uint8).T).reshape(P, KC * D)
    out["ffn0_ws"] = np.ascontiguousarray(np.broadcast_to(f["L0_ffn_weight_scale"].reshape(1, 1), (P, 1)))
    out["ffn0_bias"] = wide(f["L0_ffn_bias"])

    for n in "qkv":
        out[f"xattn1_w{n}"] = rows(f[f"L1_xattn_w_{n}"].T)
    out["xattn1_wo"] = heads(f["L1_xattn_w_o"].T)
    out["xattn1_bq"] = np.ascontiguousarray(f["L1_xattn_b_q"].reshape(KC, P).T)
    out["xattn1_bk"] = np.ascontiguousarray(f["L1_xattn_b_k"].reshape(KC, P).T)
    out["xattn1_bv"] = np.ascontiguousarray(np.broadcast_to(heads(f["L1_xattn_b_v"]), (P, KC, P)))
    out["xattn1_bo"] = wide(f["L1_xattn_b_o"])

    out["mix1_w1"] = rows(f["L1_attn_gate_w1"])
    out["mix1_b1"] = f["L1_attn_gate_b1"].reshape(GH, 1)
    out["mix1_w2"] = f["L1_attn_gate_w2"]
    out["mix1_b2"] = f["L1_attn_gate_b2"].reshape(R, 1)
    out["mix1_wu"] = rows(f["L1_attn_U_w"])
    out["mix1_wv"] = rows(f["L1_attn_V_w"])
    out["mix1_conv"] = rows(f["L1_attn_conv_w"])
    out["mix1_wo"] = f["L1_attn_out_w"]
    out["mix1_bo"] = wide(f["L1_attn_out_b"])

    w1 = np.concatenate([f["L1_ffn_rw1"], f["L1_ffn_sw1"][None]])
    w2 = np.concatenate([f["L1_ffn_rw2"], f["L1_ffn_sw2"][None]])
    w1 = w1.reshape(EX, KC, P, HID).transpose(0, 2, 1, 3).reshape(EX, P, 1, KC * HID)
    w2 = w2.reshape(EX, HM, P, D).transpose(0, 2, 1, 3).reshape(EX, P, 1, HM * D)
    out["moe1_w"] = np.ascontiguousarray(np.concatenate([w1, w2], axis=2))
    b1 = np.concatenate([f["L1_ffn_rb1"], f["L1_ffn_sb1"][None]])
    out["moe1_b1"] = np.ascontiguousarray(b1.reshape(EX, HM, P).transpose(2, 0, 1))
    out["moe1_b2"] = np.concatenate([f["L1_ffn_rb2"], f["L1_ffn_sb2"][None]])
    out["moe1_rw"] = rows(f["L1_ffn_router_w"])
    out["moe1_rb"] = wide(f["L1_ffn_router_b"])

    p = np.arange(P)
    out["ident"] = np.eye(P, dtype=np.float32)
    out["eps"] = np.full((P, 1), EPS, np.float32)
    out["head_scale"] = (((p[:, None] // DH) % L == np.arange(L)[None]) * DH ** -0.5).astype(np.float32)
    freqs = 1.0 / 10000.0 ** (np.arange(DH // 2) / (DH // 2))
    ang = (p % S)[:, None] * freqs[None]
    out["rope_cos"] = np.concatenate([np.cos(ang), np.cos(ang)], 1).astype(np.float32)
    out["rope_sin"] = np.concatenate([-np.sin(ang), np.sin(ang)], 1).astype(np.float32)
    out["causal"] = np.where(np.arange(S)[None] > (p % S)[:, None], CAUSAL, 0.0).astype(np.float32)
    q = np.arange(S)
    out["hide"] = np.where(q[:, None, None] == q[None, None, :], MASKED, 0.0).repeat(L, 1).astype(np.float32)
    out["row_pick"] = np.eye(BT * G, dtype=np.float32)
    out["mix1_keep"] = np.ascontiguousarray(np.broadcast_to((np.arange(U * P) % S != 0).astype(np.float32), (R, U * P)))
    e = np.arange(E)
    out["moe1_before"] = np.ascontiguousarray(np.broadcast_to((e[None] < e[:, None]).astype(np.float32), (P, E, E)))
    return {k: np.ascontiguousarray(v) for k, v in out.items()}


def kernel(**inputs):
    import concourse.bacc as bacc
    from concourse.bass_utils import run_bass_kernel_spmd

    arrays = layout(inputs)
    nc = bacc.Bacc("TRN2", target_bir_lowering=False, num_devices=1)
    args = {}
    for name, v in arrays.items():
        args[name] = nc.dram_tensor(f"in_{name}", v.shape, mybir.dt.from_np(v.dtype), kind="ExternalInput").ap()
    args["out"] = nc.dram_tensor("out_x", (B * S, D), F32, kind="ExternalOutput").ap()
    build(nc, args)
    r = run_bass_kernel_spmd(nc, [{f"in_{k}": v for k, v in arrays.items()}], core_ids=[0])
    return r.results[0]["out_x"].reshape(B, S, D)
```

```python
from contextlib import ExitStack

import numpy as np

import concourse.bass as bass
from concourse import mybir

F32 = mybir.dt.float32
F32R = mybir.dt.float32r
BF16 = mybir.dt.bfloat16
I32 = mybir.dt.int32
U8 = mybir.dt.uint8
FP8 = mybir.dt.float8e4
ALU = mybir.AluOpType
ACT = mybir.ActivationFunctionType
AX = mybir.AxisListType

B, S, D = 64, 32, 256
SK = 257
SP = SK + SK % 2
P = 128
NT = B * S // P
BT = P // S
H, DH = 16, 16
G = H // BT
L = BT
KC = D // P
U = 4
R, GH = 32, 64
E, HID = 8, 512
EX = E + 1
HM = HID // P
TG = 4
EPS = 1e-5
MASKED = -1e30
CAUSAL = -1e9


def build(nc, a):
    with ExitStack() as ctx:

        def sb(name, shape, dt=F32):
            return ctx.enter_context(nc.sbuf_tensor(name, shape, dt))

        def sem(name):
            return ctx.enter_context(nc.semaphore(name))

        class Scratch(ExitStack):
            def __call__(self, name, shape, dt=F32):
                return self.enter_context(nc.sbuf_tensor(name, shape, dt))

        psum = ctx.enter_context(nc.psum_tensor("psum", [P, 8, 512], F32))

        x = sb("x", [P, NT, D])
        ln_mv = sb("ln_mv", [P, NT, 2])
        ln_rstd = sb("ln_rstd", [P, NT])
        ln_tmp = sb("ln_tmp", [P, 2, NT])
        ident = sb("ident", [P, P])
        eps = sb("eps", [P, 1])
        head_scale = sb("head_scale", [P, L])
        bn_out = sb("bn_out", [P, NT, 6])

        x_loaded = sem("x_loaded")
        consts_loaded = sem("consts_loaded")
        consts_cast = sem("consts_cast")
        x_tiles = a["x"].rearrange("(t p) c -> p t c", p=P)
        out_tiles = a["out"].rearrange("(t p) c -> p t c", p=P)
        x_stats = sem("x_stats")
        chain = sem("chain")
        chained = [0]

        passed = {}

        def hold(eng, semaphore, count):
            if eng not in passed:
                passed[eng] = sem(f"passed_{len(passed)}")
            eng.wait_ge(semaphore, count)
            eng.sem_inc(passed[eng], 1)

        def link(dve, ins, n=1):
            ins.then_inc(chain, 1)
            chained[0] += 1
            dve.wait_ge(chain, chained[0])

        layers = ["xattn0", "attn0", "ffn0", "xattn1", "mix1", "moe1"]
        var_ready, sqrt_ready, rstd_ready = sem("var_ready"), sem("sqrt_ready"), sem("rstd_ready")

        def dve_variance(dve):
            mean, var, tmp = ln_mv[:, :, 0], ln_mv[:, :, 1], ln_tmp[:, 0, :]
            link(dve, nc.vector.tensor_tensor(tmp, bn_out[:, :, 1], bn_out[:, :, 4], ALU.subtract))
            link(dve, nc.vector.tensor_tensor(mean, bn_out[:, :, 1], bn_out[:, :, 4], ALU.add))
            link(dve, nc.vector.tensor_scalar(mean, mean, 0.5, None, ALU.mult))
            link(dve, nc.vector.scalar_tensor_tensor(out=tmp, in0=tmp, scalar=0.25, in1=tmp, op0=ALU.mult, op1=ALU.mult))
            link(dve, nc.vector.tensor_tensor(var, bn_out[:, :, 2], bn_out[:, :, 5], ALU.add))
            nc.vector.scalar_tensor_tensor(out=var, in0=var, scalar=1.0 / D, in1=tmp, op0=ALU.mult,
                                           op1=ALU.add).then_inc(var_ready, 1)

        def act_sqrt(act, n):
            act.wait_ge(var_ready, layers.index(n) + 1)
            nc.scalar.activation(ln_tmp[:, 0, :], ln_mv[:, :, 1], ACT.Sqrt, bias=eps[:, 0:1]).then_inc(sqrt_ready, 1)

        def dve_rstd(dve, n):
            dve.wait_ge(sqrt_ready, layers.index(n) + 1)
            r, s = ln_rstd[:, :], ln_tmp[:, 1, :]
            link(dve, nc.vector.reciprocal(r, ln_tmp[:, 0, :]))
            link(dve, nc.vector.scalar_tensor_tensor(out=s, in0=ln_mv[:, :, 1], scalar=eps[:, 0:1], in1=r,
                                                     op0=ALU.add, op1=ALU.mult))
            link(dve, nc.vector.tensor_tensor(s, s, r, ALU.mult))
            link(dve, nc.vector.tensor_scalar(s, s, -0.5, 1.5, ALU.mult, ALU.add))
            ins = nc.vector.tensor_tensor(r, r, s, ALU.mult)
            ins.then_inc(rstd_ready, 1)
            dve.wait_ge(rstd_ready, layers.index(n) + 1)

        def dve_normalise(t, out):
            return nc.vector.tensor_scalar(out, x[:, t, :], ln_mv[:, t, 0:1], ln_rstd[:, bass.ds(t, 1)],
                                           ALU.subtract, ALU.mult)

        class Small:

            def __init__(self, name, cross):
                self.name, self.cross = name, cross

        sm_xn = sb("sm_xn", [P, U, D])
        rope_cos = sb("rope_cos", [P, DH])
        rope_sin = sb("rope_sin", [P, DH])
        ident_b = sb("ident_b", [P, P], BF16)
        causal = sb("causal", [P, S])
        causal_b = sb("causal_b", [P, S], BF16)

        sm = {s: sem(f"small_{s}") for s in (
            "norm_ready", "xT_done", "xT_ready", "biased", "qk_done", "v_done", "v_ready", "rope_parts", "rope_ready", "qkT_done",
            "qbd_ready", "kT_ready", "scores_done", "max_ready", "shifted", "exp_ready", "sum_ready", "rinv_ready", "pT_done",
            "pT_ready", "pv_done", "heads_ready", "oT_done", "oT_ready", "out_done", "x_biased", "x_updated", "stats_ready")}
        smalls = []
        for name, cross in (("xattn0", True), ("attn0", False)):
            c = Small(name, cross)
            c.before = len(smalls) * NT
            c.weights_loaded, c.bias_product = sem(f"{name}_weights_loaded"), sem(f"{name}_bias_product")
            c.bias_ready = sem(f"{name}_bias_ready")
            c.ctx_loaded = [sem(f"{name}_ctx_loaded{u}") for u in range(U if cross else 0)]
            smalls.append(c)
        small = {c.name: c for c in smalls}
        sm_zeroed = sem("small_zeroed")

        def bank(u, k):
            return psum[:, 2 * u + k, :]

        def steps(eng, step):
            for s in range(U):
                step(lambda d: (s - d, (s - d) % U), lambda d: s - d >= 0)
            with eng.Fori(1, NT // U) as i:
                for u in range(U):
                    step(lambda d: (U * i + u - d, (u - d) % U), lambda d: True)
            for s in range(NT, NT + U):
                step(lambda d: (s - d, (s - d) % U), lambda d: s - d < NT)

        def small_tensor(pe, c):
            pe.wait_ge(c.weights_loaded, 16 * 5)
            for k in range(KC):
                mm = nc.tensor.matmul(bank(0, 0)[:, 0:D], c.b_v[:, k, :], c.w_o[:, k, :], start=(k == 0), stop=(k == KC - 1))
            mm.then_inc(c.bias_product, 1)
            pe.wait_ge(c.bias_ready, 1)
            first = c.before
            kv = sm_cT if c.cross else sm_xT

            def scores(u, r):
                nc.tensor.matmul(bank(u, r)[:, 0:D], ident_b[:], causal_b[:].unsqueeze(1).broadcast_to([P, D // S, S]),
                                 start=True, stop=False, skip_group_check=True)
                for k in range(KC):
                    for b in range(BT):
                        j = k * BT + b
                        mm = nc.tensor.matmul(bank(u, r)[:, j * S:(j + 1) * S], sm_qbd[64 * r:64 * r + 64, u, k, b, :],
                                              sm_kT[64 * r:64 * r + 64, u, k, b * S:(b + 1) * S],
                                              start=False, stop=(j == KC * BT - 1), skip_group_check=True)
                return mm

            def step(n, live):
                if live(4):
                    t, u = n(4)
                    pe.wait_ge(sm["heads_ready"], first + t + 1)
                    for k in range(BT // 2):
                        mm = nc.tensor.transpose(bank(u, 0)[:, k * P:(k + 1) * P],
                                                 sm_o[:, u, k * 2 * G:(k + 1) * 2 * G, :].rearrange("p j d -> p (j d)"), ident[:])
                    mm.then_inc(sm["oT_done"], 1)
                if live(2):
                    t, u = n(2)
                    pe.wait_ge(sm["rope_ready"], first + t + 1)
                    pe.wait_ge(sm["v_ready"], first + t + 1)
                    for s in range(2):
                        for k in range(KC):
                            mm = nc.tensor.transpose(bank(u, 1 - s)[:, k * P:(k + 1) * P],
                                                     sm_qk[:, u, s, k * P:(k + 1) * P], ident[:])
                    mm.then_inc(sm["qkT_done"], 1)
                if live(1):
                    t, u = n(1)
                    pe.wait_ge(sm["xT_ready"], first + t + 1)
                    if not (isinstance(t, int) and t < U):
                        pe.wait_ge(sm["x_updated"], first + t - U + 1)
                    if c.cross:
                        pe.wait_ge(c.ctx_loaded[u], 16 // U * (t - u) + 16)
                    for s in range(2):
                        for k in range(KC):
                            mm = nc.tensor.matmul(bank(u, 1)[:, s * D:(s + 1) * D], (kv if s else sm_xT)[:, u, k, :],
                                                  c.w_qkv[:, k, s * D:(s + 1) * D],
                                                  start=(k == 0), stop=(k == KC - 1), skip_group_check=True)
                    mm.then_inc(sm["qk_done"], 1)
                if live(1):
                    t, u = n(1)
                    for k in range(KC):
                        mm = nc.tensor.matmul(bank(u, 0)[:, 0:D], kv[:, u, k, :], c.w_qkv[:, k, 2 * D:3 * D],
                                              start=(k == 0), stop=(k == KC - 1))
                    mm.then_inc(sm["v_done"], 1)
                if live(3):
                    t, u = n(3)
                    pe.wait_ge(sm["exp_ready"], first + t + 1)
                    for g in range(G):
                        v = sm_p[:, u, g * BT:(g + 1) * BT, :].rearrange("p b s -> p (b s)")
                        mm = nc.tensor.transpose(bank(u, 1)[:, g * P:(g + 1) * P], v, ident[:])
                    mm.then_inc(sm["pT_done"], 1)
                if live(2):
                    t, u = n(2)
                    pe.wait_ge(sm["kT_ready"], first + t + 1)
                    pe.wait_ge(sm["qbd_ready"], first + t + 1)
                    scores(u, 0)
                if live(4):
                    t, u = n(4)
                    pe.wait_ge(sm["oT_ready"], first + t + 1)
                    for k in range(KC):
                        mm = nc.tensor.matmul(bank(u, 1)[:, 0:D], sm_oT[:, u, k, :, :].rearrange("p b s -> p (b s)"), c.w_o[:, k, :],
                                              start=(k == 0), stop=(k == KC - 1))
                    mm.then_inc(sm["out_done"], 1)
                if live(3):
                    t, u = n(3)
                    pe.wait_ge(sm["pT_ready"], first + t + 1)
                    for gp in range(G):
                        g = gp // 2 + 2 * (gp % 2)
                        mm = nc.tensor.matmul(bank(u, gp // 2)[:, (gp % 2) * D:(gp % 2 + 1) * D], sm_pT[:, u, gp, :],
                                              sm_vbd[:, u, g, :, :], start=True, stop=True, skip_group_check=True)
                    mm.then_inc(sm["pv_done"], 1)
                if live(0):
                    t, u = n(0)
                    pe.wait_ge(sm["norm_ready"], first + t + 1)
                    for k in range(KC):
                        mm = nc.tensor.transpose(bank(u, 0)[:, k * P:(k + 1) * P], sm_xn[:, u, k * P:(k + 1) * P], ident[:])
                    mm.then_inc(sm["xT_done"], 1)
                if live(2):
                    t, u = n(2)
                    mm = scores(u, 1)
                    mm.then_inc(sm["scores_done"], 1)

            steps(pe, step)

        def small_scalar(act, c):
            act.wait_ge(sm_zeroed, 1)
            act_sqrt(act, c.name)
            nc.scalar.preload_act_table(ACT.Exp)
            first = c.before

            def step(n, live):
                if live(4):
                    t, u = n(4)
                    act.wait_ge(sm["oT_done"], first + t + 1)
                    spread_heads(nc.scalar.copy, bank(u, 0), sm_oT[:, u, :, :, :]).then_inc(sm["oT_ready"], 1)
                if live(2):
                    t, u = n(2)
                    act.wait_ge(sm["qkT_done"], first + t + 1)
                    nc.scalar.activation(sm_kT[:, u, :, :].rearrange("p k s -> p (k s)"), bank(u, 0)[:, 0:D],
                                         ACT.Copy).then_inc(sm["kT_ready"], 1)
                if live(3):
                    t, u = n(3)
                    act.wait_ge(sm["pT_done"], first + t + 1)
                    nc.scalar.activation(sm_pT[:, u, :, :].rearrange("p g s -> p (g s)"), bank(u, 1), ACT.Copy).then_inc(sm["pT_ready"], 1)
                if live(1):
                    t, u = n(1)
                    act.wait_ge(sm["v_done"], first + t + 1)
                    for b in range(BT):
                        rows = slice(b * S, (b + 1) * S)
                        ins = nc.scalar.copy(sm_vbd[rows, u, :, b, :], bank(u, 0)[rows, 0:D].rearrange("p (g c) -> p g c", g=G))
                    ins.then_inc(sm["v_ready"], 1)
                if live(0):
                    t, u = n(0)
                    act.wait_ge(sm["xT_done"], first + t + 1)
                    nc.scalar.activation(sm_xT[:, u, :, :].rearrange("p k s -> p (k s)"), bank(u, 0)[:, 0:D],
                                         ACT.Copy).then_inc(sm["xT_ready"], 1)
                if live(2):
                    t, u = n(2)
                    act.wait_ge(sm["shifted"], first + t + 1)
                    v = sm_p[:, u, :, :].rearrange("p j s -> p (j s)")
                    nc.scalar.activation(v, v, ACT.Exp).then_inc(sm["exp_ready"], 1)

            steps(act, step)

        def spread_heads(copy, src, dst):
            for r in range(2):
                for rb in range(2):
                    v = src[64 * rb:64 * rb + 64, 0:D].rearrange("p (bb j r q) -> p r bb j q", bb=BT // 2, j=L // 2, r=2)[:, r]
                    w = dst[64 * r:64 * r + 64].rearrange("p j (bb rb) q -> p rb bb j q", rb=2)[:, rb]
                    ins = copy(w, v)
            return ins

        def small_vector(dve, c):
            dve_rstd(dve, c.name)
            dve.wait_ge(c.weights_loaded, 16 * 5)
            dve.wait_ge(c.bias_product, 1)
            nc.vector.tensor_tensor(c.b_o[:], bank(0, 0)[:, 0:D], c.b_o[:], ALU.add).then_inc(c.bias_ready, 1)
            first = c.before

            def step(n, live):
                if live(0):
                    t, u = n(0)
                    dve_normalise(t, sm_xn[:, u, :]).then_inc(sm["norm_ready"], 1)
                if live(2):
                    t, u = n(2)
                    dve.wait_ge(sm["qkT_done"], first + t + 1)
                    for k in range(KC):
                        ins = spread_queries(nc.vector, sm_qbd[:, u, k, :, :], bank(u, 1)[:, k * P:(k + 1) * P])
                    ins.then_inc(sm["qbd_ready"], 1)
                if live(3):
                    t, u = n(3)
                    dve.wait_ge(sm["exp_ready"], first + t + 1)
                    nc.vector.tensor_reduce(sm_sum[:, u, :], sm_p[:, u, :, :], AX.X, ALU.add).then_inc(sm["sum_ready"], 1)
                    dve.wait_ge(sm["sum_ready"], first + t + 1)
                    nc.vector.reciprocal(sm_rinv[:, u, :], sm_sum[:, u, :]).then_inc(sm["rinv_ready"], 1)
                if live(1):
                    t, u = n(1)
                    dve.wait_ge(sm["qk_done"], first + t + 1)
                    qk = sm_qk[:, u, :, :].rearrange("p s c -> p (s c)")
                    nc.vector.tensor_tensor(qk, bank(u, 1), c.b_qk[:], ALU.add).then_inc(sm["biased"], 1)
                    dve.wait_ge(sm["biased"], first + t + 1)
                    qk3 = sm_qk[:, u, :, :].rearrange("p s (h d) -> p (s h) d", d=DH)
                    cs3 = sm_cosd[:].rearrange("p s (h d) -> p (s h) d", d=DH)
                    sn3 = sm_sind[:].rearrange("p s (h d) -> p (s h) d", d=DH)
                    wide = [P, 2 * H, DH]
                    half = [P, 2 * H, DH // 2]
                    nc.vector.tensor_tensor(cs3, qk3, rope_cos[:].unsqueeze(1).broadcast_to(wide), ALU.mult).then_inc(sm["rope_parts"], 1)
                    nc.vector.tensor_tensor(sn3[:, :, 0:8], qk3[:, :, 8:16],
                                            rope_sin[:, 0:8].unsqueeze(1).broadcast_to(half), ALU.mult).then_inc(sm["rope_parts"], 1)
                    nc.vector.tensor_tensor(sn3[:, :, 8:16], qk3[:, :, 0:8],
                                            rope_sin[:, 8:16].unsqueeze(1).broadcast_to(half), ALU.mult).then_inc(sm["rope_parts"], 1)
                    dve.wait_ge(sm["rope_parts"], 3 * (first + t + 1))
                    nc.vector.tensor_tensor(qk, cs3, sn3, ALU.add).then_inc(sm["rope_ready"], 1)
                if live(4):
                    t, u = n(4)
                    dve.wait_ge(sm["out_done"], first + t + 1)
                    dve.wait_ge(sm["x_biased"], first + t + 1)
                    nc.vector.tensor_tensor(x[:, t, :], bank(u, 1)[:, 0:D], x[:, t, :], ALU.add).then_inc(sm["x_updated"], 1)
                if live(4):
                    t, u = n(4)
                    row_stats(dve, t, sm["x_updated"], first + t + 1, sm["stats_ready"])
                if live(3):
                    t, u = n(3)
                    dve.wait_ge(sm["rinv_ready"], first + t + 1)
                    dve.wait_ge(sm["pv_done"], first + t + 1)
                    pick_heads(psum[:, 2 * u:2 * u + 2, :], sm_rinv[:, u, :],
                               sm_o[:, u, :, :].rearrange("p (b g) d -> p g b d", b=BT)).then_inc(sm["heads_ready"], 1)
                if live(2):
                    t, u = n(2)
                    dve.wait_ge(sm["scores_done"], first + t + 1)
                    sc = psum[:, 2 * u:2 * u + 2, 0:D].rearrange("p r (j s) -> p r j s", s=S)
                    top = sm_max[:, u, :].rearrange("p (r j) -> p r j", r=2)
                    nc.vector.tensor_reduce(top, sc, AX.X, ALU.max).then_inc(sm["max_ready"], 1)
                    dve.wait_ge(sm["max_ready"], first + t + 1)
                    nc.vector.tensor_tensor(sm_p[:, u, :, :].rearrange("p (r j) s -> p r j s", r=2), sc,
                                            top.unsqueeze(3).broadcast_to([P, 2, BT * G // 2, S]),
                                            ALU.subtract).then_inc(sm["shifted"], 1)

            steps(dve, step)
            dve.wait_ge(sm["stats_ready"], 1 + first + NT)

        def spread_queries(eng, dst, src):
            return eng.tensor_tensor(
                dst.rearrange("p b (l q) -> p b l q", l=L),
                src.rearrange("p (b q) -> p b q", b=BT).unsqueeze(2).broadcast_to([P, BT, L, S]),
                head_scale[:].unsqueeze(1).unsqueeze(3).broadcast_to([P, BT, L, S]), ALU.mult)

        def pick_heads(src, rinv, dst):
            for l in range(L):
                q = slice(S * l, S * l + S)
                v = src[q].rearrange("p k (j l d) -> p l (k j) d", l=L, d=DH)[:, l]
                r = rinv[q].unsqueeze(2).broadcast_to([S, rinv.shape[1], DH])
                o = dst[q]
                if len(o.shape) == 4:
                    v, r = (z.rearrange("p (g b) d -> p g b d", g=G) for z in (v, r))
                ins = nc.vector.tensor_tensor(o, v, r, ALU.mult)
            return ins

        def row_stats(dve, t, updated, count, stats):
            hold(dve, updated, count)
            nc.vector.bn_stats(bn_out[:, t, :], x[:, t, :]).then_inc(stats, 1)

        def pool_bias(pool, norm_ready, x_biased, bias_ready, b_o, before=0):
            pool.wait_ge(bias_ready, 1)
            with pool.Fori(0, NT) as t:
                pool.wait_ge(norm_ready, before + t + 1)
                nc.gpsimd.tensor_tensor(x[:, t, :], x[:, t, :], b_o, ALU.add).then_inc(x_biased, 1)

        f8_bias = sb("f8_bias", [P, D])
        f8_ws = sb("f8_ws", [P, 1])
        f8_bits = sb("f8_bits", [P, KC * D], U8)
        f8_w = sb("f8_w", [P, KC, D], BF16)
        f8 = {s: sem(f"ffn0_{s}") for s in (
            "weights_loaded", "w_ready", "norm_ready", "amax_ready", "scale_ready", "inv_ready", "scaled", "exponent_ready",
            "magic_ready", "added", "q_ready", "total_ready", "qT_done", "qT_ready", "out_done", "x_biased", "x_updated",
            "stats_ready")}

        def ffn_weights(dve):
            dve.wait_ge(f8["weights_loaded"], 16 * 3)
            link(dve, nc.vector.tensor_copy(f8_int[:], f8_bits[:]))
            link(dve, nc.vector.tensor_scalar(f8_mag[:], f8_int[:], 127, None, ALU.bitwise_and))
            link(dve, nc.vector.tensor_scalar(f8_high[:], f8_mag[:], 120.0, None, ALU.is_ge))
            link(dve, nc.vector.scalar_tensor_tensor(out=f8_byte[:], in0=f8_high[:], scalar=-8.0, in1=f8_int[:],
                                                     op0=ALU.mult, op1=ALU.add))
            nc.vector.scalar_tensor_tensor(out=f8_w[:].rearrange("p k n -> p (k n)"), in0=f8_high[:], scalar=1.0,
                                           in1=f8_byte[:].bitcast(FP8), op0=ALU.add, op1=ALU.mult).then_inc(f8["w_ready"], 1)

        def ffn_vector(dve):
            dve_rstd(dve, "ffn0")
            with dve.Fori(0, NT // U) as i:
                n = lambda u: U * i + u + 1
                hold(dve, f8["stats_ready"], 1 + U * i)
                for u in range(U):
                    dve_normalise(U * i + u, f8_xn[:, u, :]).then_inc(f8["norm_ready"], 1)
                for u in range(U):
                    dve.wait_ge(f8["norm_ready"], n(u))
                    nc.vector.tensor_reduce(f8_amax[:, u:u + 1], f8_xn[:, u, :], AX.X, ALU.max,
                                            apply_absolute_value=True).then_inc(f8["amax_ready"], 1)
                dve.wait_ge(f8["amax_ready"], n(U - 1))
                nc.vector.tensor_scalar(f8_scale[:], f8_amax[:], 1e-12, 1.0 / 448.0, ALU.max, ALU.mult).then_inc(f8["scale_ready"], 1)
                dve.wait_ge(f8["scale_ready"], i + 1)
                nc.vector.reciprocal(f8_inv[:], f8_scale[:]).then_inc(f8["inv_ready"], 1)
                nc.vector.tensor_scalar(f8_total[:], f8_scale[:], f8_ws[:, 0:1], None, ALU.mult).then_inc(f8["total_ready"], 1)
                dve.wait_ge(f8["inv_ready"], i + 1)
                for u in range(U):
                    nc.vector.tensor_scalar(f8_xn[:, u, :], f8_xn[:, u, :], f8_inv[:, u:u + 1], None,
                                            ALU.mult).then_inc(f8["scaled"], 1)
                for u in range(U):
                    dve.wait_ge(f8["scaled"], n(u))
                    nc.vector.tensor_scalar(f8_magic[:, u, :].bitcast(I32), f8_xn[:, u, :].bitcast(I32), 0x7F800000, None,
                                            ALU.bitwise_and).then_inc(f8["exponent_ready"], 1)
                for u in range(U):
                    dve.wait_ge(f8["exponent_ready"], n(u))
                    nc.vector.tensor_scalar(f8_magic[:, u, :], f8_magic[:, u, :], 2.0 ** -6, 1.5 * 2.0 ** 20, ALU.max,
                                            ALU.mult).then_inc(f8["magic_ready"], 1)
                for u in range(U):
                    dve.wait_ge(f8["magic_ready"], n(u))
                    nc.vector.tensor_tensor(f8_xn[:, u, :], f8_xn[:, u, :], f8_magic[:, u, :], ALU.add).then_inc(f8["added"], 1)
                for u in range(U):
                    dve.wait_ge(f8["added"], n(u))
                    nc.vector.tensor_tensor(f8_q[:, u, :], f8_xn[:, u, :], f8_magic[:, u, :], ALU.subtract).then_inc(f8["q_ready"], 1)
                dve.wait_ge(f8["total_ready"], i + 1)
                for u in range(U):
                    t = U * i + u
                    dve.wait_ge(f8["out_done"], n(u))
                    dve.wait_ge(f8["x_biased"], n(u))
                    nc.vector.scalar_tensor_tensor(out=x[:, t, :], in0=bank(u, 1)[:, 0:D], scalar=f8_total[:, u:u + 1],
                                                   in1=x[:, t, :], op0=ALU.mult, op1=ALU.add).then_inc(f8["x_updated"], 1)
                for u in range(U):
                    row_stats(dve, U * i + u, f8["x_updated"], n(u), f8["stats_ready"])
            dve.wait_ge(f8["stats_ready"], 1 + NT)

        def ffn_tensor(pe):
            pe.wait_ge(f8["w_ready"], 1)
            with pe.Fori(0, NT // U) as i:
                n = lambda u: U * i + u + 1
                for u in range(U):
                    pe.wait_ge(f8["q_ready"], n(u))
                    for k in range(KC):
                        mm = nc.tensor.transpose(bank(u, 0).bitcast(BF16)[:, k * P:(k + 1) * P], f8_q[:, u, k * P:(k + 1) * P], ident_b[:])
                    mm.then_inc(f8["qT_done"], 1)
                for u in range(U):
                    pe.wait_ge(f8["qT_ready"], n(u))
                    for k in range(KC):
                        mm = nc.tensor.matmul(bank(u, 1)[:, 0:D], f8_qT[:, u, k, :], f8_w[:, k, :], start=(k == 0), stop=(k == KC - 1))
                    mm.then_inc(f8["out_done"], 1)

        def ffn_scalar(act):
            act_sqrt(act, "ffn0")
            with act.Fori(0, NT // U) as i:
                for u in range(U):
                    act.wait_ge(f8["qT_done"], U * i + u + 1)
                    nc.scalar.activation(f8_qT[:, u, :, :].rearrange("p k s -> p (k s)"), bank(u, 0).bitcast(BF16)[:, 0:D],
                                         ACT.Copy).then_inc(f8["qT_ready"], 1)

        x1_xn = sm_xn
        x1_wq = sb("x1_wq", [P, KC, D])
        x1_wk = sb("x1_wk", [P, KC, D])
        x1_wv = sb("x1_wv", [P, KC, D])
        x1_wo = sb("x1_wo", [P, KC, D])
        x1_bq = sb("x1_bq", [P, KC])
        x1_bk = sb("x1_bk", [P, KC])
        x1_bv = sb("x1_bv", [P, KC, P])
        x1_bo = sb("x1_bo", [P, D])
        x1_ctx = sb("x1_ctx", [P, KC, BT * SP + BT * G])
        x1_mask8 = sb("x1_mask8", [S, BT, SK], U8)
        hide = sb("hide", [S, L, S])
        hide_b = sb("hide_b", [S, L, S], BF16)
        row_pick = sb("row_pick", [2 * 32 + 2 * G, 2 * G])
        x1 = {s: sem(f"xattn1_{s}") for s in (
            "weights_loaded", "bias_product", "bias_ready", "norm_ready", "xT_done", "xT_ready", "q_done", "q_ready",
            "zeroed", "w_split", "ctx_loaded", "ctx_high", "ctx_split", "mask_loaded", "mask_ready", "q_swapped", "q_high", "q_low",
            "qbd_ready", "kv0_done", "kv1_done", "kv0_free", "kv1_free", "k_high", "vl_high", "pl_high", "scores_done",
            "max_ready", "exp_ready", "pT_done", "pT_ready", "pv_done", "last_done", "vlbd_ready", "rinv_ready",
            "heads_ready", "x_biased", "stats_ready")}
        J = BT * G

        def x1q_vector(dve):
            dve_rstd(dve, "xattn1")
            dve.wait_ge(x1["weights_loaded"], 16 * 8)
            dve.wait_ge(x1["bias_product"], 1)
            nc.vector.tensor_tensor(x1_bo[:], bank(0, 0)[:, 0:D], x1_bo[:], ALU.add).then_inc(x1["bias_ready"], 1)
            with dve.Fori(0, NT // U) as i:
                for u in range(U):
                    dve.wait_ge(x1["xT_done"], 1 + U * i)
                    dve_normalise(U * i + u, x1_xn[:, u, :]).then_inc(x1["norm_ready"], 1)

        def x1q_tensor(pe):
            pe.wait_ge(x1["weights_loaded"], 16 * 8)
            for k in range(KC):
                mm = nc.tensor.matmul(bank(0, 0)[:, 0:D], x1_bv[:, k, :], x1_wo[:, k, :], start=(k == 0), stop=(k == KC - 1))
            mm.then_inc(x1["bias_product"], 1)
            pe.wait_ge(x1["bias_ready"], 1)
            with pe.Fori(0, NT // U) as i:
                for u in range(U):
                    pe.wait_ge(x1["norm_ready"], U * i + u + 1)
                    for k in range(KC):
                        mm = nc.tensor.transpose(bank(u, 0)[:, k * P:(k + 1) * P], x1_xn[:, u, k * P:(k + 1) * P], ident[:])
                    mm.then_inc(x1["xT_done"], 1)
                pe.wait_ge(x1["xT_ready"], U * (i + 1))
                for m in range(KC):
                    for k in range(KC):
                        mm = nc.tensor.matmul(bank(m, 1), x1_wq[:, k, m * P:(m + 1) * P], x1_xT[:, k, :],
                                              start=(k == 0), stop=(k == KC - 1))
                    mm.then_inc(x1["q_done"], 1)

        def context_high(act, t, par, k):
            act.wait_ge(x1["ctx_loaded"], 16 * (t + 1))
            nc.scalar.activation(x1_cs[par][0][:, k, :], x1_ctx[:, k, :], ACT.Copy).then_inc(x1["ctx_high"], 1)

        def mask(act, t, par):
            act.wait_ge(x1["mask_loaded"], 16 * (t + 1))
            nc.scalar.activation(x1_mask[par][:, :, 0:SK], x1_mask8[:], ACT.Copy).then_inc(x1["mask_ready"], 1)

        def x1q_scalar(act):
            act_sqrt(act, "xattn1")
            for k in range(KC):
                context_high(act, 0, 0, k)
            act.wait_ge(x1["zeroed"], 2 + 2)
            mask(act, 0, 0)
            with act.Fori(0, NT // U) as i:
                for u in range(U):
                    act.wait_ge(x1["xT_done"], 1 + U * i + u + 1)
                    nc.scalar.activation(x1_xT[:, :, u * P:(u + 1) * P], bank(u, 0)[:, 0:D].rearrange("p (k s) -> p k s", k=KC),
                                         ACT.Copy).then_inc(x1["xT_ready"], 1)
                for m in range(KC):
                    hold(act, x1["q_done"], KC * i + m + 1)
                    for r in range(2):
                        rows = slice(64 * r, 64 * r + 64)
                        ins = nc.scalar.activation(x1_qT[rows, 2 * m + r, bass.ds(i * (U * P), U * P)], bank(m, 1)[rows, :],
                                                   ACT.Identity, bias=x1_bq[rows, m:m + 1])
                    ins.then_inc(x1["q_ready"], 1)

        ORDER = [(0, "k0", 1, 0), (1, "k1", 1, 0), (2, "plT", 1, -1), (3, "v", 1, 0),
                 (4, "k0", 2, 0), (5, "k1", 2, 0), (6, "oT", 1, -1), (7, "v", 2, 0), (7, "out", 0, -1),
                 (8, "k0", 3, 0), (9, "k1", 3, 0), (10, "plT", 0, 0), (11, "v", 3, 0),
                 (12, "k0", 0, 1), (13, "k1", 0, 1), (14, "oT", 0, 0), (15, "v", 0, 1), (15, "vl", 0, 1)]
        PIECES = len(ORDER)
        LEAD = 13
        HJ = J // 2
        STACK = 2 * 32 + HJ

        def kv_bank(n):
            return psum[:, n % 2, :]

        def place(kind, b=0):
            return next(n for n, (_, k, bb, _) in enumerate(ORDER) if (k, bb) == (kind, b))

        def kv_count(n, t):
            return PIECES // 2 * (t + 1) + n // 2 - (LEAD // 2 - n % 2)

        def kv_free(eng, n, t):
            eng.wait_ge(x1[f"kv{n % 2}_free"], kv_count(n, t))

        def kv_done(eng, n, t):
            eng.wait_ge(x1[f"kv{n % 2}_done"], kv_count(n, t))

        def kv_taken(eng, n, t):
            eng.wait_ge(x1[f"kv{n % 2}_free"], kv_count(n, t) + 1)

        def x1_tiles(eng, tile):
            tile(0, 0, False, True, True)
            with eng.Fori(0, (NT - 2) // 2) as i:
                for n in range(2):
                    tile(2 * i + (1 + n), (1 + n) % 2, True, True, True)
            tile(NT - 1, (NT - 1) % 2, True, True, False)
            tile(NT, NT % 2, True, False, False)

        def exact(out, pairs, first, last, **kw):
            for n, (v, w) in enumerate(pairs):
                mm = nc.tensor.matmul(out, v, w, start=(first and n == 0), stop=(last and n == len(pairs) - 1), **kw)
            return mm

        def parts(v, w):
            return ((v[0], w[0]), (v[0], w[1]), (v[1], w[0]))

        def x1_piece(pe, n, t, par):
            _, kind, b, whose = ORDER[n]
            ct = x1_cs[(par + 1) % 2 if whose == 1 else par]
            out = kv_bank(n)
            if kind == "k0" and b == 0:
                pe.wait_ge(x1["ctx_split"], t + 1 + 1)
            kv_free(pe, n, t)
            if kind == "vl":
                for h in range(2):
                    for k in range(KC):
                        cols = slice(BT * SP + h * HJ, BT * SP + (h + 1) * HJ)
                        mm = exact(out[0:HJ, h * D:(h + 1) * D], parts([c[:, k, cols] for c in ct], [w[:, k, :] for w in x1_wvs]),
                                   k == 0, k == KC - 1, skip_group_check=True)
            elif kind in ("k0", "k1"):
                m = slice(int(kind[1]) * P, int(kind[1]) * P + P)
                for k in range(KC):
                    mm = exact(out[:, 0:SP], parts([w[:, k, m] for w in x1_wks], [c[:, k, b * SP:(b + 1) * SP] for c in ct]),
                               k == 0, k == KC - 1)
            elif kind == "v":
                for c0 in range(2):
                    cols = slice(b * SP + c0 * P, b * SP + (c0 + 1) * P)
                    for k in range(KC):
                        mm = exact(out[:, c0 * D:(c0 + 1) * D], parts([c[:, k, cols] for c in ct], [w[:, k, :] for w in x1_wvs]),
                                   k == 0, k == KC - 1, skip_group_check=True)
            elif kind == "plT":
                pe.wait_ge(x1["exp_ready"], J * (t + 1 + whose) - HJ + HJ * b)
                mm = nc.tensor.transpose(out[0:HJ, 0:P], x1_p[:, HJ * b:HJ * (b + 1), SK - 1], ident[:])
            elif kind == "oT":
                pe.wait_ge(x1["heads_ready"], 2 * (t + whose) + b + 1)
                mm = nc.tensor.transpose(out[:, 0:P], x1_o[:, b * HJ:(b + 1) * HJ, :].rearrange("p j d -> p (j d)"), ident[:])
            elif kind == "out":
                kv_taken(pe, place("oT", 1), t)
                for k in range(KC):
                    mm = nc.tensor.matmul(out[:, 0:D], x1_oT[:, k, :, :].rearrange("p b s -> p (b s)"), x1_wo[:, k, :],
                                          start=(k == 0), stop=(k == KC - 1))
            mm.then_inc(x1[f"kv{n % 2}_done"], 1)

        def x1_no_piece(pe, n, t):
            kv_free(pe, n, t)
            pe.sem_inc(x1[f"kv{n % 2}_done"], 1)
            pe.sem_inc(x1[f"kv{n % 2}_free"], 1)

        def x1_tensor(pe):
            pe.wait_ge(x1["q_ready"], KC * NT // U)
            pe.wait_ge(x1["w_split"], 4)
            for k in range(2):
                pe.sem_inc(x1[f"kv{k}_free"], 1)
            for n in range(LEAD, PIECES):
                if ORDER[n][3] == 1:
                    x1_piece(pe, n, -1, 1)
                else:
                    x1_no_piece(pe, n, -1)

            def last_key(t, h):
                kv_taken(pe, place("plT", h), t)
                nc.tensor.matmul(psum[:, 6 + h, :], x1_plT[:], x1_vlbd[:, h, :, :].rearrange("p j d -> p (j d)"),
                                 start=False, stop=True, skip_group_check=True).then_inc(x1["last_done"], 1)

            def tile(t, par, before, own, after):
                there = {-1: before, 0: own, 1: after}
                for s in range(J):
                    if own:
                        b, g = s // G, s % G
                        r = 64 * (g % 2)
                        if g == 0:
                            for m in range(KC):
                                kv_taken(pe, place(f"k{m}", b), t - (b == 0))
                        if s % HJ == 0:
                            pe.wait_ge(x1["qbd_ready"], 2 * t + s // HJ + 1)
                        if s == 0:
                            pe.wait_ge(x1["mask_ready"], 1 + t + 1)
                        if s >= 2 or before:
                            pe.wait_ge(x1["exp_ready"], J * t + s - 1)
                        sc = psum[:, 2 + s % 2, 0:SP]
                        nc.tensor.matmul(sc, hide_b[:].rearrange("p l q -> p (l q)"), x1_mask[par][:, b, :], start=True, stop=False)
                        nc.tensor.matmul(sc, x1_qh[:, b // 2, g, b % 2, :], x1_k[:, b % 2, g, :], start=False, stop=False)
                        nc.tensor.matmul(sc, x1_ql[r:r + 64, b // 2, g, b % 2, :], x1_k[r:r + 64, b % 2, g, :],
                                         start=False, stop=True).then_inc(x1["scores_done"], 1)
                    if before if s < 2 else own:
                        pe.wait_ge(x1["exp_ready"], J * t + s - 1)
                        if s >= 4 or before:
                            pe.wait_ge(x1["pT_ready"], J * t + s - 3)
                        for c in range(2):
                            mm = nc.tensor.transpose(psum[:, 4 + s % 2, c * P:(c + 1) * P], x1_p[:, (s - 2) % J, c * P:(c + 1) * P], ident[:])
                        mm.then_inc(x1["pT_done"], 1)
                    if before if s < 3 else own:
                        j = (s - 3) % J
                        b, g = j // G, j % G
                        pe.wait_ge(x1["pT_ready"], J * t + s - 2)
                        if g == 0:
                            kv_taken(pe, place("v", b), t - (b == 0))
                        for c in range(2):
                            mm = nc.tensor.matmul(psum[:, 6 + b // 2, (b % 2) * D + g * 64:(b % 2) * D + (g + 1) * 64],
                                                  x1_pT[:, j % 2, c, :], x1_v[:, b % 2, c, g * 64:(g + 1) * 64],
                                                  start=(b % 2 == 0 and g == 0 and c == 0), stop=False, skip_group_check=True)
                        mm.then_inc(x1["pv_done"], 1)
                    for n, (at, _, _, whose) in enumerate(ORDER):
                        if at == s:
                            if there[whose]:
                                x1_piece(pe, n, t, par)
                            else:
                                x1_no_piece(pe, n, t)
                    if s == 4 and before:
                        last_key(t, 1)
                    if s == 12 and own:
                        pe.wait_ge(x1["vlbd_ready"], t + 1)
                        last_key(t, 0)

            x1_tiles(pe, tile)

        def x1_scalar(act):
            nc.scalar.preload_act_table(ACT.Exp)

            def take(n, t):
                _, kind, b, _ = ORDER[n]
                if kind in ("k0", "k1"):
                    m = int(kind[1])
                    hold(act, x1[f"kv{n % 2}_done"], kv_count(n, t))
                    for r in range(2):
                        rows = slice(64 * r, 64 * r + 64)
                        ins = nc.scalar.activation(x1_k[rows, b % 2, 2 * m + r, :], kv_bank(n)[rows, 0:SP], ACT.Identity,
                                                   bias=x1_bk[rows, m:m + 1])
                    ins.then_inc(x1["k_high"], 1)
                elif kind == "v":
                    kv_done(act, n, t)
                    nc.scalar.activation(x1_v[:, b % 2, :, :].rearrange("p c n -> p (c n)"), kv_bank(n),
                                         ACT.Copy).then_inc(x1[f"kv{n % 2}_free"], 1)
                elif kind == "vl":
                    if not (isinstance(t, int) and t < 0):
                        act.wait_ge(x1["vlbd_ready"], t + 1)
                    kv_done(act, n, t)
                    for row in (0, 64):
                        ins = nc.scalar.activation(x1_vls[row:row + HJ, :], kv_bank(n)[0:HJ, :], ACT.Copy)
                    ins.then_inc(x1["vl_high"], 1)
                elif kind == "oT":
                    kv_done(act, n, t)
                    for r in range(2):
                        for rb in range(2):
                            v = kv_bank(n)[64 * rb:64 * rb + 64, 0:P].rearrange("p (j r q) -> p r j q", j=L // 2, r=2)[:, r]
                            ins = nc.scalar.copy(x1_oT[64 * r:64 * r + 64, :, 2 * b + rb, :], v)
                    ins.then_inc(x1[f"kv{n % 2}_free"], 1)

            def queries_high(t):
                nc.scalar.activation(x1_qhigh[:].rearrange("p h g c -> p g h c"),
                                     x1_qT[:, :, bass.ds(t * P, P)].rearrange("p g (h c) -> p g h c", h=2),
                                     ACT.Copy).then_inc(x1["q_high"], 1)

            act.wait_ge(x1["q_swapped"], 1)
            queries_high(0)
            for n in range(LEAD, PIECES):
                if ORDER[n][3] == 1:
                    take(n, -1)

            def tile(t, par, before, own, after):
                there = {-1: before, 0: own, 1: after}
                for s in range(J):
                    if after:
                        if s in (3, 4):
                            context_high(act, t + 1, 1 - par, s - 3)
                        if s == 7:
                            mask(act, t + 1, 1 - par)
                        if s == 11:
                            hold(act, x1["qbd_ready"], 2 * (t + 1))
                            if not before:
                                act.wait_ge(x1["q_swapped"], NT // U)
                            queries_high(t + 1)
                    if own:
                        act.wait_ge(x1["max_ready"], J * t + s + 1)
                        nc.scalar.activation(x1_p[:, s, :], psum[:, 2 + s % 2, 0:SK], ACT.Exp, bias=x1_nmax[:, s:s + 1],
                                             accum_out=x1_sum[:, s:s + 1]).then_inc(x1["exp_ready"], 1)
                    for n, (at, _, _, whose) in enumerate(ORDER):
                        if at == s and there[whose]:
                            take(n, t)

            x1_tiles(act, tile)

        def x1_vector(dve):
            dve.wait_ge(x1["x_biased"], NT)

            dve.wait_ge(x1["q_ready"], KC * NT // U)
            for i in range(NT // U):
                cols = slice(i * U * P, (i + 1) * U * P)
                for r in range(2):
                    odd = x1_qT[:, :, cols].rearrange("p (k r) c -> p r k c", r=2)[:, r]
                    ins = nc.vector.tensor_copy(odd[64 * (1 - r):64 * (1 - r) + 64], odd[64 * r:64 * r + 64])
                ins.then_inc(x1["q_swapped"], 1)

            def take(n, t):
                _, kind, b, whose = ORDER[n]
                freed = x1[f"kv{n % 2}_free"]
                if kind in ("k0", "k1"):
                    m = int(kind[1])
                    dve.wait_ge(x1["k_high"], 2 * BT * (t + whose) + 2 * b + m + 1)
                    for r in range(2):
                        rows, over = slice(64 * r, 64 * r + 64), slice(64 * (1 - r), 64 * (1 - r) + 64)
                        ins = nc.vector.scalar_tensor_tensor(out=x1_k[over, b % 2, 2 * m + r, :], in0=kv_bank(n)[rows, 0:SP],
                                                             scalar=x1_bk[rows, m:m + 1],
                                                             in1=x1_k[rows, b % 2, 2 * m + r, :].bitcast(F32),
                                                             op0=ALU.add, op1=ALU.subtract)
                    ins.then_inc(freed, 1)
                elif kind == "vl":
                    dve.wait_ge(x1["vl_high"], t + 1 + 1)
                    nc.vector.tensor_tensor(x1_vls[32:32 + HJ, :], kv_bank(n)[0:HJ, :], x1_vls[0:HJ, :].bitcast(F32),
                                            ALU.subtract).then_inc(freed, 1)
                elif kind == "plT":
                    hold(dve, x1[f"kv{n % 2}_done"], kv_count(n, t))
                    nc.vector.tensor_copy(x1_plT[0:HJ, :], kv_bank(n)[0:HJ, 0:P]).then_inc(x1["pl_high"], 1)
                    nc.vector.tensor_copy(x1_plT[32:32 + HJ, :], kv_bank(n)[0:HJ, 0:P])
                    dve.wait_ge(x1["pl_high"], 2 * (t + whose) + b + 1)
                    nc.vector.tensor_tensor(x1_plT[64:64 + HJ, :], kv_bank(n)[0:HJ, 0:P], x1_plT[0:HJ, :].bitcast(F32),
                                            ALU.subtract).then_inc(freed, 1)
                elif kind == "out":
                    kv_done(dve, n, t)
                    nc.vector.tensor_tensor(x[:, bass.ds(t + whose, 1), :].rearrange("p o c -> p (o c)"), kv_bank(n)[:, 0:D],
                                            x[:, bass.ds(t + whose, 1), :].rearrange("p o c -> p (o c)"), ALU.add).then_inc(freed, 1)

            def inverse(h, n):
                c = slice(h * HJ, (h + 1) * HJ)
                nc.vector.tensor_scalar(x1_void[:, c], x1_nmax[:, c], 1e10, 0.0, ALU.mult, ALU.mult)
                nc.vector.reciprocal(x1_rinv[:, c], x1_sum[:, c]).then_inc(x1["rinv_ready"], 1)
                dve.wait_ge(x1["rinv_ready"], 2 * n + 1)
                nc.vector.tensor_tensor(x1_rinv[:, c], x1_rinv[:, c], x1_void[:, c], ALU.add).then_inc(x1["rinv_ready"], 1)

            def heads(h, n):
                dve.wait_ge(x1["rinv_ready"], 2 * n + 2)
                dve.wait_ge(x1["last_done"], n + 1)
                c = slice(h * HJ, (h + 1) * HJ)
                pick_heads(psum[:, 6 + h:7 + h, :], x1_rinv[:, c], x1_o[:, c, :]).then_inc(x1["heads_ready"], 1)

            for n in range(LEAD, PIECES):
                if ORDER[n][3] == 1 and ORDER[n][1] != "vl":
                    take(n, -1)

            def tile(t, par, before, own, after):
                there = {-1: before, 0: own, 1: after}
                for s in range(J):
                    if own:
                        dve.wait_ge(x1["scores_done"], J * t + s + 1)
                        nc.vector.tensor_reduce(x1_nmax[:, s:s + 1], psum[:, 2 + s % 2, 0:SK], AX.X, ALU.max,
                                                negate=True).then_inc(x1["max_ready"], 1)
                    if before if s < 2 else own:
                        dve.wait_ge(x1["pT_done"], J * t + s - 1)
                        if s >= 4 or before:
                            dve.wait_ge(x1["pv_done"], J * t + s - 3)
                        nc.vector.tensor_copy(x1_pT[:, s % 2, :, :].rearrange("p c n -> p (c n)"),
                                              psum[:, 4 + s % 2, 0:D]).then_inc(x1["pT_ready"], 1)
                    for n, (at, _, _, whose) in enumerate(ORDER):
                        if at == s - 1 and there[whose]:
                            take(n, t)
                    if s == 0 and own:
                        take(place("vl"), t - 1)
                    if s == 3 and before:
                        dve.wait_ge(x1["exp_ready"], J * t)
                        inverse(1, 2 * t - 1)
                    if s == 4 and before:
                        heads(1, 2 * t - 1)
                    if s == 11 and own:
                        dve.wait_ge(x1["exp_ready"], J * t + HJ)
                        inverse(0, 2 * t)
                    if s == 12 and own:
                        heads(0, 2 * t)
                    if s == 15 and before:
                        n = place("out")
                        hold(dve, x1[f"kv{n % 2}_free"], kv_count(n, t) + 1)
                        nc.vector.bn_stats(bn_out[:, bass.ds(t - 1, 1), :].rearrange("p o c -> p (o c)"),
                                           x[:, bass.ds(t - 1, 1), :].rearrange("p o c -> p (o c)")).then_inc(x1["stats_ready"], 1)

            x1_tiles(dve, tile)
            dve.wait_ge(x1["stats_ready"], NT)

        def x1_pool_weights(pool):
            pool.wait_ge(x1["weights_loaded"], 16 * 8)
            pool.wait_ge(var_ready, layers.index("xattn1") + 1)
            for v in x1_mask:
                nc.gpsimd.memset(v[:], 0.0).then_inc(x1["zeroed"], 1)
            for v in (x1_plT, x1_vls):
                nc.gpsimd.memset(v[:].bitcast(F32), 0.0).then_inc(x1["zeroed"], 1)
            for w, (high, low) in ((x1_wk, x1_wks), (x1_wv, x1_wvs)):
                nc.gpsimd.tensor_copy(high[:], w[:]).then_inc(x1["w_split"], 1)
                pool.wait_ge(x1["w_split"], 1 if w is x1_wk else 3)
                nc.gpsimd.tensor_tensor(low[:], w[:], high[:].bitcast(F32), ALU.subtract).then_inc(x1["w_split"], 1)

        def x1_pool(pool):
            def context(t, par):
                high, low = x1_cs[par]
                pool.wait_ge(x1["ctx_high"], KC * (t + 1))
                nc.gpsimd.tensor_tensor(low[:], x1_ctx[:], high[:].bitcast(F32), ALU.subtract).then_inc(x1["ctx_split"], 1)

            def queries(t):
                own = x1_qT[:, :, bass.ds(t * P, P)].rearrange("p g (h c) -> p g h c", h=2)
                hold(pool, x1["q_high"], t + 1)
                nc.gpsimd.tensor_tensor(x1_qlow[:].rearrange("p h g c -> p g h c"), own, x1_qhigh[:].rearrange("p h g c -> p g h c").bitcast(F32),
                                        ALU.subtract).then_inc(x1["q_low"], 1)

            def spread(t, h):
                if h == 0:
                    pool.wait_ge(x1["q_low"], t + 1)
                for dst, src in ((x1_qh, x1_qhigh), (x1_ql, x1_qlow)):
                    shape = [P, 2 * G, L, S]
                    ins = nc.gpsimd.tensor_tensor(
                        dst[:, h].rearrange("p g b (l q) -> p (g b) l q", l=L),
                        src[:, h].rearrange("p g (b q) -> p (g b) q", b=2).unsqueeze(2).broadcast_to(shape),
                        head_scale[:].unsqueeze(1).unsqueeze(3).broadcast_to(shape), ALU.mult)
                ins.then_inc(x1["qbd_ready"], 1)

            context(0, 0)
            queries(0)
            spread(0, 0)
            spread(0, 1)

            def tile(t, par, before, own, after):
                if after:
                    if before:
                        pool.wait_ge(x1["scores_done"], J * t)
                    context(t + 1, 1 - par)
                if own:
                    if before:
                        pool.wait_ge(x1["last_done"], 2 * t)
                    kv_taken(pool, place("vl"), t - 1)
                    shape = [STACK, 2, G, 64]
                    for h in range(2):
                        ins = nc.gpsimd.tensor_tensor(
                            x1_vlbd[:, h].rearrange("p (b g) d -> p b g d", b=2),
                            x1_vls[:, h * D:(h + 1) * D].rearrange("p (g d) -> p g d", g=G).unsqueeze(1).broadcast_to(shape),
                            row_pick[:].rearrange("p (b g) -> p b g", b=2).unsqueeze(3).broadcast_to(shape), ALU.mult)
                    ins.then_inc(x1["vlbd_ready"], 1)
                if after:
                    queries(t + 1)
                    for h in range(2):
                        pool.wait_ge(x1["scores_done"], J * t + HJ * (h + 1))
                        spread(t + 1, h)

            x1_tiles(pool, tile)

        mx_w1 = sb("mx_w1", [P, KC, GH])
        mx_b1 = sb("mx_b1", [GH, 1])
        mx_w2 = sb("mx_w2", [GH, R])
        mx_b2 = sb("mx_b2", [R, 1])
        mx_wu = sb("mx_wu", [P, KC, R])
        mx_wv = sb("mx_wv", [P, KC, R])
        mx_conv = sb("mx_conv", [P, KC, 3])
        mx_wo = sb("mx_wo", [R, D])
        mx_bo = sb("mx_bo", [P, D])
        mx_keep = sb("mx_keep", [R, U * P])
        mx = {s: sem(f"mix1_{s}") for s in (
            "weights_loaded", "taps_ready", "bias_ready", "norm_ready", "xT_done", "xT_ready", "h_done", "h_ready", "uv_done",
            "gate_done", "gate_ready", "sum_ready", "gu_ready", "glob_ready", "out_done", "x_biased", "x_updated", "stats_ready")}

        def mix_vector(dve):
            dve.wait_ge(mx["weights_loaded"], 16 * 10)
            for k in range(KC):
                for j in range(3):
                    nc.vector.tensor_scalar(mx_taps[:, k, j, :], ident[:], mx_conv[:, k, j:j + 1], None,
                                            ALU.mult).then_inc(mx["taps_ready"], 1)
            nc.vector.memset(mx_xT[:], 0.0).then_inc(mx["taps_ready"], 1)
            dve_rstd(dve, "mix1")
            with dve.Fori(0, NT // U) as i:
                n = lambda u: U * i + u + 1
                hold(dve, mx["stats_ready"], 1 + U * i)
                for u in range(U):
                    dve_normalise(U * i + u, sm_xn[:, u, :]).then_inc(mx["norm_ready"], 1)
                dve.wait_ge(mx["uv_done"], i + 1)
                nc.vector.tensor_tensor_scan(mx_sum[:], mx_keep[:], psum[0:R, 3, :], 0.0, ALU.mult, ALU.add).then_inc(mx["sum_ready"], 1)
                dve.wait_ge(mx["gate_ready"], i + 1)
                nc.vector.tensor_tensor(mx_gu[:], psum[0:R, 5, :], mx_gate[:], ALU.mult).then_inc(mx["gu_ready"], 1)
                dve.wait_ge(mx["gu_ready"], i + 1)
                dve.wait_ge(mx["sum_ready"], i + 1)
                nc.vector.tensor_tensor(mx_glob[:], mx_gu[:], mx_sum[:], ALU.mult).then_inc(mx["glob_ready"], 1)
                for u in range(U):
                    dve.wait_ge(mx["out_done"], n(u))
                    dve.wait_ge(mx["x_biased"], n(u))
                    nc.vector.tensor_tensor(x[:, U * i + u, :], bank(u, 0)[:, 0:D], x[:, U * i + u, :], ALU.add).then_inc(mx["x_updated"], 1)
                for u in range(U):
                    row_stats(dve, U * i + u, mx["x_updated"], n(u), mx["stats_ready"])
            dve.wait_ge(mx["stats_ready"], 1 + NT)

        def mix_tensor(pe):
            pe.wait_ge(mx["weights_loaded"], 16 * 10)
            pe.wait_ge(mx["taps_ready"], 3 * KC + 1)
            with pe.Fori(0, NT // U) as i:
                for u in range(U):
                    pe.wait_ge(mx["norm_ready"], U * i + u + 1)
                    for k in range(KC):
                        mm = nc.tensor.transpose(bank(u, 0)[:, k * P:(k + 1) * P], sm_xn[:, u, k * P:(k + 1) * P], ident[:])
                    mm.then_inc(mx["xT_done"], 1)
                pe.wait_ge(mx["xT_ready"], U * (i + 1))
                rows = [mx_xT[:, 1, k, 1:1 + U * P] for k in range(KC)]
                for k in range(KC):
                    mm = nc.tensor.matmul(psum[0:GH, 1, :], mx_w1[:, k, :], rows[k], start=(k == 0), stop=(k == KC - 1))
                mm.then_inc(mx["h_done"], 1)
                for w, q in ((mx_wv, 3), (mx_wu, 5)):
                    for k in range(KC):
                        mm = nc.tensor.matmul(psum[0:R, q, :], w[:, k, :], rows[k], start=(k == 0), stop=(k == KC - 1))
                mm.then_inc(mx["uv_done"], 1)
                hold(pe, mx["h_ready"], i + 1)
                nc.tensor.matmul(psum[0:R, 7, :], mx_w2[:], mx_h[:], start=True, stop=True).then_inc(mx["gate_done"], 1)
                for u in range(U):
                    for k in range(KC):
                        for j in range(3):
                            nc.tensor.matmul(bank(u, 0)[:, k * P:(k + 1) * P], mx_xT[:, j, k, u * P + j:(u + 1) * P + j],
                                             mx_taps[:, k, j, :], start=(k == 0 and j == 0), stop=False, skip_group_check=True)
                pe.wait_ge(mx["glob_ready"], i + 1)
                for u in range(U):
                    nc.tensor.matmul(bank(u, 0)[:, 0:D], mx_glob[:, u * P:(u + 1) * P], mx_wo[:], start=False, stop=True,
                                     skip_group_check=True).then_inc(mx["out_done"], 1)

        def mix_scalar(act):
            act_sqrt(act, "mix1")
            nc.scalar.preload_act_table(ACT.Sigmoid)
            act.wait_ge(mx["taps_ready"], 3 * KC + 1)
            with act.Fori(0, NT // U) as i:
                for u in range(U):
                    act.wait_ge(mx["xT_done"], U * i + u + 1)
                    for j, (s0, s1) in enumerate(((0, S - 1), (0, S), (1, S))):
                        src = bank(u, 0)[:, 0:D].rearrange("p (k b s) -> p k b s", k=KC, b=BT)
                        dst = mx_xT[:, j, :, 1 + u * P:1 + (u + 1) * P].rearrange("p k (b s) -> p k b s", b=BT)
                        ins = nc.scalar.activation(dst[:, :, :, s0:s1], src[:, :, :, s0:s1], ACT.Copy)
                    ins.then_inc(mx["xT_ready"], 1)
                act.wait_ge(mx["h_done"], i + 1)
                nc.scalar.activation(mx_h[:], psum[0:GH, 1, :], ACT.Relu, bias=mx_b1[:, 0:1]).then_inc(mx["h_ready"], 1)
                act.wait_ge(mx["gate_done"], i + 1)
                nc.scalar.activation(mx_gate[:], psum[0:R, 7, :], ACT.Sigmoid, bias=mx_b2[:, 0:1]).then_inc(mx["gate_ready"], 1)

        me_raw = sb("me_raw", [P, 2, 1024])
        me_b1 = sb("me_b1", [P, EX, HM])
        me_b2 = sb("me_b2", [EX, D])
        me_rw = sb("me_rw", [P, KC, E])
        me_rb = sb("me_rb", [P, E])
        me_before = sb("me_before", [P, E, E])
        me = {s: sem(f"moe1_{s}") for s in (
            "weights_loaded", "router_split", "norm_ready", "xT_done", "xh_ready", "xl_ready", "lT_done", "lT_ready", "logits_done", "logits_read",
            "exp_ready", "gate_ready", "gT_done", "gT_ready", "raw_loaded", "w1h", "w1_split", "w2_split",
            "up_done", "h_ready", "hh_ready", "hl_ready", "down_done", "acc_ready", "stored")}

        def split(dve, high, low, src, sem_h, count, sem_l):
            nc.vector.tensor_copy(high, src).then_inc(sem_h, 1)
            dve.wait_ge(sem_h, count)
            nc.vector.tensor_tensor(low, src, high.bitcast(F32), ALU.subtract).then_inc(sem_l, 1)

        def moe_weights(dve, e, par):
            dve.wait_ge(me["raw_loaded"], 16 * (e + 1))
            split(dve, me_wh[par][:, 0, :], me_wl[par][:, 0, :], me_raw[:, 0, :], me["w1h"], 2 * e + 1, me["w1_split"])
            split(dve, me_wh[par][:, 1, :], me_wl[par][:, 1, :], me_raw[:, 1, :], me["w1h"], 2 * e + 2, me["w2_split"])

        def moe_prep_vector(dve):
            dve.wait_ge(me["weights_loaded"], 16 * 5)
            link(dve, nc.vector.tensor_copy(me_rwh[:], me_rw[:]))
            link(dve, nc.vector.tensor_tensor(me_rwl[:], me_rw[:], me_rwh[:].bitcast(F32), ALU.subtract))
            nc.vector.memset(me_gate[:], 1.0).then_inc(me["router_split"], 1)
            moe_weights(dve, 0, 0)
            dve_rstd(dve, "moe1")
            with dve.Fori(0, NT // U) as i:
                for u in range(U):
                    dve_normalise(U * i + u, sm_xn[:, u, :]).then_inc(me["norm_ready"], 1)
                for u in range(U):
                    t = U * i + u
                    dve.wait_ge(me["xh_ready"], t + 1)
                    nc.vector.tensor_tensor(me_xl[:, :, bass.ds(t * P, P)], bank(u, 0)[:, 0:D].rearrange("p (k s) -> p k s", k=KC),
                                            me_xh[:, :, bass.ds(t * P, P)].bitcast(F32), ALU.subtract).then_inc(me["xl_ready"], 1)

        def moe_gates(dve):
            dve.wait_ge(me["logits_done"], 1)
            dve.wait_ge(me["router_split"], 1)
            wide = [P, NT, E]
            link(dve, nc.vector.tensor_tensor(me_pr[:], logits(), me_rb[:].unsqueeze(1).broadcast_to(wide), ALU.add))
            link(dve, nc.vector.tensor_reduce(me_st[:], me_pr[:], AX.X, ALU.max))
            nc.vector.tensor_tensor(me_pr[:], me_pr[:], me_st[:].unsqueeze(2).broadcast_to(wide), ALU.subtract).then_inc(me["logits_read"], 1)
            dve.wait_ge(me["exp_ready"], 1)
            link(dve, nc.vector.tensor_reduce(me_st[:], me_pr[:], AX.X, ALU.add))
            link(dve, nc.vector.reciprocal(me_st[:], me_st[:]))
            link(dve, nc.vector.tensor_tensor(me_pr[:], me_pr[:], me_st[:].unsqueeze(2).broadcast_to(wide), ALU.mult))
            full = [P, NT, E, E]
            mine, other = me_pr[:].unsqueeze(3).broadcast_to(full), me_pr[:].unsqueeze(2).broadcast_to(full)
            link(dve, nc.vector.tensor_tensor(me_cmp[:], other, mine, ALU.is_equal))
            link(dve, nc.vector.tensor_tensor(me_cmp[:], me_cmp[:], me_before[:].unsqueeze(1).broadcast_to(full), ALU.mult))
            link(dve, nc.vector.tensor_tensor(me_cmp2[:], other, mine, ALU.is_gt))
            link(dve, nc.vector.tensor_tensor(me_cmp[:], me_cmp[:], me_cmp2[:], ALU.add))
            link(dve, nc.vector.tensor_reduce(me_rank[:], me_cmp[:], AX.X, ALU.add))
            link(dve, nc.vector.tensor_scalar(me_rank[:], me_rank[:], 2.0, None, ALU.is_lt))
            nc.vector.tensor_tensor(me_gate[:, :, 0:E], me_rank[:], me_pr[:], ALU.mult).then_inc(me["gate_ready"], 1)

        def logits():
            return bank(3, 1)[:, 0:NT * E].rearrange("p (t e) -> p t e", t=NT)

        def moe_prep_tensor(pe):
            pe.wait_ge(me["router_split"], 1)
            with pe.Fori(0, NT // U) as i:
                for u in range(U):
                    pe.wait_ge(me["norm_ready"], U * i + u + 1)
                    for k in range(KC):
                        mm = nc.tensor.transpose(bank(u, 0)[:, k * P:(k + 1) * P], sm_xn[:, u, k * P:(k + 1) * P], ident[:])
                    mm.then_inc(me["xT_done"], 1)
                pe.wait_ge(me["xl_ready"], U * (i + 1))
                pe.wait_ge(me["lT_ready"], 1 + i)
                for k in range(KC):
                    rows = [v[:, k, bass.ds(i * (U * P), U * P)] for v in (me_xh, me_xl)]
                    mm = exact(bank(1, 1)[0:E, :], parts([w[:, k, :] for w in (me_rwh, me_rwl)], rows), k == 0, k == KC - 1)
                mm.then_inc(me["lT_done"], 1)
            pe.wait_ge(me["lT_ready"], 1 + NT // U)
            for t in range(NT):
                mm = nc.tensor.transpose(bank(3, 1)[:, t * E:(t + 1) * E], me_lT[:, t * P:(t + 1) * P], ident[0:E, 0:E])
            mm.then_inc(me["logits_done"], 1)

        def moe_prep_scalar(act):
            act_sqrt(act, "moe1")
            with act.Fori(0, NT // U) as i:
                for u in range(U):
                    t = U * i + u
                    hold(act, me["xT_done"], t + 1)
                    nc.scalar.activation(me_xh[:, :, bass.ds(t * P, P)], bank(u, 0)[:, 0:D].rearrange("p (k s) -> p k s", k=KC),
                                         ACT.Copy).then_inc(me["xh_ready"], 1)
                hold(act, me["lT_done"], i + 1)
                nc.scalar.activation(me_lT[:, bass.ds(i * (U * P), U * P)], bank(1, 1)[0:E, :], ACT.Copy).then_inc(me["lT_ready"], 1)
            act.wait_ge(me["logits_read"], 1)
            nc.scalar.activation(me_pr[:], me_pr[:], ACT.Exp).then_inc(me["exp_ready"], 1)

        NG = NT // TG

        def down_psum(gr, tau):
            return psum[:, 4 + 2 * (gr % 2) + tau // 2, (tau % 2) * D:(tau % 2) * D + D]

        def moe_experts(eng, expert):
            expert(0, 0)
            gates_turned(eng)
            with eng.Fori(0, (EX - 3) // 2) as i:
                for n in range(2):
                    expert(2 * i + (1 + n), (1 + n) % 2)
            expert(EX - 2, (EX - 2) % 2)
            expert(EX - 1, (EX - 1) % 2)

        def gates_turned(eng):
            for i in range(NT // U):
                if eng is nc.tensor:
                    if i == 0:
                        eng.wait_ge(me["h_ready"], HM * NG)
                        eng.wait_ge(me["gate_ready"], 1)
                    for u in range(U):
                        mm = nc.tensor.transpose(psum[0:EX, i, u * P:(u + 1) * P], me_gate[:, U * i + u, :], ident[:])
                    mm.then_inc(me["gT_done"], 1)
                elif eng is nc.scalar:
                    eng.wait_ge(me["gT_done"], i + 1)
                    nc.scalar.copy(me_gT[:, i * U * P:(i + 1) * U * P], psum[0:EX, i, :]).then_inc(me["gT_ready"], 1)

        def moe_tensor(pe):
            pairs = lambda vh, vl, wh, wl: ((vh, wh), (vh, wl), (vl, wh))

            def expert(e, par):
                wh, wl = me_wh[par], me_wl[par]
                last = isinstance(e, int) and e == EX - 1
                if not isinstance(e, int):
                    pe.wait_ge(me["gT_ready"], NT // U)
                pe.wait_ge(me["w1_split"], e + 1)
                for gr in range(NG):
                    done = NG * e + gr
                    toks = slice(gr * 512, (gr + 1) * 512)
                    for m in range(HM):
                        n = 0
                        for k in range(KC):
                            cols = slice(k * 512 + m * P, k * 512 + (m + 1) * P)
                            for w, v in pairs(wh[:, 0, cols], wl[:, 0, cols], me_xh[:, k, toks], me_xl[:, k, toks]):
                                mm = nc.tensor.matmul(psum[:, m, :], w, v, start=(n == 0), stop=(n == 5))
                                n += 1
                        mm.then_inc(me["up_done"], 1)
                    if gr == 0:
                        pe.wait_ge(me["w2_split"], 1 + e + 1)
                    if not isinstance(e, int) or done >= 2:
                        pe.wait_ge(me["acc_ready"], TG * (done - 1))
                    for m in range(HM):
                        pe.wait_ge(me["hl_ready"], HM * done + m + 1)
                        w2 = slice(m * D, (m + 1) * D)
                        for tau in range(TG):
                            rows = slice(tau * P, (tau + 1) * P)
                            if last and m == 0:
                                t = TG * gr + tau
                                nc.tensor.matmul(down_psum(gr, tau), me_gT[:, t * P:(t + 1) * P], me_b2[:], start=(tau % 2 == 0),
                                                 stop=False, skip_group_check=True)
                            for n, (v, w) in enumerate(pairs(me_hh[:, m, rows], me_hl[:, m, rows], wh[:, 1, w2], wl[:, 1, w2])):
                                mm = nc.tensor.matmul(down_psum(gr, tau), v, w, start=(not last and m == 0 and n == 0 and tau % 2 == 0),
                                                      stop=(m == HM - 1 and n == 2), skip_group_check=True)
                    mm.then_inc(me["down_done"], 1)

            moe_experts(pe, expert)

        def moe_scalar(act):
            nc.scalar.preload_act_table(ACT.Gelu)

            def expert(e, par):
                for gr in range(NG):
                    for m in range(HM):
                        n = HM * (NG * e + gr) + m + 1
                        hold(act, me["up_done"], 1 + n)
                        bias = me_b1[:, e, m:m + 1] if isinstance(e, int) else me_b1[:, bass.ds(e, 1), m:m + 1].rearrange("p e m -> p (e m)")
                        nc.scalar.activation(me_h[:, m, :], psum[:, m, :], ACT.Gelu, bias=bias).then_inc(me["h_ready"], 1)

            moe_experts(act, expert)

        def moe_vector(dve):
            def expert(e, par):
                for gr in range(NG):
                    for m in range(HM):
                        n = HM * (NG * e + gr) + m + 1
                        dve.wait_ge(me["h_ready"], n)
                        split(dve, me_hh[:, m, :], me_hl[:, m, :], me_h[:, m, :], me["hh_ready"], n, me["hl_ready"])
                    dve.wait_ge(me["down_done"], 1 + NG * e + gr + 1)
                    for tau in range(TG):
                        t = TG * gr + tau
                        nc.vector.scalar_tensor_tensor(out=x[:, t, :], in0=down_psum(gr, tau), scalar=me_gate[:, t, bass.ds(e, 1)],
                                                       in1=x[:, t, :], op0=ALU.mult, op1=ALU.add).then_inc(me["acc_ready"], 1)
                    if gr == 1 and not (isinstance(e, int) and e == EX - 1):
                        moe_weights(dve, e + 1, 1 - par)

            moe_gates(dve)
            moe_experts(dve, expert)

        with Scratch() as scratch:
            for c in smalls:
                c.w_qkv = scratch(f"{c.name}_w_qkv", [P, KC, 3 * D])
                c.w_o = scratch(f"{c.name}_w_o", [P, KC, D])
                c.b_qk = scratch(f"{c.name}_b_qk", [P, 2 * D])
                c.b_v = scratch(f"{c.name}_b_v", [P, KC, P])
                c.b_o = scratch(f"{c.name}_b_o", [P, D])
            sm_xT = scratch("sm_xT", [P, U, KC, P])
            sm_cT = scratch("sm_cT", [P, U, KC, P])
            sm_qk = scratch("sm_qk", [P, U, 2, D])
            sm_cosd = scratch("sm_cosd", [P, 2, D])
            sm_sind = scratch("sm_sind", [P, 2, D])
            sm_vbd = scratch("sm_vbd", [P, U, G, BT, 64])
            sm_qbd = scratch("sm_qbd", [P, U, KC, BT, P])
            sm_kT = scratch("sm_kT", [P, U, KC, P])
            sm_p = scratch("sm_p", [P, U, BT * G, S])
            sm_max = scratch("sm_max", [P, U, BT * G])
            sm_sum = scratch("sm_sum", [P, U, BT * G])
            sm_rinv = scratch("sm_rinv", [P, U, BT * G])
            sm_pT = scratch("sm_pT", [P, U, G, P])
            sm_o = scratch("sm_o", [P, U, BT * G, DH])
            sm_oT = scratch("sm_oT", [P, U, KC, BT, S])
            f8_xn = scratch("f8_xn", [P, U, D])
            f8_magic = scratch("f8_magic", [P, U, D])
            f8_q = scratch("f8_q", [P, U, D], BF16)
            f8_qT = scratch("f8_qT", [P, U, KC, P], BF16)
            f8_amax = scratch("f8_amax", [P, U])
            f8_scale = scratch("f8_scale", [P, U])
            f8_inv = scratch("f8_inv", [P, U])
            f8_total = scratch("f8_total", [P, U])
            f8_int = scratch("f8_int", [P, KC * D], I32)
            f8_mag = scratch("f8_mag", [P, KC * D], I32)
            f8_high = scratch("f8_high", [P, KC * D])
            f8_byte = scratch("f8_byte", [P, KC * D], U8)
        with Scratch() as scratch:
            x1_xT = scratch("x1_xT", [P, KC, U * P])
            x1_qT = scratch("x1_qT", [P, G, NT * P])
            x1_mask = [scratch(f"x1_mask{n}", [S, BT, SP], BF16) for n in range(2)]
            x1_wks = [scratch(f"x1_wk{n}", [P, KC, D], F32R) for n in ("h", "l")]
            x1_wvs = [scratch(f"x1_wv{n}", [P, KC, D], F32R) for n in ("h", "l")]
            x1_cs = [[scratch(f"x1_ctx{par}{n}", [P, KC, BT * SP + BT * G], F32R) for n in ("h", "l")] for par in range(2)]
            x1_qhigh = scratch("x1_qhigh", [P, 2, G, 2 * S], F32R)
            x1_qlow = scratch("x1_qlow", [P, 2, G, 2 * S], F32R)
            x1_qh = scratch("x1_qh", [P, 2, G, 2, P], F32R)
            x1_ql = scratch("x1_ql", [P, 2, G, 2, P], F32R)
            x1_k = scratch("x1_k", [P, 2, G, SP], F32R)
            x1_v = scratch("x1_v", [P, 2, 2, D])
            x1_vls = scratch("x1_vls", [STACK, 2 * D], F32R)
            x1_vlbd = scratch("x1_vlbd", [STACK, 2, HJ, 64], F32R)
            x1_p = scratch("x1_p", [P, BT * G, SK])
            x1_nmax = scratch("x1_nmax", [P, BT * G])
            x1_sum = scratch("x1_sum", [P, BT * G])
            x1_rinv = scratch("x1_rinv", [P, BT * G])
            x1_void = scratch("x1_void", [P, BT * G])
            x1_pT = scratch("x1_pT", [P, 2, 2, P])
            x1_plT = scratch("x1_plT", [STACK, P], F32R)
            x1_o = scratch("x1_o", [P, BT * G, DH])
            x1_oT = scratch("x1_oT", [P, KC, BT, S])
        with Scratch() as scratch:
            mx_taps = scratch("mx_taps", [P, KC, 3, P])
            mx_xT = scratch("mx_xT", [P, 3, KC, U * P + 2])
            mx_h = scratch("mx_h", [GH, U * P])
            mx_gate = scratch("mx_gate", [R, U * P])
            mx_sum = scratch("mx_sum", [R, U * P])
            mx_gu = scratch("mx_gu", [R, U * P])
            mx_glob = scratch("mx_glob", [R, U * P])
        with Scratch() as scratch:
            me_xh = scratch("me_xh", [P, KC, NT * P], F32R)
            me_xl = scratch("me_xl", [P, KC, NT * P], F32R)
            me_wh = [scratch(f"me_wh{n}", [P, 2, 1024], F32R) for n in range(2)]
            me_wl = [scratch(f"me_wl{n}", [P, 2, 1024], F32R) for n in range(2)]
            me_h = scratch("me_h", [P, HM, 512])
            me_hh = scratch("me_hh", [P, HM, 512], F32R)
            me_hl = scratch("me_hl", [P, HM, 512], F32R)
            me_rwh = scratch("me_rwh", [P, KC, E], F32R)
            me_rwl = scratch("me_rwl", [P, KC, E], F32R)
            me_lT = scratch("me_lT", [E, NT * P])
            me_pr = scratch("me_pr", [P, NT, E])
            me_st = scratch("me_st", [P, NT])
            me_cmp = scratch("me_cmp", [P, NT, E, E])
            me_cmp2 = scratch("me_cmp2", [P, NT, E, E])
            me_rank = scratch("me_rank", [P, NT, E])
            me_gate = scratch("me_gate", [P, NT, EX])
            me_gT = scratch("me_gT", [EX, NT * P])

        block = ctx.enter_context(nc.Block())

        @block.sync
        def _(sp):
            for dst, src in ((ident, "ident"), (eps, "eps"), (head_scale, "head_scale"), (rope_cos, "rope_cos"),
                             (rope_sin, "rope_sin"), (causal, "causal"), (hide, "hide"),
                             (row_pick, "row_pick")):
                sp.dma_start(dst[:], a[src]).then_inc(consts_loaded, 16)
            sp.dma_start(f8_bits[:], a["ffn0_w"]).then_inc(f8["weights_loaded"], 16)
            sp.dma_start(f8_ws[:], a["ffn0_ws"]).then_inc(f8["weights_loaded"], 16)
            sp.dma_start(f8_bias[:], a["ffn0_bias"]).then_inc(f8["weights_loaded"], 16)
            sp.dma_start(x[:], x_tiles).then_inc(x_loaded, 16)
            for c in smalls:
                for w, dst in (("w_qkv", c.w_qkv), ("w_o", c.w_o), ("b_qk", c.b_qk), ("b_v", c.b_v), ("b_o", c.b_o)):
                    sp.dma_start(dst[:], a[f"{c.name}_{w}"]).then_inc(c.weights_loaded, 16)
                if c.cross:
                    for u in range(U):
                        sp.dma_start(sm_cT[:, u], a["ctx32"][u]).then_inc(c.ctx_loaded[u], 16)
                    with sp.Fori(1, NT // U) as i:
                        for u in range(U):
                            hold(sp, sm["v_done"], U * (i - 1) + u + 1)
                            sp.dma_start(sm_cT[:, u], a["ctx32"][U * i + u]).then_inc(c.ctx_loaded[u], 16)
            for dst, src in ((x1_wq, "wq"), (x1_wk, "wk"), (x1_wv, "wv"), (x1_wo, "wo"), (x1_bq, "bq"), (x1_bk, "bk"),
                             (x1_bv, "bv"), (x1_bo, "bo")):
                sp.dma_start(dst[:], a[f"xattn1_{src}"]).then_inc(x1["weights_loaded"], 16)
            for dst, src in ((mx_w1, "w1"), (mx_b1, "b1"), (mx_w2, "w2"), (mx_b2, "b2"), (mx_wu, "wu"), (mx_wv, "wv"),
                             (mx_conv, "conv"), (mx_wo, "wo"), (mx_bo, "bo"), (mx_keep, "keep")):
                sp.dma_start(dst[:], a[f"mix1_{src}"]).then_inc(mx["weights_loaded"], 16)
            for dst, src in ((me_b1, "b1"), (me_b2, "b2"), (me_rw, "rw"), (me_rb, "rb"), (me_before, "before")):
                sp.dma_start(dst[:], a[f"moe1_{src}"]).then_inc(me["weights_loaded"], 16)
            sp.dma_start(x1_ctx[:], a["ctx"][0]).then_inc(x1["ctx_loaded"], 16)
            sp.dma_start(x1_mask8[:], a["mask"][0]).then_inc(x1["mask_loaded"], 16)
            with sp.Fori(1, NT) as t:
                hold(sp, x1["ctx_split"], t)
                sp.dma_start(x1_ctx[:], a["ctx"][t]).then_inc(x1["ctx_loaded"], 16)
                hold(sp, x1["mask_ready"], 1 + t)
                sp.dma_start(x1_mask8[:], a["mask"][t]).then_inc(x1["mask_loaded"], 16)
            with sp.Fori(0, EX) as e:
                hold(sp, me["w2_split"], 1 + e)
                sp.dma_start(me_raw[:], a["moe1_w"][e]).then_inc(me["raw_loaded"], 16)
            for gr in range(NG):
                sp.wait_ge(me["acc_ready"], TG * (NG * (EX - 1) + gr + 1))
                sp.dma_start(out_tiles[:, TG * gr:TG * (gr + 1), :], x[:, TG * gr:TG * (gr + 1), :]).then_inc(me["stored"], 16)
            sp.wait_ge(me["stored"], 16 * NG)

        @block.tensor
        def _(pe):
            for s in (x1["xT_done"], me["lT_ready"], me["up_done"], me["down_done"]):
                pe.sem_inc(s, 1)
            pe.wait_ge(consts_loaded, 16 * 8)
            pe.wait_ge(consts_cast, 3)
            small_tensor(pe, small["xattn0"])
            small_tensor(pe, small["attn0"])
            ffn_tensor(pe)
            x1q_tensor(pe)
            x1_tensor(pe)
            mix_tensor(pe)
            moe_prep_tensor(pe)
            moe_tensor(pe)

        @block.scalar
        def _(act):
            act.wait_ge(consts_loaded, 16 * 8)
            small_scalar(act, small["xattn0"])
            small_scalar(act, small["attn0"])
            ffn_scalar(act)
            x1q_scalar(act)
            x1_scalar(act)
            mix_scalar(act)
            moe_prep_scalar(act)
            moe_scalar(act)

        @block.vector
        def _(dve):
            for s in (x_stats, sm["stats_ready"], f8["stats_ready"], mx["stats_ready"], me["w2_split"]):
                dve.sem_inc(s, 1)
            dve.wait_ge(consts_loaded, 16 * 8)
            ffn_weights(dve)
            dve.wait_ge(x_loaded, 16)
            with dve.Fori(0, NT) as t:
                nc.vector.bn_stats(bn_out[:, t, :], x[:, t, :]).then_inc(x_stats, 1)
            dve.wait_ge(x_stats, 1 + NT)
            dve_variance(dve)
            small_vector(dve, small["xattn0"])
            dve_variance(dve)
            small_vector(dve, small["attn0"])
            dve_variance(dve)
            ffn_vector(dve)
            dve_variance(dve)
            x1q_vector(dve)
            x1_vector(dve)
            dve_variance(dve)
            mix_vector(dve)
            dve_variance(dve)
            moe_prep_vector(dve)
            moe_vector(dve)

        @block.gpsimd
        def _(pool):
            pool.sem_inc(x1["mask_ready"], 1)
            nc.gpsimd.memset(sm_vbd[:], 0.0).then_inc(sm_zeroed, 1)
            pool.wait_ge(consts_loaded, 16 * 8)
            nc.gpsimd.tensor_copy(ident_b[:], ident[:]).then_inc(consts_cast, 1)
            nc.gpsimd.tensor_copy(causal_b[:], causal[:]).then_inc(consts_cast, 1)
            nc.gpsimd.tensor_copy(hide_b[:], hide[:]).then_inc(consts_cast, 1)
            for c in smalls:
                pool_bias(pool, sm["norm_ready"], sm["x_biased"], c.bias_ready, c.b_o[:], c.before)
            pool_bias(pool, f8["norm_ready"], f8["x_biased"], f8["w_ready"], f8_bias[:])
            x1_pool_weights(pool)
            pool_bias(pool, x1["norm_ready"], x1["x_biased"], x1["bias_ready"], x1_bo[:])
            x1_pool(pool)
            pool_bias(pool, mx["norm_ready"], mx["x_biased"], mx["taps_ready"], mx_bo[:])


def layout(inputs):
    f = {k: np.asarray(v) for k, v in inputs.items()}
    out = {}
    rows = lambda w: np.ascontiguousarray(w.reshape(KC, P, -1).transpose(1, 0, 2))
    wide = lambda v: np.ascontiguousarray(np.broadcast_to(v.reshape(1, -1), (P, v.size)))
    heads = lambda w, order=range(G): np.ascontiguousarray(
        w.reshape(G, 2, 2, DH, -1)[list(order)].transpose(2, 0, 3, 1, 4).reshape(P, KC, -1))
    parity = [g for r in range(2) for g in range(r, G, 2)]
    half = np.array([h * DH + d for h in range(H) for d in list(range(0, DH, 2)) + list(range(1, DH, 2))])

    out["x"] = f["x"].reshape(B * S, D)
    ctx = f["ctx_1024"].reshape(NT, BT, SK, KC, P).transpose(0, 4, 3, 1, 2)
    pairs = np.concatenate([ctx, ctx[..., 2 * SK - SP:SK]], axis=-1)
    last = np.repeat(ctx[..., SK - 1], G, axis=-1)
    out["ctx"] = np.concatenate([pairs.reshape(NT, P, KC, BT * SP), last], axis=-1)
    out["ctx32"] = np.ascontiguousarray(
        ctx[..., :S].reshape(NT, P, KC, BT * S))
    out["mask"] = np.ascontiguousarray(f["mask_Bx1xSxS2_bf0"].reshape(NT, BT, S, SK).transpose(0, 2, 1, 3))

    for name, q, k, v, o, perm in (
            ("xattn0", "L0_xattn_q", "L0_xattn_k", "L0_xattn_v", "L0_xattn_o", slice(None)),
            ("attn0", "q", "k", "v", "o", half)):
        if name == "xattn0":
            w = [f[f"{n}_w"].T for n in (q, k, v, o)]
            b = [f[f"{n}_b"] for n in (q, k, v, o)]
        else:
            w = [f[f"L0_attn_W{n}"] for n in (q, k, v, o)]
            b = [f[f"L0_attn_b{n}"] for n in (q, k, v, o)]
        out[f"{name}_w_qkv"] = rows(np.concatenate([w[0][:, perm], w[1][:, perm], w[2]], axis=1))
        out[f"{name}_w_o"] = heads(w[3], parity)
        out[f"{name}_b_qk"] = wide(np.concatenate([b[0][perm], b[1][perm]]))
        out[f"{name}_b_v"] = np.ascontiguousarray(np.broadcast_to(heads(b[2], parity), (P, KC, P)))
        out[f"{name}_b_o"] = wide(b[3])

    out["ffn0_w"] = rows(f["L0_ffn_weight"].view(np.uint8).T).reshape(P, KC * D)
    out["ffn0_ws"] = np.ascontiguousarray(np.broadcast_to(f["L0_ffn_weight_scale"].reshape(1, 1), (P, 1)))
    out["ffn0_bias"] = wide(f["L0_ffn_bias"])

    for n in "qkv":
        out[f"xattn1_w{n}"] = rows(f[f"L1_xattn_w_{n}"].T)
    out["xattn1_wo"] = heads(f["L1_xattn_w_o"].T)
    out["xattn1_bq"] = np.ascontiguousarray(f["L1_xattn_b_q"].reshape(KC, P).T)
    out["xattn1_bk"] = np.ascontiguousarray(f["L1_xattn_b_k"].reshape(KC, P).T)
    out["xattn1_bv"] = np.ascontiguousarray(np.broadcast_to(heads(f["L1_xattn_b_v"]), (P, KC, P)))
    out["xattn1_bo"] = wide(f["L1_xattn_b_o"])

    out["mix1_w1"] = rows(f["L1_attn_gate_w1"])
    out["mix1_b1"] = f["L1_attn_gate_b1"].reshape(GH, 1)
    out["mix1_w2"] = f["L1_attn_gate_w2"]
    out["mix1_b2"] = f["L1_attn_gate_b2"].reshape(R, 1)
    out["mix1_wu"] = rows(f["L1_attn_U_w"])
    out["mix1_wv"] = rows(f["L1_attn_V_w"])
    out["mix1_conv"] = rows(f["L1_attn_conv_w"])
    out["mix1_wo"] = f["L1_attn_out_w"]
    out["mix1_bo"] = wide(f["L1_attn_out_b"])

    w1 = np.concatenate([f["L1_ffn_rw1"], f["L1_ffn_sw1"][None]])
    w2 = np.concatenate([f["L1_ffn_rw2"], f["L1_ffn_sw2"][None]])
    w1 = w1.reshape(EX, KC, P, HID).transpose(0, 2, 1, 3).reshape(EX, P, 1, KC * HID)
    w2 = w2.reshape(EX, HM, P, D).transpose(0, 2, 1, 3).reshape(EX, P, 1, HM * D)
    out["moe1_w"] = np.ascontiguousarray(np.concatenate([w1, w2], axis=2))
    b1 = np.concatenate([f["L1_ffn_rb1"], f["L1_ffn_sb1"][None]])
    out["moe1_b1"] = np.ascontiguousarray(b1.reshape(EX, HM, P).transpose(2, 0, 1))
    out["moe1_b2"] = np.concatenate([f["L1_ffn_rb2"], f["L1_ffn_sb2"][None]])
    out["moe1_rw"] = rows(f["L1_ffn_router_w"])
    out["moe1_rb"] = wide(f["L1_ffn_router_b"])

    p = np.arange(P)
    out["ident"] = np.eye(P, dtype=np.float32)
    out["eps"] = np.full((P, 1), EPS, np.float32)
    out["head_scale"] = (((p[:, None] // DH) % L == np.arange(L)[None]) * DH ** -0.5).astype(np.float32)
    freqs = 1.0 / 10000.0 ** (np.arange(DH // 2) / (DH // 2))
    ang = (p % S)[:, None] * freqs[None]
    out["rope_cos"] = np.concatenate([np.cos(ang), np.cos(ang)], 1).astype(np.float32)
    out["rope_sin"] = np.concatenate([-np.sin(ang), np.sin(ang)], 1).astype(np.float32)
    out["causal"] = np.where(np.arange(S)[None] > (p % S)[:, None], CAUSAL, 0.0).astype(np.float32)
    q = np.arange(S)
    out["hide"] = np.where(q[:, None, None] == q[None, None, :], MASKED, 0.0).repeat(L, 1).astype(np.float32)
    out["row_pick"] = np.zeros((2 * 32 + 2 * G, 2 * G), np.float32)
    for row in range(3):
        out["row_pick"][32 * row:32 * row + 2 * G] = np.eye(2 * G)
    out["mix1_keep"] = np.ascontiguousarray(np.broadcast_to((np.arange(U * P) % S != 0).astype(np.float32), (R, U * P)))
    e = np.arange(E)
    out["moe1_before"] = np.ascontiguousarray(np.broadcast_to((e[None] < e[:, None]).astype(np.float32), (P, E, E)))
    return {k: np.ascontiguousarray(v) for k, v in out.items()}


def kernel(**inputs):
    import concourse.bacc as bacc
    from concourse.bass_utils import run_bass_kernel_spmd

    arrays = layout(inputs)
    nc = bacc.Bacc("TRN2", target_bir_lowering=False, num_devices=1)
    args = {}
    for name, v in arrays.items():
        args[name] = nc.dram_tensor(f"in_{name}", v.shape, mybir.dt.from_np(v.dtype), kind="ExternalInput").ap()
    args["out"] = nc.dram_tensor("out_x", (B * S, D), F32, kind="ExternalOutput").ap()
    build(nc, args)
    r = run_bass_kernel_spmd(nc, [{f"in_{k}": v for k, v in arrays.items()}], core_ids=[0])
    return r.results[0]["out_x"].reshape(B, S, D)
```

```python
from contextlib import ExitStack

import numpy as np

import concourse.bass as bass
from concourse import mybir

F32 = mybir.dt.float32
F32R = mybir.dt.float32r
BF16 = mybir.dt.bfloat16
I32 = mybir.dt.int32
U8 = mybir.dt.uint8
FP8 = mybir.dt.float8e4
ALU = mybir.AluOpType
ACT = mybir.ActivationFunctionType
AX = mybir.AxisListType

B, S, D = 64, 32, 256
SK = 257
SP = SK + SK % 2
P = 128
NT = B * S // P
BT = P // S
H, DH = 16, 16
G = H // BT
L = BT
LAST = 32 + 2 * G
KC = D // P
U = 4
R, GH = 32, 64
E, HID = 8, 512
EX = E + 1
HM = HID // P
TG = 4
EPS = 1e-5
MASKED = -1e30
CAUSAL = -1e9


def build(nc, a):
    with ExitStack() as ctx:

        def sb(name, shape, dt=F32):
            return ctx.enter_context(nc.sbuf_tensor(name, shape, dt))

        def sem(name):
            return ctx.enter_context(nc.semaphore(name))

        class Scratch(ExitStack):
            def __call__(self, name, shape, dt=F32):
                return self.enter_context(nc.sbuf_tensor(name, shape, dt))

        psum = ctx.enter_context(nc.psum_tensor("psum", [P, 8, 512], F32))

        x = sb("x", [P, NT, D])
        ln_mv = sb("ln_mv", [P, NT, 2])
        ln_rstd = sb("ln_rstd", [P, NT])
        ln_tmp = sb("ln_tmp", [P, 2, NT])
        ident = sb("ident", [P, P])
        eps = sb("eps", [P, 1])
        head_scale = sb("head_scale", [P, L])
        bn_out = sb("bn_out", [P, NT, 6])

        x_loaded = [sem(f"x_loaded{i}") for i in range(NT // U)]
        consts_loaded = sem("consts_loaded")
        consts_cast = sem("consts_cast")
        x_tiles = a["x"].rearrange("(t p) c -> p t c", p=P)
        out_tiles = a["out"].rearrange("(t p) c -> p t c", p=P)
        x_stats = sem("x_stats")
        chain = sem("chain")
        chained = [0]

        passed = {}

        def hold(eng, semaphore, count):
            if eng not in passed:
                passed[eng] = sem(f"passed_{len(passed)}")
            eng.wait_ge(semaphore, count)
            eng.sem_inc(passed[eng], 1)

        def link(dve, ins, n=1):
            ins.then_inc(chain, 1)
            chained[0] += 1
            dve.wait_ge(chain, chained[0])

        layers = ["xattn0", "attn0", "ffn0", "xattn1", "mix1", "moe1"]
        var_ready, sqrt_ready, rstd_ready = sem("var_ready"), sem("sqrt_ready"), sem("rstd_ready")

        def dve_variance(dve):
            mean, var, tmp = ln_mv[:, :, 0], ln_mv[:, :, 1], ln_tmp[:, 0, :]
            link(dve, nc.vector.tensor_tensor(tmp, bn_out[:, :, 1], bn_out[:, :, 4], ALU.subtract))
            link(dve, nc.vector.tensor_tensor(mean, bn_out[:, :, 1], bn_out[:, :, 4], ALU.add))
            link(dve, nc.vector.tensor_scalar(mean, mean, 0.5, None, ALU.mult))
            link(dve, nc.vector.scalar_tensor_tensor(out=tmp, in0=tmp, scalar=0.25, in1=tmp, op0=ALU.mult, op1=ALU.mult))
            link(dve, nc.vector.tensor_tensor(var, bn_out[:, :, 2], bn_out[:, :, 5], ALU.add))
            nc.vector.scalar_tensor_tensor(out=var, in0=var, scalar=1.0 / D, in1=tmp, op0=ALU.mult,
                                           op1=ALU.add).then_inc(var_ready, 1)

        def act_sqrt(act, n):
            nc.scalar.preload_act_table(ACT.Sqrt)
            act.wait_ge(var_ready, layers.index(n) + 1)
            nc.scalar.activation(ln_tmp[:, 0, :], ln_mv[:, :, 1], ACT.Sqrt, bias=eps[:, 0:1]).then_inc(sqrt_ready, 1)

        def dve_rstd(dve, n):
            dve.wait_ge(sqrt_ready, layers.index(n) + 1)
            r, s = ln_rstd[:, :], ln_tmp[:, 1, :]
            link(dve, nc.vector.reciprocal(r, ln_tmp[:, 0, :]))
            link(dve, nc.vector.scalar_tensor_tensor(out=s, in0=ln_mv[:, :, 1], scalar=eps[:, 0:1], in1=r,
                                                     op0=ALU.add, op1=ALU.mult))
            link(dve, nc.vector.tensor_tensor(s, s, r, ALU.mult))
            link(dve, nc.vector.tensor_scalar(s, s, -0.5, 1.5, ALU.mult, ALU.add))
            ins = nc.vector.tensor_tensor(r, r, s, ALU.mult)
            ins.then_inc(rstd_ready, 1)
            dve.wait_ge(rstd_ready, layers.index(n) + 1)

        def dve_normalise(t, out):
            return nc.vector.tensor_scalar(out, x[:, t, :], ln_mv[:, t, 0:1], ln_rstd[:, bass.ds(t, 1)],
                                           ALU.subtract, ALU.mult)

        class Small:

            def __init__(self, name, cross):
                self.name, self.cross = name, cross

        sm_xn = sb("sm_xn", [P, U, D])
        rope_cos = sb("rope_cos", [P, DH])
        rope_sin = sb("rope_sin", [P, DH])
        ident_b = sb("ident_b", [P, P], BF16)
        causal = sb("causal", [P, S])
        causal_b = sb("causal_b", [P, S], BF16)

        sm = {s: sem(f"small_{s}") for s in (
            "norm_ready", "xT_done", "xT_ready", "biased", "qk_done", "v_done", "v_ready", "rope_parts", "rope_ready", "qkT_done",
            "qbd_ready", "kT_ready", "scores_done", "max_ready", "shifted", "exp_ready", "sum_ready", "rinv_ready", "pT_done",
            "pT_ready", "pv_done", "heads_ready", "oT_done", "oT_ready", "out_done", "x_biased", "x_updated", "stats_ready")}
        smalls = []
        for name, cross in (("xattn0", True), ("attn0", False)):
            c = Small(name, cross)
            c.before = len(smalls) * NT
            c.weights_loaded, c.bias_product = sem(f"{name}_weights_loaded"), sem(f"{name}_bias_product")
            c.bias_ready = sem(f"{name}_bias_ready")
            c.ctx_loaded = [sem(f"{name}_ctx_loaded{u}") for u in range(U if cross else 0)]
            smalls.append(c)
        small = {c.name: c for c in smalls}
        sm_zeroed = sem("small_zeroed")

        def bank(u, k):
            return psum[:, 2 * u + k, :]

        def steps(eng, step):
            for s in range(U):
                step(lambda d: (s - d, (s - d) % U), lambda d: s - d >= 0)
            with eng.Fori(1, NT // U) as i:
                for u in range(U):
                    step(lambda d: (U * i + u - d, (u - d) % U), lambda d: True)
            for s in range(NT, NT + U):
                step(lambda d: (s - d, (s - d) % U), lambda d: s - d < NT)

        def small_tensor(pe, c):
            pe.wait_ge(c.weights_loaded, 16 * 5)
            for k in range(KC):
                mm = nc.tensor.matmul(bank(0, 0)[:, 0:D], c.b_v[:, k, :], c.w_o[:, k, :], start=(k == 0), stop=(k == KC - 1))
            mm.then_inc(c.bias_product, 1)
            pe.wait_ge(c.bias_ready, 1)
            first = c.before
            kv = sm_cT if c.cross else sm_xT

            def scores(u, r):
                nc.tensor.matmul(bank(u, r)[:, 0:D], ident_b[:], causal_b[:].unsqueeze(1).broadcast_to([P, D // S, S]),
                                 start=True, stop=False, skip_group_check=True)
                for k in range(KC):
                    for b in range(BT):
                        j = k * BT + b
                        mm = nc.tensor.matmul(bank(u, r)[:, j * S:(j + 1) * S], sm_qbd[64 * r:64 * r + 64, u, k, b, :],
                                              sm_kT[64 * r:64 * r + 64, u, k, b * S:(b + 1) * S],
                                              start=False, stop=(j == KC * BT - 1), skip_group_check=True)
                return mm

            def step(n, live):
                if live(4):
                    t, u = n(4)
                    pe.wait_ge(sm["heads_ready"], first + t + 1)
                    for k in range(BT // 2):
                        mm = nc.tensor.transpose(bank(u, 0)[:, k * P:(k + 1) * P],
                                                 sm_o[:, u, k * 2 * G:(k + 1) * 2 * G, :].rearrange("p j d -> p (j d)"), ident[:])
                    mm.then_inc(sm["oT_done"], 1)
                if live(2):
                    t, u = n(2)
                    pe.wait_ge(sm["rope_ready"], first + t + 1)
                    pe.wait_ge(sm["v_ready"], first + t + 1)
                    for s in range(2):
                        for k in range(KC):
                            mm = nc.tensor.transpose(bank(u, 1 - s)[:, k * P:(k + 1) * P],
                                                     sm_qk[:, u, s, k * P:(k + 1) * P], ident[:])
                    mm.then_inc(sm["qkT_done"], 1)
                if live(1):
                    t, u = n(1)
                    pe.wait_ge(sm["xT_ready"], first + t + 1)
                    if not (isinstance(t, int) and t < U):
                        pe.wait_ge(sm["x_updated"], first + t - U + 1)
                    if c.cross:
                        pe.wait_ge(c.ctx_loaded[u], 16 // U * (t - u) + 16)
                    for s in range(2):
                        for k in range(KC):
                            mm = nc.tensor.matmul(bank(u, 1)[:, s * D:(s + 1) * D], (kv if s else sm_xT)[:, u, k, :],
                                                  c.w_qkv[:, k, s * D:(s + 1) * D],
                                                  start=(k == 0), stop=(k == KC - 1), skip_group_check=True)
                    mm.then_inc(sm["qk_done"], 1)
                if live(1):
                    t, u = n(1)
                    for k in range(KC):
                        mm = nc.tensor.matmul(bank(u, 0)[:, 0:D], kv[:, u, k, :], c.w_qkv[:, k, 2 * D:3 * D],
                                              start=(k == 0), stop=(k == KC - 1))
                    mm.then_inc(sm["v_done"], 1)
                if live(3):
                    t, u = n(3)
                    pe.wait_ge(sm["exp_ready"], first + t + 1)
                    for g in range(G):
                        v = sm_p[:, u, g * BT:(g + 1) * BT, :].rearrange("p b s -> p (b s)")
                        mm = nc.tensor.transpose(bank(u, 1)[:, g * P:(g + 1) * P], v, ident[:])
                    mm.then_inc(sm["pT_done"], 1)
                if live(2):
                    t, u = n(2)
                    pe.wait_ge(sm["kT_ready"], first + t + 1)
                    pe.wait_ge(sm["qbd_ready"], first + t + 1)
                    scores(u, 0)
                if live(4):
                    t, u = n(4)
                    pe.wait_ge(sm["oT_ready"], first + t + 1)
                    for k in range(KC):
                        mm = nc.tensor.matmul(bank(u, 1)[:, 0:D], sm_oT[:, u, k, :, :].rearrange("p b s -> p (b s)"), c.w_o[:, k, :],
                                              start=(k == 0), stop=(k == KC - 1))
                    mm.then_inc(sm["out_done"], 1)
                if live(3):
                    t, u = n(3)
                    pe.wait_ge(sm["pT_ready"], first + t + 1)
                    for gp in range(G):
                        g = gp // 2 + 2 * (gp % 2)
                        mm = nc.tensor.matmul(bank(u, gp // 2)[:, (gp % 2) * D:(gp % 2 + 1) * D], sm_pT[:, u, gp, :],
                                              sm_vbd[:, u, g, :, :], start=True, stop=True, skip_group_check=True)
                    mm.then_inc(sm["pv_done"], 1)
                if live(0):
                    t, u = n(0)
                    pe.wait_ge(sm["norm_ready"], first + t + 1)
                    for k in range(KC):
                        mm = nc.tensor.transpose(bank(u, 0)[:, k * P:(k + 1) * P], sm_xn[:, u, k * P:(k + 1) * P], ident[:])
                    mm.then_inc(sm["xT_done"], 1)
                if live(2):
                    t, u = n(2)
                    mm = scores(u, 1)
                    mm.then_inc(sm["scores_done"], 1)

            steps(pe, step)

        def small_scalar(act, c):
            act.wait_ge(sm_zeroed, 1)
            act_sqrt(act, c.name)
            nc.scalar.preload_act_table(ACT.Exp)
            first = c.before

            def step(n, live):
                if live(4):
                    t, u = n(4)
                    act.wait_ge(sm["oT_done"], first + t + 1)
                    spread_heads(nc.scalar.copy, bank(u, 0), sm_oT[:, u, :, :, :]).then_inc(sm["oT_ready"], 1)
                if live(2):
                    t, u = n(2)
                    act.wait_ge(sm["qkT_done"], first + t + 1)
                    nc.scalar.activation(sm_kT[:, u, :, :].rearrange("p k s -> p (k s)"), bank(u, 0)[:, 0:D],
                                         ACT.Copy).then_inc(sm["kT_ready"], 1)
                if live(3):
                    t, u = n(3)
                    act.wait_ge(sm["pT_done"], first + t + 1)
                    nc.scalar.activation(sm_pT[:, u, :, :].rearrange("p g s -> p (g s)"), bank(u, 1), ACT.Copy).then_inc(sm["pT_ready"], 1)
                if live(1):
                    t, u = n(1)
                    act.wait_ge(sm["v_done"], first + t + 1)
                    for b in range(BT):
                        rows = slice(b * S, (b + 1) * S)
                        ins = nc.scalar.copy(sm_vbd[rows, u, :, b, :], bank(u, 0)[rows, 0:D].rearrange("p (g c) -> p g c", g=G))
                    ins.then_inc(sm["v_ready"], 1)
                if live(0):
                    t, u = n(0)
                    act.wait_ge(sm["xT_done"], first + t + 1)
                    nc.scalar.activation(sm_xT[:, u, :, :].rearrange("p k s -> p (k s)"), bank(u, 0)[:, 0:D],
                                         ACT.Copy).then_inc(sm["xT_ready"], 1)
                if live(2):
                    t, u = n(2)
                    act.wait_ge(sm["shifted"], first + t + 1)
                    v = sm_p[:, u, :, :].rearrange("p j s -> p (j s)")
                    nc.scalar.activation(v, v, ACT.Exp).then_inc(sm["exp_ready"], 1)

            steps(act, step)

        def spread_heads(copy, src, dst):
            for r in range(2):
                for rb in range(2):
                    v = src[64 * rb:64 * rb + 64, 0:D].rearrange("p (bb j r q) -> p r bb j q", bb=BT // 2, j=L // 2, r=2)[:, r]
                    w = dst[64 * r:64 * r + 64].rearrange("p j (bb rb) q -> p rb bb j q", rb=2)[:, rb]
                    ins = copy(w, v)
            return ins

        def small_vector(dve, c):
            dve.wait_ge(c.weights_loaded, 16 * 5)
            dve.wait_ge(c.bias_product, 1)
            nc.vector.tensor_tensor(c.b_o[:], bank(0, 0)[:, 0:D], c.b_o[:], ALU.add).then_inc(c.bias_ready, 1)
            dve_rstd(dve, c.name)
            first = c.before

            def step(n, live):
                if live(0):
                    t, u = n(0)
                    dve_normalise(t, sm_xn[:, u, :]).then_inc(sm["norm_ready"], 1)
                if live(2):
                    t, u = n(2)
                    dve.wait_ge(sm["qkT_done"], first + t + 1)
                    for k in range(KC):
                        ins = spread_queries(nc.vector, sm_qbd[:, u, k, :, :], bank(u, 1)[:, k * P:(k + 1) * P])
                    ins.then_inc(sm["qbd_ready"], 1)
                if live(3):
                    t, u = n(3)
                    dve.wait_ge(sm["exp_ready"], first + t + 1)
                    nc.vector.tensor_reduce(sm_sum[:, u, :], sm_p[:, u, :, :], AX.X, ALU.add).then_inc(sm["sum_ready"], 1)
                    dve.wait_ge(sm["sum_ready"], first + t + 1)
                    nc.vector.reciprocal(sm_rinv[:, u, :], sm_sum[:, u, :]).then_inc(sm["rinv_ready"], 1)
                if live(1):
                    t, u = n(1)
                    dve.wait_ge(sm["qk_done"], first + t + 1)
                    qk = sm_qk[:, u, :, :].rearrange("p s c -> p (s c)")
                    nc.vector.tensor_tensor(qk, bank(u, 1), c.b_qk[:], ALU.add).then_inc(sm["biased"], 1)
                    dve.wait_ge(sm["biased"], first + t + 1)
                    qk3 = sm_qk[:, u, :, :].rearrange("p s (h d) -> p (s h) d", d=DH)
                    cs3 = sm_cosd[:].rearrange("p s (h d) -> p (s h) d", d=DH)
                    sn3 = sm_sind[:].rearrange("p s (h d) -> p (s h) d", d=DH)
                    wide = [P, 2 * H, DH]
                    half = [P, 2 * H, DH // 2]
                    nc.vector.tensor_tensor(cs3, qk3, rope_cos[:].unsqueeze(1).broadcast_to(wide), ALU.mult).then_inc(sm["rope_parts"], 1)
                    nc.vector.tensor_tensor(sn3[:, :, 0:8], qk3[:, :, 8:16],
                                            rope_sin[:, 0:8].unsqueeze(1).broadcast_to(half), ALU.mult).then_inc(sm["rope_parts"], 1)
                    nc.vector.tensor_tensor(sn3[:, :, 8:16], qk3[:, :, 0:8],
                                            rope_sin[:, 8:16].unsqueeze(1).broadcast_to(half), ALU.mult).then_inc(sm["rope_parts"], 1)
                    dve.wait_ge(sm["rope_parts"], 3 * (first + t + 1))
                    nc.vector.tensor_tensor(qk, cs3, sn3, ALU.add).then_inc(sm["rope_ready"], 1)
                if live(4):
                    t, u = n(4)
                    dve.wait_ge(sm["out_done"], first + t + 1)
                    dve.wait_ge(sm["x_biased"], first + t + 1)
                    nc.vector.tensor_tensor(x[:, t, :], bank(u, 1)[:, 0:D], x[:, t, :], ALU.add).then_inc(sm["x_updated"], 1)
                if live(4):
                    t, u = n(4)
                    row_stats(dve, t, sm["x_updated"], first + t + 1, sm["stats_ready"])
                if live(3):
                    t, u = n(3)
                    dve.wait_ge(sm["rinv_ready"], first + t + 1)
                    dve.wait_ge(sm["pv_done"], first + t + 1)
                    pick_heads(psum[:, 2 * u:2 * u + 2, :], sm_rinv[:, u, :],
                               sm_o[:, u, :, :].rearrange("p (b g) d -> p g b d", b=BT)).then_inc(sm["heads_ready"], 1)
                if live(2):
                    t, u = n(2)
                    dve.wait_ge(sm["scores_done"], first + t + 1)
                    sc = psum[:, 2 * u:2 * u + 2, 0:D].rearrange("p r (j s) -> p r j s", s=S)
                    top = sm_max[:, u, :].rearrange("p (r j) -> p r j", r=2)
                    nc.vector.tensor_reduce(top, sc, AX.X, ALU.max).then_inc(sm["max_ready"], 1)
                    dve.wait_ge(sm["max_ready"], first + t + 1)
                    nc.vector.tensor_tensor(sm_p[:, u, :, :].rearrange("p (r j) s -> p r j s", r=2), sc,
                                            top.unsqueeze(3).broadcast_to([P, 2, BT * G // 2, S]),
                                            ALU.subtract).then_inc(sm["shifted"], 1)

            steps(dve, step)
            dve.wait_ge(sm["stats_ready"], 1 + first + NT)

        def spread_queries(eng, dst, src):
            return eng.tensor_tensor(
                dst.rearrange("p b (l q) -> p b l q", l=L),
                src.rearrange("p (b q) -> p b q", b=BT).unsqueeze(2).broadcast_to([P, BT, L, S]),
                head_scale[:].unsqueeze(1).unsqueeze(3).broadcast_to([P, BT, L, S]), ALU.mult)

        def pick_heads(src, rinv, dst):
            for l in range(L):
                q = slice(S * l, S * l + S)
                v = src[q].rearrange("p k (j l d) -> p l (k j) d", l=L, d=DH)[:, l]
                r = rinv[q].unsqueeze(2).broadcast_to([S, rinv.shape[1], DH])
                o = dst[q]
                if len(o.shape) == 4:
                    v, r = (z.rearrange("p (g b) d -> p g b d", g=G) for z in (v, r))
                ins = nc.vector.tensor_tensor(o, v, r, ALU.mult)
            return ins

        def row_stats(dve, t, updated, count, stats):
            hold(dve, updated, count)
            nc.vector.bn_stats(bn_out[:, t, :], x[:, t, :]).then_inc(stats, 1)

        def pool_bias(pool, norm_ready, x_biased, bias_ready, b_o, before=0):
            pool.wait_ge(bias_ready, 1)
            with pool.Fori(0, NT) as t:
                pool.wait_ge(norm_ready, before + t + 1)
                nc.gpsimd.tensor_tensor(x[:, t, :], x[:, t, :], b_o, ALU.add).then_inc(x_biased, 1)

        f8_bias = sb("f8_bias", [P, D])
        f8_ws = sb("f8_ws", [P, 1])
        f8_bits = sb("f8_bits", [P, KC * D], U8)
        f8_w = sb("f8_w", [P, KC, D], BF16)
        f8 = {s: sem(f"ffn0_{s}") for s in (
            "weights_loaded", "w_ready", "shift_ready", "norm_ready", "amax_ready", "scale_ready", "inv_ready", "scaled", "exponent_ready",
            "magic_ready", "added", "q_ready", "total_ready", "qT_done", "qT_ready", "out_done", "x_biased", "x_updated",
            "stats_ready")}

        ROUNDS = NT // U

        def ffn_weights(dve):
            dve.wait_ge(f8["weights_loaded"], 16 * 3)
            link(dve, nc.vector.tensor_copy(f8_int[:], f8_bits[:]))
            link(dve, nc.vector.tensor_scalar(f8_mag[:], f8_int[:], 127, None, ALU.bitwise_and))
            link(dve, nc.vector.tensor_scalar(f8_high[:], f8_mag[:], 120.0, None, ALU.is_ge))
            link(dve, nc.vector.scalar_tensor_tensor(out=f8_byte[:], in0=f8_high[:], scalar=-8.0, in1=f8_int[:],
                                                     op0=ALU.mult, op1=ALU.add))
            nc.vector.scalar_tensor_tensor(out=f8_w[:].rearrange("p k n -> p (k n)"), in0=f8_high[:], scalar=1.0,
                                           in1=f8_byte[:].bitcast(FP8), op0=ALU.add, op1=ALU.mult).then_inc(f8["w_ready"], 1)

        def ffn_vector(dve):
            dve_rstd(dve, "ffn0")
            nc.vector.scalar_tensor_tensor(out=f8_shift[:], in0=ln_mv[:, :, 0], scalar=-1.0, in1=ln_rstd[:], op0=ALU.mult,
                                           op1=ALU.mult).then_inc(f8["shift_ready"], 1)

            def scales(i):
                for u in range(U):
                    dve.wait_ge(f8["norm_ready"], U * i + u + 1)
                    nc.vector.tensor_reduce(f8_amax[:, u:u + 1], f8_xn[:, i % 2, u, :], AX.X, ALU.max,
                                            apply_absolute_value=True).then_inc(f8["amax_ready"], 1)
                dve.wait_ge(f8["amax_ready"], U * (i + 1))
                nc.vector.tensor_scalar(f8_scale[:], f8_amax[:], 1e-12, 1.0 / 448.0, ALU.max, ALU.mult).then_inc(f8["scale_ready"], 1)
                dve.wait_ge(f8["scale_ready"], i + 1)
                nc.vector.reciprocal(f8_inv[:], f8_scale[:]).then_inc(f8["inv_ready"], 1)
                nc.vector.tensor_scalar(f8_total[:, i % 2, :], f8_scale[:], f8_ws[:, 0:1], None, ALU.mult).then_inc(f8["total_ready"], 1)

            def outputs(i):
                dve.wait_ge(f8["total_ready"], i + 1)
                for u in range(U):
                    t = U * i + u
                    dve.wait_ge(f8["out_done"], t + 1)
                    dve.wait_ge(f8["x_biased"], t + 1)
                    nc.vector.scalar_tensor_tensor(out=x[:, t, :], in0=bank(u, 1)[:, 0:D], scalar=f8_total[:, i % 2, u:u + 1],
                                                   in1=x[:, t, :], op0=ALU.mult, op1=ALU.add).then_inc(f8["x_updated"], 1)
                for u in range(U):
                    row_stats(dve, U * i + u, f8["x_updated"], U * i + u + 1, f8["stats_ready"])

            scales(0)
            for i in range(ROUNDS):
                for u in range(U):
                    if i > 0:
                        dve.wait_ge(f8["q_ready"], U * (i - 1) + u + 1)
                    dve.wait_ge(f8["scaled"], U * i + u + 1)
                    nc.vector.tensor_scalar(f8_magic[:, u, :].bitcast(I32), f8_xn[:, i % 2, u, :].bitcast(I32), 0x7F800000, None,
                                            ALU.bitwise_and).then_inc(f8["exponent_ready"], 1)
                for u in range(U):
                    dve.wait_ge(f8["exponent_ready"], U * i + u + 1)
                    nc.vector.tensor_scalar(f8_magic[:, u, :], f8_magic[:, u, :], 2.0 ** -6, 1.5 * 2.0 ** 20, ALU.max,
                                            ALU.mult).then_inc(f8["magic_ready"], 1)
                if i > 0:
                    outputs(i - 1)
                if i + 1 < ROUNDS:
                    scales(i + 1)
                for u in range(U):
                    dve.wait_ge(f8["added"], U * i + u + 1)
                    nc.vector.tensor_tensor(f8_q[:, u, :], f8_xn[:, i % 2, u, :], f8_magic[:, u, :], ALU.subtract).then_inc(f8["q_ready"], 1)
            outputs(ROUNDS - 1)
            dve.wait_ge(f8["stats_ready"], NT)

        def ffn_pool(pool):
            pool.wait_ge(f8["w_ready"], 1)
            for i in range(ROUNDS):
                for u in range(U):
                    t = U * i + u
                    pool.wait_ge(f8["norm_ready"], t + 1)
                    nc.gpsimd.tensor_tensor(x[:, t, :], x[:, t, :], f8_bias[:], ALU.add).then_inc(f8["x_biased"], 1)
                for u in range(U):
                    pool.wait_ge(f8["magic_ready"], U * i + u + 1)
                    v = f8_xn[:, i % 2, u, :]
                    nc.gpsimd.tensor_tensor(v, v, f8_magic[:, u, :], ALU.add).then_inc(f8["added"], 1)

        def ffn_tensor(pe):
            pe.wait_ge(f8["w_ready"], 1)
            for i in range(ROUNDS):
                n = lambda u: U * i + u + 1
                for u in range(U):
                    pe.wait_ge(f8["q_ready"], n(u))
                    for k in range(KC):
                        mm = nc.tensor.transpose(bank(u, 0).bitcast(BF16)[:, k * P:(k + 1) * P], f8_q[:, u, k * P:(k + 1) * P], ident_b[:])
                    mm.then_inc(f8["qT_done"], 1)
                for u in range(U):
                    pe.wait_ge(f8["qT_ready"], n(u))
                    for k in range(KC):
                        mm = nc.tensor.matmul(bank(u, 1)[:, 0:D], f8_qT[:, u, k, :], f8_w[:, k, :], start=(k == 0), stop=(k == KC - 1))
                    mm.then_inc(f8["out_done"], 1)

        def ffn_scalar(act):
            act_sqrt(act, "ffn0")
            act.wait_ge(f8["shift_ready"], 1)

            def normalise(i):
                for u in range(U):
                    t = U * i + u
                    nc.scalar.activation(f8_xn[:, i % 2, u, :], x[:, t, :], ACT.Identity, bias=f8_shift[:, t:t + 1],
                                         scale=ln_rstd[:, t:t + 1]).then_inc(f8["norm_ready"], 1)

            def scale(i):
                act.wait_ge(f8["inv_ready"], i + 1)
                for u in range(U):
                    v = f8_xn[:, i % 2, u, :]
                    nc.scalar.activation(v, v, ACT.Identity, scale=f8_inv[:, u:u + 1]).then_inc(f8["scaled"], 1)

            normalise(0)
            scale(0)
            for i in range(ROUNDS):
                if i + 1 < ROUNDS:
                    normalise(i + 1)
                    scale(i + 1)
                for u in range(U):
                    act.wait_ge(f8["qT_done"], U * i + u + 1)
                    nc.scalar.activation(f8_qT[:, u, :, :].rearrange("p k s -> p (k s)"), bank(u, 0).bitcast(BF16)[:, 0:D],
                                         ACT.Copy).then_inc(f8["qT_ready"], 1)

        x1_xn = sm_xn
        x1_wq = sb("x1_wq", [P, KC, D])
        x1_wk = sb("x1_wk", [P, KC, D])
        x1_wv = sb("x1_wv", [P, KC, D])
        x1_wo = sb("x1_wo", [P, KC, D])
        x1_bq = sb("x1_bq", [P, KC])
        x1_bk = sb("x1_bk", [P, KC])
        x1_bv = sb("x1_bv", [P, KC, P])
        x1_bo = sb("x1_bo", [P, D])
        x1_ctx = sb("x1_ctx", [P, KC, BT * SP + LAST])
        x1_mask8 = sb("x1_mask8", [S, BT, SK], U8)
        hide = sb("hide", [S, L, S])
        hide_b = sb("hide_b", [S, L, S], BF16)
        row_pick = sb("row_pick", [2 * 32 + 2 * G, 2 * G])
        x1 = {s: sem(f"xattn1_{s}") for s in (
            "weights_loaded", "bias_product", "bias_ready", "norm_ready", "xT_done", "xT_ready", "q_done", "q_ready",
            "zeroed", "w_split", "ctx_loaded", "ctx_high", "ctx_split", "mask_loaded", "mask_ready", "q_swapped", "q_high", "q_low",
            "qbd_ready", "kv0_done", "kv1_done", "kv0_free", "kv1_free", "k_high", "vl_high", "pl_high", "scores_done",
            "max_ready", "exp_ready", "pT_done", "pT_ready", "pv_done", "last_done", "vlbd_ready", "rinv_ready",
            "heads_ready", "x_biased", "stats_ready")}
        J = BT * G

        def x1q_vector(dve):
            dve.wait_ge(x1["weights_loaded"], 16 * 8)
            dve.wait_ge(x1["bias_product"], 1)
            nc.vector.tensor_tensor(x1_bo[:], bank(0, 0)[:, 0:D], x1_bo[:], ALU.add).then_inc(x1["bias_ready"], 1)
            dve_rstd(dve, "xattn1")
            for i in range(NT // U + 1):
                for u in range(U if i < NT // U else 0):
                    if i > 0:
                        dve.wait_ge(x1["xT_done"], 1 + U * i)
                    dve_normalise(U * i + u, x1_xn[:, u, :]).then_inc(x1["norm_ready"], 1)
                if i > 0:
                    dve.wait_ge(x1["q_ready"], KC * i)
                    cols = slice((i - 1) * U * P, i * U * P)
                    for r in range(2):
                        odd = x1_qT[:, :, cols].rearrange("p (k r) c -> p r k c", r=2)[:, r]
                        ins = nc.vector.tensor_copy(odd[64 * (1 - r):64 * (1 - r) + 64], odd[64 * r:64 * r + 64])
                    ins.then_inc(x1["q_swapped"], 1)

        def x1q_tensor(pe):
            pe.wait_ge(x1["weights_loaded"], 16 * 8)
            for k in range(KC):
                mm = nc.tensor.matmul(bank(0, 0)[:, 0:D], x1_bv[:, k, :], x1_wo[:, k, :], start=(k == 0), stop=(k == KC - 1))
            mm.then_inc(x1["bias_product"], 1)
            pe.wait_ge(x1["bias_ready"], 1)
            with pe.Fori(0, NT // U) as i:
                for u in range(U):
                    pe.wait_ge(x1["norm_ready"], U * i + u + 1)
                    for k in range(KC):
                        mm = nc.tensor.transpose(bank(u, 0)[:, k * P:(k + 1) * P], x1_xn[:, u, k * P:(k + 1) * P], ident[:])
                    mm.then_inc(x1["xT_done"], 1)
                pe.wait_ge(x1["xT_ready"], U * (i + 1))
                for m in range(KC):
                    for k in range(KC):
                        mm = nc.tensor.matmul(bank(m, 1), x1_wq[:, k, m * P:(m + 1) * P], x1_xT[:, k, :],
                                              start=(k == 0), stop=(k == KC - 1))
                    mm.then_inc(x1["q_done"], 1)

        def context_high(act, t, par, k):
            act.wait_ge(x1["ctx_loaded"], 16 * (t + 1))
            nc.scalar.activation(x1_cs[par][0][:, k, :], x1_ctx[:, k, :], ACT.Copy).then_inc(x1["ctx_high"], 1)

        def mask(act, t, par):
            act.wait_ge(x1["mask_loaded"], 16 * (t + 1))
            nc.scalar.activation(x1_mask[par][:, :, 0:SK], x1_mask8[:], ACT.Copy).then_inc(x1["mask_ready"], 1)

        def queries_high(act, t):
            nc.scalar.activation(x1_qhigh[:].rearrange("p h g c -> p g h c"),
                                 x1_qT[:, :, bass.ds(t * P, P)].rearrange("p g (h c) -> p g h c", h=2),
                                 ACT.Copy).then_inc(x1["q_high"], 1)

        def x1q_scalar(act):
            act_sqrt(act, "xattn1")
            for k in range(KC):
                context_high(act, 0, 0, k)
            act.wait_ge(x1["zeroed"], 2 + 2)
            mask(act, 0, 0)
            for i in range(NT // U):
                if i == 2:
                    act.wait_ge(x1["q_swapped"], 1)
                    queries_high(act, 0)
                for u in range(U):
                    act.wait_ge(x1["xT_done"], 1 + U * i + u + 1)
                    nc.scalar.activation(x1_xT[:, :, u * P:(u + 1) * P], bank(u, 0)[:, 0:D].rearrange("p (k s) -> p k s", k=KC),
                                         ACT.Copy).then_inc(x1["xT_ready"], 1)
                for m in range(KC):
                    act.wait_ge(x1["q_done"], KC * i + m + 1)
                    for r in range(2):
                        rows = slice(64 * r, 64 * r + 64)
                        ins = nc.scalar.activation(x1_qT[rows, 2 * m + r, i * U * P:(i + 1) * U * P], bank(m, 1)[rows, :],
                                                   ACT.Identity, bias=x1_bq[rows, m:m + 1])
                    ins.then_inc(x1["q_ready"], 1)

        ORDER = [(0, "k0", 1, 0), (1, "k1", 1, 0), (2, "plT", 1, -1), (3, "v", 1, 0),
                 (4, "k0", 2, 0), (5, "k1", 2, 0), (6, "oT", 1, -1), (7, "v", 2, 0), (7, "out", 0, -1),
                 (8, "k0", 3, 0), (9, "k1", 3, 0), (10, "plT", 0, 0), (11, "v", 3, 0),
                 (12, "k0", 0, 1), (13, "k1", 0, 1), (14, "oT", 0, 0), (15, "v", 0, 1), (15, "vl", 0, 1)]
        PIECES = len(ORDER)
        LEAD = 13
        HJ = J // 2
        STACK = 2 * 32 + HJ

        def kv_bank(n):
            return psum[:, n % 2, :]

        def place(kind, b=0):
            return next(n for n, (_, k, bb, _) in enumerate(ORDER) if (k, bb) == (kind, b))

        def kv_count(n, t):
            return PIECES // 2 * (t + 1) + n // 2 - (LEAD // 2 - n % 2)

        def kv_free(eng, n, t):
            eng.wait_ge(x1[f"kv{n % 2}_free"], kv_count(n, t))

        def kv_done(eng, n, t):
            eng.wait_ge(x1[f"kv{n % 2}_done"], kv_count(n, t))

        def kv_taken(eng, n, t):
            eng.wait_ge(x1[f"kv{n % 2}_free"], kv_count(n, t) + 1)

        def x1_tiles(eng, tile):
            tile(0, 0, False, True, True)
            with eng.Fori(0, (NT - 2) // 2) as i:
                for n in range(2):
                    tile(2 * i + (1 + n), (1 + n) % 2, True, True, True)
            tile(NT - 1, (NT - 1) % 2, True, True, False)
            tile(NT, NT % 2, True, False, False)

        def exact(out, pairs, first, last, **kw):
            for n, (v, w) in enumerate(pairs):
                mm = nc.tensor.matmul(out, v, w, start=(first and n == 0), stop=(last and n == len(pairs) - 1), **kw)
            return mm

        def parts(v, w):
            return ((v[0], w[0]), (v[0], w[1]), (v[1], w[0]))

        def x1_piece(pe, n, t, par):
            _, kind, b, whose = ORDER[n]
            ct = x1_cs[(par + 1) % 2 if whose == 1 else par]
            out = kv_bank(n)
            if kind == "k0" and b == 0:
                pe.wait_ge(x1["ctx_split"], t + 1 + 1)
            kv_free(pe, n, t)
            if kind == "vl":
                for k in range(KC):
                    mm = exact(out[0:LAST, 0:D], parts([c[:, k, BT * SP:] for c in ct], [w[:, k, :] for w in x1_wvs]),
                               k == 0, k == KC - 1)
            elif kind in ("k0", "k1"):
                m = slice(int(kind[1]) * P, int(kind[1]) * P + P)
                for k in range(KC):
                    mm = exact(out[:, 0:SP], parts([w[:, k, m] for w in x1_wks], [c[:, k, b * SP:(b + 1) * SP] for c in ct]),
                               k == 0, k == KC - 1)
            elif kind == "v":
                for c0 in range(2):
                    cols = slice(b * SP + c0 * P, b * SP + (c0 + 1) * P)
                    for k in range(KC):
                        mm = exact(out[:, c0 * D:(c0 + 1) * D], parts([c[:, k, cols] for c in ct], [w[:, k, :] for w in x1_wvs]),
                                   k == 0, k == KC - 1, skip_group_check=True)
            elif kind == "plT":
                pe.wait_ge(x1["exp_ready"], J * (t + 1 + whose) - HJ + HJ * b)
                mm = nc.tensor.transpose(out[0:HJ, 0:P], x1_p[:, HJ * b:HJ * (b + 1), SK - 1], ident[:])
            elif kind == "oT":
                pe.wait_ge(x1["heads_ready"], 2 * (t + whose) + b + 1)
                mm = nc.tensor.transpose(out[:, 0:P], x1_o[:, b * HJ:(b + 1) * HJ, :].rearrange("p j d -> p (j d)"), ident[:])
            elif kind == "out":
                kv_taken(pe, place("oT", 1), t)
                for k in range(KC):
                    mm = nc.tensor.matmul(out[:, 0:D], x1_oT[:, k, :, :].rearrange("p b s -> p (b s)"), x1_wo[:, k, :],
                                          start=(k == 0), stop=(k == KC - 1))
            mm.then_inc(x1[f"kv{n % 2}_done"], 1)

        def x1_no_piece(pe, n, t):
            kv_free(pe, n, t)
            pe.sem_inc(x1[f"kv{n % 2}_done"], 1)
            pe.sem_inc(x1[f"kv{n % 2}_free"], 1)

        def x1_tensor(pe):
            pe.wait_ge(x1["q_ready"], KC * NT // U)
            pe.wait_ge(x1["w_split"], 4)
            for k in range(2):
                pe.sem_inc(x1[f"kv{k}_free"], 1)
            for n in range(LEAD, PIECES):
                if ORDER[n][3] == 1:
                    x1_piece(pe, n, -1, 1)
                else:
                    x1_no_piece(pe, n, -1)

            def last_key(t, h):
                kv_taken(pe, place("plT", h), t)
                nc.tensor.matmul(psum[:, 6 + h, :], x1_plT[:], x1_vlbd[:, h, :, :].rearrange("p j d -> p (j d)"),
                                 start=False, stop=True, skip_group_check=True).then_inc(x1["last_done"], 1)

            def tile(t, par, before, own, after):
                there = {-1: before, 0: own, 1: after}
                for s in range(J):
                    if own:
                        b, g = s // G, s % G
                        r = 64 * (g % 2)
                        if g == 0:
                            for m in range(KC):
                                kv_taken(pe, place(f"k{m}", b), t - (b == 0))
                        if s % HJ == 0:
                            pe.wait_ge(x1["qbd_ready"], 2 * t + s // HJ + 1)
                        if s == 0:
                            pe.wait_ge(x1["mask_ready"], 1 + t + 1)
                        if s >= 2 or before:
                            pe.wait_ge(x1["exp_ready"], J * t + s - 1)
                        sc = psum[:, 2 + s % 2, 0:SP]
                        nc.tensor.matmul(sc, hide_b[:].rearrange("p l q -> p (l q)"), x1_mask[par][:, b, :], start=True, stop=False)
                        nc.tensor.matmul(sc, x1_qh[:, b // 2, g, b % 2, :], x1_k[:, b % 2, g, :], start=False, stop=False)
                        nc.tensor.matmul(sc, x1_ql[r:r + 64, b // 2, g, b % 2, :], x1_k[r:r + 64, b % 2, g, :],
                                         start=False, stop=True).then_inc(x1["scores_done"], 1)
                    if before if s < 2 else own:
                        pe.wait_ge(x1["exp_ready"], J * t + s - 1)
                        if s >= 4 or before:
                            pe.wait_ge(x1["pT_ready"], J * t + s - 3)
                        for c in range(2):
                            mm = nc.tensor.transpose(psum[:, 4 + s % 2, c * P:(c + 1) * P], x1_p[:, (s - 2) % J, c * P:(c + 1) * P], ident[:])
                        mm.then_inc(x1["pT_done"], 1)
                    if before if s < 3 else own:
                        j = (s - 3) % J
                        b, g = j // G, j % G
                        pe.wait_ge(x1["pT_ready"], J * t + s - 2)
                        if g == 0:
                            kv_taken(pe, place("v", b), t - (b == 0))
                        for c in range(2):
                            mm = nc.tensor.matmul(psum[:, 6 + b // 2, (b % 2) * D + g * 64:(b % 2) * D + (g + 1) * 64],
                                                  x1_pT[:, j % 2, c, :], x1_v[:, b % 2, c, g * 64:(g + 1) * 64],
                                                  start=(b % 2 == 0 and g == 0 and c == 0), stop=False, skip_group_check=True)
                        mm.then_inc(x1["pv_done"], 1)
                    for n, (at, _, _, whose) in enumerate(ORDER):
                        if at == s:
                            if there[whose]:
                                x1_piece(pe, n, t, par)
                            else:
                                x1_no_piece(pe, n, t)
                    if s == 4 and before:
                        last_key(t, 1)
                    if s == 12 and own:
                        pe.wait_ge(x1["vlbd_ready"], t + 1)
                        last_key(t, 0)

            x1_tiles(pe, tile)

        def x1_scalar(act):
            nc.scalar.preload_act_table(ACT.Exp)

            def take(n, t):
                _, kind, b, _ = ORDER[n]
                if kind in ("k0", "k1"):
                    m = int(kind[1])
                    hold(act, x1[f"kv{n % 2}_done"], kv_count(n, t))
                    for r in range(2):
                        rows = slice(64 * r, 64 * r + 64)
                        ins = nc.scalar.activation(x1_k[rows, b % 2, 2 * m + r, :], kv_bank(n)[rows, 0:SP], ACT.Identity,
                                                   bias=x1_bk[rows, m:m + 1])
                    ins.then_inc(x1["k_high"], 1)
                elif kind == "v":
                    kv_done(act, n, t)
                    nc.scalar.activation(x1_v[:, b % 2, :, :].rearrange("p c n -> p (c n)"), kv_bank(n),
                                         ACT.Copy).then_inc(x1[f"kv{n % 2}_free"], 1)
                elif kind == "vl":
                    if not (isinstance(t, int) and t < 0):
                        act.wait_ge(x1["vlbd_ready"], t + 1)
                    kv_done(act, n, t)
                    for h, row in ((0, 0), (0, 64), (1, 0), (1, 64), (1, 32)):
                        ins = nc.scalar.activation(x1_vls[row:row + HJ, h * D:(h + 1) * D], kv_bank(n)[32 * h:32 * h + HJ, 0:D], ACT.Copy)
                    ins.then_inc(x1["vl_high"], 1)
                elif kind == "oT":
                    kv_done(act, n, t)
                    for r in range(2):
                        for rb in range(2):
                            v = kv_bank(n)[64 * rb:64 * rb + 64, 0:P].rearrange("p (j r q) -> p r j q", j=L // 2, r=2)[:, r]
                            ins = nc.scalar.copy(x1_oT[64 * r:64 * r + 64, :, 2 * b + rb, :], v)
                    ins.then_inc(x1[f"kv{n % 2}_free"], 1)

            for n in range(LEAD, PIECES):
                if ORDER[n][3] == 1:
                    take(n, -1)

            def tile(t, par, before, own, after):
                there = {-1: before, 0: own, 1: after}
                for s in range(J):
                    if after:
                        if s in (3, 4):
                            context_high(act, t + 1, 1 - par, s - 3)
                        if s == 7:
                            mask(act, t + 1, 1 - par)
                        if s == 11:
                            hold(act, x1["qbd_ready"], 2 * (t + 1))
                            if not before:
                                act.wait_ge(x1["q_swapped"], NT // U)
                            queries_high(act, t + 1)
                    if own:
                        act.wait_ge(x1["max_ready"], J * t + s + 1)
                        nc.scalar.activation(x1_p[:, s, :], psum[:, 2 + s % 2, 0:SK], ACT.Exp, bias=x1_nmax[:, s:s + 1],
                                             accum_out=x1_sum[:, s:s + 1]).then_inc(x1["exp_ready"], 1)
                    for n, (at, _, _, whose) in enumerate(ORDER):
                        if at == s and there[whose]:
                            take(n, t)

            x1_tiles(act, tile)

        def x1_vector(dve):
            dve.wait_ge(x1["x_biased"], NT)

            def take(n, t):
                _, kind, b, whose = ORDER[n]
                freed = x1[f"kv{n % 2}_free"]
                if kind in ("k0", "k1"):
                    m = int(kind[1])
                    dve.wait_ge(x1["k_high"], 2 * BT * (t + whose) + 2 * b + m + 1)
                    for r in range(2):
                        rows, over = slice(64 * r, 64 * r + 64), slice(64 * (1 - r), 64 * (1 - r) + 64)
                        ins = nc.vector.scalar_tensor_tensor(out=x1_k[over, b % 2, 2 * m + r, :], in0=kv_bank(n)[rows, 0:SP],
                                                             scalar=x1_bk[rows, m:m + 1],
                                                             in1=x1_k[rows, b % 2, 2 * m + r, :].bitcast(F32),
                                                             op0=ALU.add, op1=ALU.subtract)
                    ins.then_inc(freed, 1)
                elif kind == "vl":
                    dve.wait_ge(x1["vl_high"], t + 1 + 1)
                    for h in range(2):
                        rows = slice(32 * h, 32 * h + HJ)
                        ins = nc.vector.tensor_tensor(x1_vls[32:32 + HJ, h * D:(h + 1) * D], kv_bank(n)[rows, 0:D],
                                                      x1_vls[rows, h * D:(h + 1) * D].bitcast(F32), ALU.subtract)
                    ins.then_inc(freed, 1)
                elif kind == "plT":
                    hold(dve, x1[f"kv{n % 2}_done"], kv_count(n, t))
                    nc.vector.tensor_copy(x1_plT[0:HJ, :], kv_bank(n)[0:HJ, 0:P]).then_inc(x1["pl_high"], 1)
                    nc.vector.tensor_copy(x1_plT[32:32 + HJ, :], kv_bank(n)[0:HJ, 0:P])
                    dve.wait_ge(x1["pl_high"], 2 * (t + whose) + b + 1)
                    nc.vector.tensor_tensor(x1_plT[64:64 + HJ, :], kv_bank(n)[0:HJ, 0:P], x1_plT[0:HJ, :].bitcast(F32),
                                            ALU.subtract).then_inc(freed, 1)
                elif kind == "out":
                    kv_done(dve, n, t)
                    nc.vector.tensor_tensor(x[:, bass.ds(t + whose, 1), :].rearrange("p o c -> p (o c)"), kv_bank(n)[:, 0:D],
                                            x[:, bass.ds(t + whose, 1), :].rearrange("p o c -> p (o c)"), ALU.add).then_inc(freed, 1)

            def inverse(h, n):
                c = slice(h * HJ, (h + 1) * HJ)
                nc.vector.tensor_scalar(x1_void[:, c], x1_nmax[:, c], 1e10, 0.0, ALU.mult, ALU.mult)
                nc.vector.reciprocal(x1_rinv[:, c], x1_sum[:, c]).then_inc(x1["rinv_ready"], 1)
                dve.wait_ge(x1["rinv_ready"], 2 * n + 1)
                nc.vector.tensor_tensor(x1_rinv[:, c], x1_rinv[:, c], x1_void[:, c], ALU.add).then_inc(x1["rinv_ready"], 1)

            def heads(h, n):
                dve.wait_ge(x1["rinv_ready"], 2 * n + 2)
                dve.wait_ge(x1["last_done"], n + 1)
                c = slice(h * HJ, (h + 1) * HJ)
                pick_heads(psum[:, 6 + h:7 + h, :], x1_rinv[:, c], x1_o[:, c, :]).then_inc(x1["heads_ready"], 1)

            for n in range(LEAD, PIECES):
                if ORDER[n][3] == 1 and ORDER[n][1] != "vl":
                    take(n, -1)

            def tile(t, par, before, own, after):
                there = {-1: before, 0: own, 1: after}
                for s in range(J):
                    if own:
                        dve.wait_ge(x1["scores_done"], J * t + s + 1)
                        nc.vector.tensor_reduce(x1_nmax[:, s:s + 1], psum[:, 2 + s % 2, 0:SK], AX.X, ALU.max,
                                                negate=True).then_inc(x1["max_ready"], 1)
                    if before if s < 2 else own:
                        dve.wait_ge(x1["pT_done"], J * t + s - 1)
                        if s >= 4 or before:
                            dve.wait_ge(x1["pv_done"], J * t + s - 3)
                        nc.vector.tensor_copy(x1_pT[:, s % 2, :, :].rearrange("p c n -> p (c n)"),
                                              psum[:, 4 + s % 2, 0:D]).then_inc(x1["pT_ready"], 1)
                    for n, (at, _, _, whose) in enumerate(ORDER):
                        if at == s - 1 and there[whose]:
                            take(n, t)
                    if s == 0 and own:
                        take(place("vl"), t - 1)
                    if s == 3 and before:
                        dve.wait_ge(x1["exp_ready"], J * t)
                        inverse(1, 2 * t - 1)
                    if s == 4 and before:
                        heads(1, 2 * t - 1)
                    if s == 11 and own:
                        dve.wait_ge(x1["exp_ready"], J * t + HJ)
                        inverse(0, 2 * t)
                    if s == 12 and own:
                        heads(0, 2 * t)
                    if s == 15 and before:
                        n = place("out")
                        hold(dve, x1[f"kv{n % 2}_free"], kv_count(n, t) + 1)
                        nc.vector.bn_stats(bn_out[:, bass.ds(t - 1, 1), :].rearrange("p o c -> p (o c)"),
                                           x[:, bass.ds(t - 1, 1), :].rearrange("p o c -> p (o c)")).then_inc(x1["stats_ready"], 1)

            x1_tiles(dve, tile)
            dve.wait_ge(x1["stats_ready"], NT)

        def x1_pool_weights(pool):
            pool.wait_ge(x1["weights_loaded"], 16 * 8)
            pool.wait_ge(var_ready, layers.index("xattn1") + 1)
            for v in x1_mask:
                nc.gpsimd.memset(v[:], 0.0).then_inc(x1["zeroed"], 1)
            for v in (x1_plT, x1_vls):
                nc.gpsimd.memset(v[:].bitcast(F32), 0.0).then_inc(x1["zeroed"], 1)
            for w, (high, low) in ((x1_wk, x1_wks), (x1_wv, x1_wvs)):
                nc.gpsimd.tensor_copy(high[:], w[:]).then_inc(x1["w_split"], 1)
                pool.wait_ge(x1["w_split"], 1 if w is x1_wk else 3)
                nc.gpsimd.tensor_tensor(low[:], w[:], high[:].bitcast(F32), ALU.subtract).then_inc(x1["w_split"], 1)

        def x1_context(pool, t, par):
            high, low = x1_cs[par]
            pool.wait_ge(x1["ctx_high"], KC * (t + 1))
            nc.gpsimd.tensor_tensor(low[:], x1_ctx[:], high[:].bitcast(F32), ALU.subtract).then_inc(x1["ctx_split"], 1)

        def x1_pool(pool):
            def queries(t):
                own = x1_qT[:, :, bass.ds(t * P, P)].rearrange("p g (h c) -> p g h c", h=2)
                hold(pool, x1["q_high"], t + 1)
                nc.gpsimd.tensor_tensor(x1_qlow[:].rearrange("p h g c -> p g h c"), own, x1_qhigh[:].rearrange("p h g c -> p g h c").bitcast(F32),
                                        ALU.subtract).then_inc(x1["q_low"], 1)

            def spread(t, h):
                if h == 0:
                    pool.wait_ge(x1["q_low"], t + 1)
                for dst, src in ((x1_qh, x1_qhigh), (x1_ql, x1_qlow)):
                    shape = [P, 2 * G, L, S]
                    ins = nc.gpsimd.tensor_tensor(
                        dst[:, h].rearrange("p g b (l q) -> p (g b) l q", l=L),
                        src[:, h].rearrange("p g (b q) -> p (g b) q", b=2).unsqueeze(2).broadcast_to(shape),
                        head_scale[:].unsqueeze(1).unsqueeze(3).broadcast_to(shape), ALU.mult)
                ins.then_inc(x1["qbd_ready"], 1)

            queries(0)
            spread(0, 0)
            spread(0, 1)

            def tile(t, par, before, own, after):
                if after:
                    if before:
                        pool.wait_ge(x1["scores_done"], J * t)
                    x1_context(pool, t + 1, 1 - par)
                if own:
                    if before:
                        pool.wait_ge(x1["last_done"], 2 * t)
                    kv_taken(pool, place("vl"), t - 1)
                    shape = [STACK, 2, G, 64]
                    for h in range(2):
                        ins = nc.gpsimd.tensor_tensor(
                            x1_vlbd[:, h].rearrange("p (b g) d -> p b g d", b=2),
                            x1_vls[:, h * D:(h + 1) * D].rearrange("p (g d) -> p g d", g=G).unsqueeze(1).broadcast_to(shape),
                            row_pick[:].rearrange("p (b g) -> p b g", b=2).unsqueeze(3).broadcast_to(shape), ALU.mult)
                    ins.then_inc(x1["vlbd_ready"], 1)
                if after:
                    queries(t + 1)
                    for h in range(2):
                        pool.wait_ge(x1["scores_done"], J * t + HJ * (h + 1))
                        spread(t + 1, h)

            x1_tiles(pool, tile)

        on_u, on_v = slice(GH, GH + R), slice(GH + R, GH + 2 * R)
        mx_w = sb("mx_w", [P, KC, GH + 2 * R])
        mx_b1 = sb("mx_b1", [GH, 1])
        mx_w2 = sb("mx_w2", [GH, R])
        mx_b2 = sb("mx_b2", [GH + R, 1])
        mx_conv = sb("mx_conv", [P, KC, 3])
        mx_wo = sb("mx_wo", [GH + R, D])
        mx_bo = sb("mx_bo", [P, D])
        mx_keep = sb("mx_keep", [P, U * P])
        mx = {s: sem(f"mix1_{s}") for s in (
            "weights_loaded", "taps_ready", "bias_ready", "norm_ready", "xT_done", "xT_ready", "huv_done", "h_ready",
            "gate_done", "gate_ready", "sum_ready", "gu_ready", "glob_ready", "out_done", "x_biased", "x_updated", "stats_ready")}

        def turned(u):
            return psum[:, 5 + 2 * (u // 2), (u % 2) * D:(u % 2 + 1) * D]

        def mix_vector(dve):
            dve.wait_ge(mx["weights_loaded"], 16 * 8)
            for k in range(KC):
                for j in range(3):
                    nc.vector.tensor_scalar(mx_taps[:, k, j, :], ident[:], mx_conv[:, k, j:j + 1], None,
                                            ALU.mult).then_inc(mx["taps_ready"], 1)
            for xT in mx_xT:
                for j, first in ((0, 0), (2, S + 1)):
                    nc.vector.memset(xT[:, j, :, first:first + U * P - S + 1:S], 0.0).then_inc(mx["taps_ready"], 1)
            dve_rstd(dve, "mix1")

            def normalise(i):
                if i > 0:
                    dve.wait_ge(mx["xT_done"], U * i)
                for u in range(U):
                    dve_normalise(U * i + u, sm_xn[:, u, :]).then_inc(mx["norm_ready"], 1)

            normalise(0)
            for i in range(ROUNDS):
                n = lambda u: U * i + u + 1
                if i + 1 < ROUNDS:
                    normalise(i + 1)
                dve.wait_ge(mx["huv_done"], i + 1)
                dve.wait_ge(mx["h_ready"], i + 1)
                nc.vector.tensor_tensor_scan(mx_sum[on_u, :], mx_keep[on_v, :], psum[on_v, 1, :], 0.0, ALU.mult,
                                             ALU.add).then_inc(mx["sum_ready"], 1)
                dve.wait_ge(mx["gate_ready"], i + 1)
                nc.vector.tensor_tensor(mx_gu[on_u, :], psum[on_u, 1, :], mx_gate[on_u, :], ALU.mult).then_inc(mx["gu_ready"], 1)
                dve.wait_ge(mx["gu_ready"], i + 1)
                dve.wait_ge(mx["sum_ready"], i + 1)
                nc.vector.tensor_tensor(mx_glob[on_u, :], mx_gu[on_u, :], mx_sum[on_u, :], ALU.mult).then_inc(mx["glob_ready"], 1)
                for u in range(U):
                    dve.wait_ge(mx["out_done"], n(u))
                    dve.wait_ge(mx["x_biased"], n(u))
                    nc.vector.tensor_tensor(x[:, U * i + u, :], bank(u, 0)[:, 0:D], x[:, U * i + u, :], ALU.add).then_inc(mx["x_updated"], 1)
                for u in range(U):
                    row_stats(dve, U * i + u, mx["x_updated"], n(u), mx["stats_ready"])
            dve.wait_ge(mx["stats_ready"], NT)

        def mix_tensor(pe):
            pe.wait_ge(mx["weights_loaded"], 16 * 8)

            def turn(i):
                for u in range(U):
                    pe.wait_ge(mx["norm_ready"], U * i + u + 1)
                    for k in range(KC):
                        mm = nc.tensor.transpose(turned(u)[:, k * P:(k + 1) * P], sm_xn[:, u, k * P:(k + 1) * P], ident[:])
                    mm.then_inc(mx["xT_done"], 1)

            turn(0)
            pe.wait_ge(mx["taps_ready"], 3 * KC + 4)
            for i in range(ROUNDS):
                xT = mx_xT[i % 2]
                pe.wait_ge(mx["xT_ready"], U * (i + 1))
                for k in range(KC):
                    mm = nc.tensor.matmul(psum[:, 1, :], mx_w[:, k, :], xT[:, 1, k, 1:1 + U * P], start=(k == 0), stop=(k == KC - 1))
                mm.then_inc(mx["huv_done"], 1)
                for u in range(U):
                    if i > 0:
                        pe.wait_ge(mx["x_updated"], U * (i - 1) + u + 1)
                    for k in range(KC):
                        for j in range(3):
                            nc.tensor.matmul(bank(u, 0)[:, k * P:(k + 1) * P], xT[:, j, k, u * P + j:(u + 1) * P + j],
                                             mx_taps[:, k, j, :], start=(k == 0 and j == 0), stop=False, skip_group_check=True)
                    if u == 0:
                        pe.wait_ge(mx["h_ready"], i + 1)
                        nc.tensor.matmul(psum[on_u, 3, :], mx_w2[:], mx_h[:], start=True, stop=True).then_inc(mx["gate_done"], 1)
                        if i + 1 < ROUNDS:
                            turn(i + 1)
                pe.wait_ge(mx["glob_ready"], i + 1)
                for u in range(U):
                    nc.tensor.matmul(bank(u, 0)[:, 0:D], mx_glob[on_u, u * P:(u + 1) * P], mx_wo[on_u, :], start=False, stop=True,
                                     skip_group_check=True).then_inc(mx["out_done"], 1)

        def mix_scalar(act):
            act_sqrt(act, "mix1")
            nc.scalar.preload_act_table(ACT.Sigmoid)
            act.wait_ge(mx["taps_ready"], 3 * KC + 4)

            def take(i):
                for u in range(U):
                    act.wait_ge(mx["xT_done"], U * i + (u // 2 + 1) * 2)
                    for j, (s0, s1) in enumerate(((0, S - 1), (0, S), (1, S))):
                        src = turned(u).rearrange("p (k b s) -> p k b s", k=KC, b=BT)
                        dst = mx_xT[i % 2][:, j, :, 1 + u * P:1 + (u + 1) * P].rearrange("p k (b s) -> p k b s", b=BT)
                        ins = nc.scalar.activation(dst[:, :, :, s0:s1], src[:, :, :, s0:s1], ACT.Copy)
                    ins.then_inc(mx["xT_ready"], 1)

            take(0)
            for i in range(ROUNDS):
                act.wait_ge(mx["huv_done"], i + 1)
                nc.scalar.activation(mx_h[:], psum[0:GH, 1, :], ACT.Relu, bias=mx_b1[:, 0:1]).then_inc(mx["h_ready"], 1)
                act.wait_ge(mx["gate_done"], i + 1)
                nc.scalar.activation(mx_gate[on_u, :], psum[on_u, 3, :], ACT.Sigmoid, bias=mx_b2[on_u, 0:1]).then_inc(mx["gate_ready"], 1)
                if i + 1 < ROUNDS:
                    take(i + 1)

        me_raw = sb("me_raw", [P, 2, 1024])
        me_b1 = sb("me_b1", [P, EX, HM])
        me_b2 = sb("me_b2", [EX, D])
        me_rw = sb("me_rw", [P, KC, E])
        me_rb = sb("me_rb", [P, E])
        me_before = sb("me_before", [P, E, E])
        me = {s: sem(f"moe1_{s}") for s in (
            "weights_loaded", "router_split", "norm_ready", "xT_done", "xh_ready", "xl_ready", "lT_done", "lT_ready", "logits_done", "logits_read",
            "exp_ready", "gate_ready", "gT_done", "gT_ready", "raw_loaded", "w_high", "w1_split", "w2_split",
            "up_done", "h_ready", "hh_ready", "hl_ready", "down_done", "acc_ready", "stored")}

        def split(dve, high, low, src, sem_h, count, sem_l):
            nc.vector.tensor_copy(high, src).then_inc(sem_h, 1)
            dve.wait_ge(sem_h, count)
            nc.vector.tensor_tensor(low, src, high.bitcast(F32), ALU.subtract).then_inc(sem_l, 1)

        def moe_weights(dve, e, par):
            dve.wait_ge(me["raw_loaded"], 16 * (e + 1))
            split(dve, me_wh[par][:, 0, :], me_wl[par][:, 0, :], me_raw[:, 0, :], me["w_high"], 2 * e + 1, me["w1_split"])
            split(dve, me_wh[par][:, 1, :], me_wl[par][:, 1, :], me_raw[:, 1, :], me["w_high"], 2 * e + 2, me["w2_split"])

        def moe_prep_vector(dve):
            dve.wait_ge(me["weights_loaded"], 16 * 5)
            link(dve, nc.vector.tensor_copy(me_rwh[:], me_rw[:]))
            link(dve, nc.vector.tensor_tensor(me_rwl[:], me_rw[:], me_rwh[:].bitcast(F32), ALU.subtract))
            nc.vector.memset(me_gate[:], 1.0).then_inc(me["router_split"], 1)
            dve_rstd(dve, "moe1")
            with dve.Fori(0, NT // U) as i:
                for u in range(U):
                    dve_normalise(U * i + u, sm_xn[:, u, :]).then_inc(me["norm_ready"], 1)
                for u in range(U):
                    t = U * i + u
                    dve.wait_ge(me["xh_ready"], t + 1)
                    nc.vector.tensor_tensor(me_xl[:, :, bass.ds(t * P, P)], bank(u, 0)[:, 0:D].rearrange("p (k s) -> p k s", k=KC),
                                            me_xh[:, :, bass.ds(t * P, P)].bitcast(F32), ALU.subtract).then_inc(me["xl_ready"], 1)

        def moe_gates(dve):
            dve.wait_ge(me["logits_done"], 1)
            dve.wait_ge(me["router_split"], 1)
            wide = [P, NT, E]
            link(dve, nc.vector.tensor_tensor(me_pr[:], logits(), me_rb[:].unsqueeze(1).broadcast_to(wide), ALU.add))
            link(dve, nc.vector.tensor_reduce(me_st[:], me_pr[:], AX.X, ALU.max))
            nc.vector.tensor_tensor(me_pr[:], me_pr[:], me_st[:].unsqueeze(2).broadcast_to(wide), ALU.subtract).then_inc(me["logits_read"], 1)

        def moe_gates_end(dve):
            wide = [P, NT, E]
            dve.wait_ge(me["exp_ready"], 1)
            link(dve, nc.vector.tensor_reduce(me_st[:], me_pr[:], AX.X, ALU.add))
            link(dve, nc.vector.reciprocal(me_st[:], me_st[:]))
            link(dve, nc.vector.tensor_tensor(me_pr[:], me_pr[:], me_st[:].unsqueeze(2).broadcast_to(wide), ALU.mult))
            full = [P, NT, E, E]
            mine, other = me_pr[:].unsqueeze(3).broadcast_to(full), me_pr[:].unsqueeze(2).broadcast_to(full)
            link(dve, nc.vector.tensor_tensor(me_cmp[:], other, mine, ALU.is_equal))
            link(dve, nc.vector.tensor_tensor(me_cmp[:], me_cmp[:], me_before[:].unsqueeze(1).broadcast_to(full), ALU.mult))
            link(dve, nc.vector.tensor_tensor(me_cmp2[:], other, mine, ALU.is_gt))
            link(dve, nc.vector.tensor_tensor(me_cmp[:], me_cmp[:], me_cmp2[:], ALU.add))
            link(dve, nc.vector.tensor_reduce(me_rank[:], me_cmp[:], AX.X, ALU.add))
            link(dve, nc.vector.tensor_scalar(me_rank[:], me_rank[:], 2.0, None, ALU.is_lt))
            nc.vector.tensor_tensor(me_gate[:, :, 0:E], me_rank[:], me_pr[:], ALU.mult).then_inc(me["gate_ready"], 1)

        def logits():
            return bank(3, 1)[:, 0:NT * E].rearrange("p (t e) -> p t e", t=NT)

        def moe_prep_tensor(pe):
            pe.wait_ge(me["router_split"], 1)
            with pe.Fori(0, NT // U) as i:
                for u in range(U):
                    pe.wait_ge(me["norm_ready"], U * i + u + 1)
                    for k in range(KC):
                        mm = nc.tensor.transpose(bank(u, 0)[:, k * P:(k + 1) * P], sm_xn[:, u, k * P:(k + 1) * P], ident[:])
                    mm.then_inc(me["xT_done"], 1)
                pe.wait_ge(me["xl_ready"], U * (i + 1))
                pe.wait_ge(me["lT_ready"], 1 + i)
                for k in range(KC):
                    rows = [v[:, k, bass.ds(i * (U * P), U * P)] for v in (me_xh, me_xl)]
                    mm = exact(bank(1, 1)[0:E, :], parts([w[:, k, :] for w in (me_rwh, me_rwl)], rows), k == 0, k == KC - 1)
                mm.then_inc(me["lT_done"], 1)
            pe.wait_ge(me["lT_ready"], 1 + NT // U)
            for t in range(NT):
                mm = nc.tensor.transpose(bank(3, 1)[:, t * E:(t + 1) * E], me_lT[:, t * P:(t + 1) * P], ident[0:E, 0:E])
            mm.then_inc(me["logits_done"], 1)

        def moe_prep_scalar(act):
            act_sqrt(act, "moe1")
            act.wait_ge(me["raw_loaded"], 16)
            for m in range(2):
                nc.scalar.activation(me_wh[0][:, m, :], me_raw[:, m, :], ACT.Copy).then_inc(me["w_high"], 1)
            with act.Fori(0, NT // U) as i:
                for u in range(U):
                    t = U * i + u
                    hold(act, me["xT_done"], t + 1)
                    nc.scalar.activation(me_xh[:, :, bass.ds(t * P, P)], bank(u, 0)[:, 0:D].rearrange("p (k s) -> p k s", k=KC),
                                         ACT.Copy).then_inc(me["xh_ready"], 1)
                hold(act, me["lT_done"], i + 1)
                nc.scalar.activation(me_lT[:, bass.ds(i * (U * P), U * P)], bank(1, 1)[0:E, :], ACT.Copy).then_inc(me["lT_ready"], 1)
            act.wait_ge(me["logits_read"], 1)
            nc.scalar.activation(me_pr[:], me_pr[:], ACT.Exp).then_inc(me["exp_ready"], 1)

        NG = NT // TG

        def down_psum(gr, tau):
            return psum[:, 4 + 2 * (gr % 2) + tau // 2, (tau % 2) * D:(tau % 2) * D + D]

        def moe_experts(eng, expert):
            expert(0, 0)
            gates_turned(eng)
            with eng.Fori(0, (EX - 3) // 2) as i:
                for n in range(2):
                    expert(2 * i + (1 + n), (1 + n) % 2)
            expert(EX - 2, (EX - 2) % 2)
            expert(EX - 1, (EX - 1) % 2)

        def gates_turned(eng):
            for i in range(NT // U):
                if eng is nc.tensor:
                    if i == 0:
                        eng.wait_ge(me["h_ready"], HM * NG)
                        eng.wait_ge(me["gate_ready"], 1)
                    for u in range(U):
                        mm = nc.tensor.transpose(psum[0:EX, i, u * P:(u + 1) * P], me_gate[:, U * i + u, :], ident[:])
                    mm.then_inc(me["gT_done"], 1)
                elif eng is nc.scalar:
                    eng.wait_ge(me["gT_done"], i + 1)
                    nc.scalar.copy(me_gT[:, i * U * P:(i + 1) * U * P], psum[0:EX, i, :]).then_inc(me["gT_ready"], 1)

        def moe_tensor(pe):
            pairs = lambda vh, vl, wh, wl: ((vh, wh), (vh, wl), (vl, wh))

            def expert(e, par):
                wh, wl = me_wh[par], me_wl[par]
                last = isinstance(e, int) and e == EX - 1
                if not isinstance(e, int):
                    pe.wait_ge(me["gT_ready"], NT // U)
                pe.wait_ge(me["w1_split"], e + 1)
                for gr in range(NG):
                    done = NG * e + gr
                    toks = slice(gr * 512, (gr + 1) * 512)
                    for m in range(HM):
                        n = 0
                        for k in range(KC):
                            cols = slice(k * 512 + m * P, k * 512 + (m + 1) * P)
                            for w, v in pairs(wh[:, 0, cols], wl[:, 0, cols], me_xh[:, k, toks], me_xl[:, k, toks]):
                                mm = nc.tensor.matmul(psum[:, m, :], w, v, start=(n == 0), stop=(n == 5))
                                n += 1
                        mm.then_inc(me["up_done"], 1)
                    if gr == 0:
                        pe.wait_ge(me["w2_split"], 1 + e + 1)
                    if not isinstance(e, int) or done >= 2:
                        pe.wait_ge(me["acc_ready"], TG * (done - 1))
                    for m in range(HM):
                        pe.wait_ge(me["hl_ready"], HM * done + m + 1)
                        w2 = slice(m * D, (m + 1) * D)
                        for tau in range(TG):
                            rows = slice(tau * P, (tau + 1) * P)
                            if last and m == 0:
                                t = TG * gr + tau
                                nc.tensor.matmul(down_psum(gr, tau), me_gT[:, t * P:(t + 1) * P], me_b2[:], start=(tau % 2 == 0),
                                                 stop=False, skip_group_check=True)
                            for n, (v, w) in enumerate(pairs(me_hh[:, m, rows], me_hl[:, m, rows], wh[:, 1, w2], wl[:, 1, w2])):
                                mm = nc.tensor.matmul(down_psum(gr, tau), v, w, start=(not last and m == 0 and n == 0 and tau % 2 == 0),
                                                      stop=(m == HM - 1 and n == 2), skip_group_check=True)
                    mm.then_inc(me["down_done"], 1)

            moe_experts(pe, expert)

        def moe_scalar(act):
            nc.scalar.preload_act_table(ACT.Gelu)

            def expert(e, par):
                for gr in range(NG):
                    for m in range(HM):
                        n = HM * (NG * e + gr) + m + 1
                        hold(act, me["up_done"], 1 + n)
                        bias = me_b1[:, e, m:m + 1] if isinstance(e, int) else me_b1[:, bass.ds(e, 1), m:m + 1].rearrange("p e m -> p (e m)")
                        nc.scalar.activation(me_h[:, m, :], psum[:, m, :], ACT.Gelu, bias=bias).then_inc(me["h_ready"], 1)

            moe_experts(act, expert)

        def moe_vector(dve):
            def expert(e, par):
                for gr in range(NG):
                    for m in range(HM):
                        n = HM * (NG * e + gr) + m + 1
                        dve.wait_ge(me["h_ready"], n)
                        split(dve, me_hh[:, m, :], me_hl[:, m, :], me_h[:, m, :], me["hh_ready"], n, me["hl_ready"])
                    if isinstance(e, int) and (e, gr) == (0, 0):
                        moe_gates_end(dve)
                        dve.wait_ge(me["gate_ready"], 1)
                    dve.wait_ge(me["down_done"], 1 + NG * e + gr + 1)
                    for tau in range(TG):
                        t = TG * gr + tau
                        nc.vector.scalar_tensor_tensor(out=x[:, t, :], in0=down_psum(gr, tau), scalar=me_gate[:, t, bass.ds(e, 1)],
                                                       in1=x[:, t, :], op0=ALU.mult, op1=ALU.add).then_inc(me["acc_ready"], 1)
                    if gr == 1 and not (isinstance(e, int) and e == EX - 1):
                        moe_weights(dve, e + 1, 1 - par)

            moe_gates(dve)
            moe_experts(dve, expert)

        with Scratch() as scratch:
            for c in smalls:
                c.w_qkv = scratch(f"{c.name}_w_qkv", [P, KC, 3 * D])
                c.w_o = scratch(f"{c.name}_w_o", [P, KC, D])
                c.b_qk = scratch(f"{c.name}_b_qk", [P, 2 * D])
                c.b_v = scratch(f"{c.name}_b_v", [P, KC, P])
                c.b_o = scratch(f"{c.name}_b_o", [P, D])
            sm_xT = scratch("sm_xT", [P, U, KC, P])
            sm_cT = scratch("sm_cT", [P, U, KC, P])
            sm_qk = scratch("sm_qk", [P, U, 2, D])
            sm_cosd = scratch("sm_cosd", [P, 2, D])
            sm_sind = scratch("sm_sind", [P, 2, D])
            sm_vbd = scratch("sm_vbd", [P, U, G, BT, 64])
            sm_qbd = scratch("sm_qbd", [P, U, KC, BT, P])
            sm_kT = scratch("sm_kT", [P, U, KC, P])
            sm_p = scratch("sm_p", [P, U, BT * G, S])
            sm_max = scratch("sm_max", [P, U, BT * G])
            sm_sum = scratch("sm_sum", [P, U, BT * G])
            sm_rinv = scratch("sm_rinv", [P, U, BT * G])
            sm_pT = scratch("sm_pT", [P, U, G, P])
            sm_o = scratch("sm_o", [P, U, BT * G, DH])
            sm_oT = scratch("sm_oT", [P, U, KC, BT, S])
            f8_xn = scratch("f8_xn", [P, 2, U, D])
            f8_magic = scratch("f8_magic", [P, U, D])
            f8_q = scratch("f8_q", [P, U, D], BF16)
            f8_qT = scratch("f8_qT", [P, U, KC, P], BF16)
            f8_amax = scratch("f8_amax", [P, U])
            f8_scale = scratch("f8_scale", [P, U])
            f8_inv = scratch("f8_inv", [P, U])
            f8_total = scratch("f8_total", [P, 2, U])
            f8_shift = scratch("f8_shift", [P, NT])
            f8_int = scratch("f8_int", [P, KC * D], I32)
            f8_mag = scratch("f8_mag", [P, KC * D], I32)
            f8_high = scratch("f8_high", [P, KC * D])
            f8_byte = scratch("f8_byte", [P, KC * D], U8)
        with Scratch() as scratch:
            x1_xT = scratch("x1_xT", [P, KC, U * P])
            x1_qT = scratch("x1_qT", [P, G, NT * P])
            x1_mask = [scratch(f"x1_mask{n}", [S, BT, SP], BF16) for n in range(2)]
            x1_wks = [scratch(f"x1_wk{n}", [P, KC, D], F32R) for n in ("h", "l")]
            x1_wvs = [scratch(f"x1_wv{n}", [P, KC, D], F32R) for n in ("h", "l")]
            x1_cs = [[scratch(f"x1_ctx{par}{n}", [P, KC, BT * SP + LAST], F32R) for n in ("h", "l")] for par in range(2)]
            x1_qhigh = scratch("x1_qhigh", [P, 2, G, 2 * S], F32R)
            x1_qlow = scratch("x1_qlow", [P, 2, G, 2 * S], F32R)
            x1_qh = scratch("x1_qh", [P, 2, G, 2, P], F32R)
            x1_ql = scratch("x1_ql", [P, 2, G, 2, P], F32R)
            x1_k = scratch("x1_k", [P, 2, G, SP], F32R)
            x1_v = scratch("x1_v", [P, 2, 2, D])
            x1_vls = scratch("x1_vls", [STACK, 2 * D], F32R)
            x1_vlbd = scratch("x1_vlbd", [STACK, 2, HJ, 64], F32R)
            x1_p = scratch("x1_p", [P, BT * G, SK])
            x1_nmax = scratch("x1_nmax", [P, BT * G])
            x1_sum = scratch("x1_sum", [P, BT * G])
            x1_rinv = scratch("x1_rinv", [P, BT * G])
            x1_void = scratch("x1_void", [P, BT * G])
            x1_pT = scratch("x1_pT", [P, 2, 2, P])
            x1_plT = scratch("x1_plT", [STACK, P], F32R)
            x1_o = scratch("x1_o", [P, BT * G, DH])
            x1_oT = scratch("x1_oT", [P, KC, BT, S])
        with Scratch() as scratch:
            mx_taps = scratch("mx_taps", [P, KC, 3, P])
            mx_xT = [scratch(f"mx_xT{n}", [P, 3, KC, U * P + 2]) for n in range(2)]
            mx_h = scratch("mx_h", [GH, U * P])
            mx_gate = scratch("mx_gate", [GH + R, U * P])
            mx_sum = scratch("mx_sum", [GH + R, U * P])
            mx_gu = scratch("mx_gu", [GH + R, U * P])
            mx_glob = scratch("mx_glob", [GH + R, U * P])
        with Scratch() as scratch:
            me_xh = scratch("me_xh", [P, KC, NT * P], F32R)
            me_xl = scratch("me_xl", [P, KC, NT * P], F32R)
            me_wh = [scratch(f"me_wh{n}", [P, 2, 1024], F32R) for n in range(2)]
            me_wl = [scratch(f"me_wl{n}", [P, 2, 1024], F32R) for n in range(2)]
            me_h = scratch("me_h", [P, HM, 512])
            me_hh = scratch("me_hh", [P, HM, 512], F32R)
            me_hl = scratch("me_hl", [P, HM, 512], F32R)
            me_rwh = scratch("me_rwh", [P, KC, E], F32R)
            me_rwl = scratch("me_rwl", [P, KC, E], F32R)
            me_lT = scratch("me_lT", [E, NT * P])
            me_pr = scratch("me_pr", [P, NT, E])
            me_st = scratch("me_st", [P, NT])
            me_cmp = scratch("me_cmp", [P, NT, E, E])
            me_cmp2 = scratch("me_cmp2", [P, NT, E, E])
            me_rank = scratch("me_rank", [P, NT, E])
            me_gate = scratch("me_gate", [P, NT, EX])
            me_gT = scratch("me_gT", [EX, NT * P])

        block = ctx.enter_context(nc.Block())

        @block.sync
        def _(sp):
            for i in range(NT // U):
                sp.dma_start(x[:, U * i:U * (i + 1), :], x_tiles[:, U * i:U * (i + 1), :]).then_inc(x_loaded[i], 16)
            for dst, src in ((ident, "ident"), (eps, "eps"), (head_scale, "head_scale"), (rope_cos, "rope_cos"),
                             (rope_sin, "rope_sin"), (causal, "causal"), (hide, "hide"),
                             (row_pick, "row_pick")):
                sp.dma_start(dst[:], a[src]).then_inc(consts_loaded, 16)
            sp.dma_start(f8_bits[:], a["ffn0_w"]).then_inc(f8["weights_loaded"], 16)
            sp.dma_start(f8_ws[:], a["ffn0_ws"]).then_inc(f8["weights_loaded"], 16)
            sp.dma_start(f8_bias[:], a["ffn0_bias"]).then_inc(f8["weights_loaded"], 16)
            for c in smalls:
                for w, dst in (("w_qkv", c.w_qkv), ("w_o", c.w_o), ("b_qk", c.b_qk), ("b_v", c.b_v), ("b_o", c.b_o)):
                    sp.dma_start(dst[:], a[f"{c.name}_{w}"]).then_inc(c.weights_loaded, 16)
                if c.cross:
                    for u in range(U):
                        sp.dma_start(sm_cT[:, u], a["ctx32"][u]).then_inc(c.ctx_loaded[u], 16)
                    with sp.Fori(1, NT // U) as i:
                        for u in range(U):
                            hold(sp, sm["v_done"], U * (i - 1) + u + 1)
                            sp.dma_start(sm_cT[:, u], a["ctx32"][U * i + u]).then_inc(c.ctx_loaded[u], 16)
            for dst, src in ((x1_wq, "wq"), (x1_wk, "wk"), (x1_wv, "wv"), (x1_wo, "wo"), (x1_bq, "bq"), (x1_bk, "bk"),
                             (x1_bv, "bv"), (x1_bo, "bo")):
                sp.dma_start(dst[:], a[f"xattn1_{src}"]).then_inc(x1["weights_loaded"], 16)
            for dst, src in ((mx_w[:], "w"), (mx_b1[:], "b1"), (mx_w2[:], "w2"), (mx_b2[on_u, :], "b2"), (mx_conv[:], "conv"),
                             (mx_wo[on_u, :], "wo"), (mx_bo[:], "bo"), (mx_keep[on_v, :], "keep")):
                sp.dma_start(dst, a[f"mix1_{src}"]).then_inc(mx["weights_loaded"], 16)
            for dst, src in ((me_b1, "b1"), (me_b2, "b2"), (me_rw, "rw"), (me_rb, "rb"), (me_before, "before")):
                sp.dma_start(dst[:], a[f"moe1_{src}"]).then_inc(me["weights_loaded"], 16)
            sp.dma_start(x1_ctx[:], a["ctx"][0]).then_inc(x1["ctx_loaded"], 16)
            sp.dma_start(x1_mask8[:], a["mask"][0]).then_inc(x1["mask_loaded"], 16)
            with sp.Fori(1, NT) as t:
                hold(sp, x1["ctx_split"], t)
                sp.dma_start(x1_ctx[:], a["ctx"][t]).then_inc(x1["ctx_loaded"], 16)
                hold(sp, x1["mask_ready"], 1 + t)
                sp.dma_start(x1_mask8[:], a["mask"][t]).then_inc(x1["mask_loaded"], 16)
            with sp.Fori(0, EX) as e:
                hold(sp, me["w2_split"], 1 + e)
                sp.dma_start(me_raw[:], a["moe1_w"][e]).then_inc(me["raw_loaded"], 16)
            for gr in range(NG):
                sp.wait_ge(me["acc_ready"], TG * (NG * (EX - 1) + gr + 1))
                sp.dma_start(out_tiles[:, TG * gr:TG * (gr + 1), :], x[:, TG * gr:TG * (gr + 1), :]).then_inc(me["stored"], 16)
            sp.wait_ge(me["stored"], 16 * NG)

        @block.tensor
        def _(pe):
            for s in (x1["xT_done"], me["lT_ready"], me["up_done"], me["down_done"]):
                pe.sem_inc(s, 1)
            pe.wait_ge(consts_loaded, 16 * 8)
            pe.wait_ge(consts_cast, 3)
            small_tensor(pe, small["xattn0"])
            small_tensor(pe, small["attn0"])
            ffn_tensor(pe)
            x1q_tensor(pe)
            x1_tensor(pe)
            mix_tensor(pe)
            moe_prep_tensor(pe)
            moe_tensor(pe)

        @block.scalar
        def _(act):
            act.wait_ge(consts_loaded, 16 * 8)
            small_scalar(act, small["xattn0"])
            small_scalar(act, small["attn0"])
            ffn_scalar(act)
            x1q_scalar(act)
            x1_scalar(act)
            mix_scalar(act)
            moe_prep_scalar(act)
            moe_scalar(act)

        @block.vector
        def _(dve):
            for s in (sm["stats_ready"], me["w2_split"]):
                dve.sem_inc(s, 1)
            for i in range(NT // U):
                dve.wait_ge(x_loaded[i], 16)
                for t in range(U * i, U * (i + 1)):
                    nc.vector.bn_stats(bn_out[:, t, :], x[:, t, :]).then_inc(x_stats, 1)
            dve.wait_ge(x_stats, NT)
            dve.wait_ge(consts_loaded, 16 * 8)
            dve_variance(dve)
            ffn_weights(dve)
            small_vector(dve, small["xattn0"])
            dve_variance(dve)
            small_vector(dve, small["attn0"])
            dve_variance(dve)
            ffn_vector(dve)
            dve_variance(dve)
            x1q_vector(dve)
            x1_vector(dve)
            dve_variance(dve)
            mix_vector(dve)
            dve_variance(dve)
            moe_prep_vector(dve)
            moe_vector(dve)

        @block.gpsimd
        def _(pool):
            pool.sem_inc(x1["mask_ready"], 1)
            nc.gpsimd.memset(sm_vbd[:], 0.0).then_inc(sm_zeroed, 1)
            pool.wait_ge(consts_loaded, 16 * 8)
            nc.gpsimd.tensor_copy(ident_b[:], ident[:]).then_inc(consts_cast, 1)
            nc.gpsimd.tensor_copy(causal_b[:], causal[:]).then_inc(consts_cast, 1)
            nc.gpsimd.tensor_copy(hide_b[:], hide[:]).then_inc(consts_cast, 1)
            for c in smalls:
                pool_bias(pool, sm["norm_ready"], sm["x_biased"], c.bias_ready, c.b_o[:], c.before)
            ffn_pool(pool)
            x1_pool_weights(pool)
            x1_context(pool, 0, 0)
            pool_bias(pool, x1["norm_ready"], x1["x_biased"], x1["bias_ready"], x1_bo[:])
            x1_pool(pool)
            pool_bias(pool, mx["norm_ready"], mx["x_biased"], mx["taps_ready"], mx_bo[:])
            for m, ready in enumerate((me["w1_split"], me["w2_split"])):
                pool.wait_ge(me["w_high"], m + 1)
                nc.gpsimd.tensor_tensor(me_wl[0][:, m, :], me_raw[:, m, :], me_wh[0][:, m, :].bitcast(F32),
                                        ALU.subtract).then_inc(ready, 1)


def layout(inputs):
    f = {k: np.asarray(v) for k, v in inputs.items()}
    out = {}
    rows = lambda w: np.ascontiguousarray(w.reshape(KC, P, -1).transpose(1, 0, 2))
    wide = lambda v: np.ascontiguousarray(np.broadcast_to(v.reshape(1, -1), (P, v.size)))
    heads = lambda w, order=range(G): np.ascontiguousarray(
        w.reshape(G, 2, 2, DH, -1)[list(order)].transpose(2, 0, 3, 1, 4).reshape(P, KC, -1))
    parity = [g for r in range(2) for g in range(r, G, 2)]
    half = np.array([h * DH + d for h in range(H) for d in list(range(0, DH, 2)) + list(range(1, DH, 2))])

    out["x"] = f["x"].reshape(B * S, D)
    ctx = f["ctx_1024"].reshape(NT, BT, SK, KC, P).transpose(0, 4, 3, 1, 2)
    pairs = np.concatenate([ctx, ctx[..., 2 * SK - SP:SK]], axis=-1)
    last = np.repeat(ctx[..., SK - 1], G, axis=-1)
    last = [last[..., :2 * G]] * (32 // (2 * G)) + [last[..., 2 * G:]]
    out["ctx"] = np.concatenate([pairs.reshape(NT, P, KC, BT * SP), *last], axis=-1)
    out["ctx32"] = np.ascontiguousarray(
        ctx[..., :S].reshape(NT, P, KC, BT * S))
    out["mask"] = np.ascontiguousarray(f["mask_Bx1xSxS2_bf0"].reshape(NT, BT, S, SK).transpose(0, 2, 1, 3))

    for name, q, k, v, o, perm in (
            ("xattn0", "L0_xattn_q", "L0_xattn_k", "L0_xattn_v", "L0_xattn_o", slice(None)),
            ("attn0", "q", "k", "v", "o", half)):
        if name == "xattn0":
            w = [f[f"{n}_w"].T for n in (q, k, v, o)]
            b = [f[f"{n}_b"] for n in (q, k, v, o)]
        else:
            w = [f[f"L0_attn_W{n}"] for n in (q, k, v, o)]
            b = [f[f"L0_attn_b{n}"] for n in (q, k, v, o)]
        out[f"{name}_w_qkv"] = rows(np.concatenate([w[0][:, perm], w[1][:, perm], w[2]], axis=1))
        out[f"{name}_w_o"] = heads(w[3], parity)
        out[f"{name}_b_qk"] = wide(np.concatenate([b[0][perm], b[1][perm]]))
        out[f"{name}_b_v"] = np.ascontiguousarray(np.broadcast_to(heads(b[2], parity), (P, KC, P)))
        out[f"{name}_b_o"] = wide(b[3])

    out["ffn0_w"] = rows(f["L0_ffn_weight"].view(np.uint8).T).reshape(P, KC * D)
    out["ffn0_ws"] = np.ascontiguousarray(np.broadcast_to(f["L0_ffn_weight_scale"].reshape(1, 1), (P, 1)))
    out["ffn0_bias"] = wide(f["L0_ffn_bias"])

    for n in "qkv":
        out[f"xattn1_w{n}"] = rows(f[f"L1_xattn_w_{n}"].T)
    out["xattn1_wo"] = heads(f["L1_xattn_w_o"].T)
    out["xattn1_bq"] = np.ascontiguousarray(f["L1_xattn_b_q"].reshape(KC, P).T)
    out["xattn1_bk"] = np.ascontiguousarray(f["L1_xattn_b_k"].reshape(KC, P).T)
    out["xattn1_bv"] = np.ascontiguousarray(np.broadcast_to(heads(f["L1_xattn_b_v"]), (P, KC, P)))
    out["xattn1_bo"] = wide(f["L1_xattn_b_o"])

    out["mix1_w"] = rows(np.concatenate([f["L1_attn_gate_w1"], f["L1_attn_U_w"], f["L1_attn_V_w"]], axis=1))
    out["mix1_b1"] = f["L1_attn_gate_b1"].reshape(GH, 1)
    out["mix1_w2"] = f["L1_attn_gate_w2"]
    out["mix1_b2"] = f["L1_attn_gate_b2"].reshape(R, 1)
    out["mix1_conv"] = rows(f["L1_attn_conv_w"])
    out["mix1_wo"] = f["L1_attn_out_w"]
    out["mix1_bo"] = wide(f["L1_attn_out_b"])

    w1 = np.concatenate([f["L1_ffn_rw1"], f["L1_ffn_sw1"][None]])
    w2 = np.concatenate([f["L1_ffn_rw2"], f["L1_ffn_sw2"][None]])
    w1 = w1.reshape(EX, KC, P, HID).transpose(0, 2, 1, 3).reshape(EX, P, 1, KC * HID)
    w2 = w2.reshape(EX, HM, P, D).transpose(0, 2, 1, 3).reshape(EX, P, 1, HM * D)
    out["moe1_w"] = np.ascontiguousarray(np.concatenate([w1, w2], axis=2))
    b1 = np.concatenate([f["L1_ffn_rb1"], f["L1_ffn_sb1"][None]])
    out["moe1_b1"] = np.ascontiguousarray(b1.reshape(EX, HM, P).transpose(2, 0, 1))
    out["moe1_b2"] = np.concatenate([f["L1_ffn_rb2"], f["L1_ffn_sb2"][None]])
    out["moe1_rw"] = rows(f["L1_ffn_router_w"])
    out["moe1_rb"] = wide(f["L1_ffn_router_b"])

    p = np.arange(P)
    out["ident"] = np.eye(P, dtype=np.float32)
    out["eps"] = np.full((P, 1), EPS, np.float32)
    out["head_scale"] = (((p[:, None] // DH) % L == np.arange(L)[None]) * DH ** -0.5).astype(np.float32)
    freqs = 1.0 / 10000.0 ** (np.arange(DH // 2) / (DH // 2))
    ang = (p % S)[:, None] * freqs[None]
    out["rope_cos"] = np.concatenate([np.cos(ang), np.cos(ang)], 1).astype(np.float32)
    out["rope_sin"] = np.concatenate([-np.sin(ang), np.sin(ang)], 1).astype(np.float32)
    out["causal"] = np.where(np.arange(S)[None] > (p % S)[:, None], CAUSAL, 0.0).astype(np.float32)
    q = np.arange(S)
    out["hide"] = np.where(q[:, None, None] == q[None, None, :], MASKED, 0.0).repeat(L, 1).astype(np.float32)
    out["row_pick"] = np.zeros((2 * 32 + 2 * G, 2 * G), np.float32)
    for row in range(3):
        out["row_pick"][32 * row:32 * row + 2 * G] = np.eye(2 * G)
    out["mix1_keep"] = np.ascontiguousarray(np.broadcast_to((np.arange(U * P) % S != 0).astype(np.float32), (R, U * P)))
    e = np.arange(E)
    out["moe1_before"] = np.ascontiguousarray(np.broadcast_to((e[None] < e[:, None]).astype(np.float32), (P, E, E)))
    return {k: np.ascontiguousarray(v) for k, v in out.items()}


def kernel(**inputs):
    import concourse.bacc as bacc
    from concourse.bass_utils import run_bass_kernel_spmd

    arrays = layout(inputs)
    nc = bacc.Bacc("TRN2", target_bir_lowering=False, num_devices=1)
    args = {}
    for name, v in arrays.items():
        args[name] = nc.dram_tensor(f"in_{name}", v.shape, mybir.dt.from_np(v.dtype), kind="ExternalInput").ap()
    args["out"] = nc.dram_tensor("out_x", (B * S, D), F32, kind="ExternalOutput").ap()
    build(nc, args)
    r = run_bass_kernel_spmd(nc, [{f"in_{k}": v for k, v in arrays.items()}], core_ids=[0])
    return r.results[0]["out_x"].reshape(B, S, D)
```
